# Optimizing a Trainium2 kernel written in Bass

```python
import numpy as np
import jax
import jax.numpy as jnp

def _softmax(x, axis=-1):
    return jax.nn.softmax(x, axis=axis)

def _gelu(x):
    return jax.nn.gelu(x, approximate=True)

def _silu(x):
    return jax.nn.silu(x)

def _sigmoid(x):
    return jax.nn.sigmoid(x)

def _layernorm(x, axis=-1, eps=1e-05):
    m = jnp.mean(x, axis=axis, keepdims=True)
    v = jnp.var(x, axis=axis, keepdims=True)
    return (x - m) / jnp.sqrt(v + eps)

def _scatter_add(tgt, idx, src, axis=0):
    return tgt.at[idx].add(src)

def _segment_sum(src, seg, n):
    return jax.ops.segment_sum(src, seg, n)
kernel_name = 'mk_lm_tower_d1_tok_ids1024_r4_4e2a29'

def setup_inputs(seed: int=0):
    np.random.seed(seed)
    _w = jnp.asarray

    def _rec_inputs():
        import jax
        import jax.numpy as jnp
        _rk = jax.random.key(seed)
        x = jax.random.randint(jax.random.fold_in(_rk, 1), (4, 512), 0, 12564, jnp.int32)
        return x
    x = _rec_inputs()

    def _L0_tok_setup():
        import jax, jax.numpy as jnp
        import numpy as np
        VOCAB = 50257
        NUM_DIM = 256
        BATCH = 4
        SEQ = 1024
        key = jax.random.key(seed)
        k_tok, k_w, k_b = jax.random.split(key, 3)
        tokens = jax.random.randint(k_tok, (BATCH, SEQ), 0, VOCAB)
        weight = jax.random.normal(k_w, (NUM_DIM, VOCAB), dtype=jnp.float32) * 0.02
        bias = jax.random.normal(k_b, (NUM_DIM,), dtype=jnp.float32) * 0.02
        return {'tokens': tokens, 'weight': weight, 'bias': bias}
    _L0_tok_all = _L0_tok_setup()
    _L0_tok_in = {k: v for k, v in _L0_tok_all.items() if k in ('weight', 'bias')}
    del _L0_tok_all

    def _L0_attn_setup():
        import jax, jax.numpy as jnp
        import numpy as np
        B, T, C = (4, 256, 256)
        HS = 64
        H = C // HS
        D_W, D_A, D_V, D_G = (64, 64, 32, 128)
        EPS = 0.00064

        def _wkv(r, w, k, v, a, b):
            Bv, Tv, Cv = r.shape
            rs = lambda t: t.reshape(Bv, Tv, H, HS)
            r, k, v, a, b = (rs(r), rs(k), rs(v), rs(a), rs(b))
            wd = jnp.exp(-jnp.exp(rs(w)))

            def step(S, xs):
                r_, w_, k_, v_, a_, b_ = xs
                sa = jnp.einsum('bhij,bhj->bhi', S, a_)
                S = S * w_[:, :, None, :] + sa[..., None] * b_[:, :, None, :] + v_[..., None] * k_[:, :, None, :]
                y = jnp.einsum('bhij,bhj->bhi', S, r_)
                return (S, y)
            xs = tuple((jnp.swapaxes(t, 0, 1) for t in (r, wd, k, v, a, b)))
            S0 = jnp.zeros((Bv, H, HS, HS), r.dtype)
            _, ys = jax.lax.scan(step, S0, xs)
            return jnp.swapaxes(ys, 0, 1).reshape(Bv, Tv, Cv)

        def _forward(x, x_r, x_w, x_k, x_v, x_a, x_g, w0, w1, w2, a0, a1, a2, v0, v1, v2, g1, g2, k_k, k_a, r_k, Wr, Wk, Wv, Wo, ln_w, ln_b):
            Bv, Tv, Cv = x.shape
            xx = jnp.concatenate([jnp.zeros_like(x[:, :1]), x[:, :-1]], axis=1) - x
            xr = x + xx * x_r
            xw = x + xx * x_w
            xk = x + xx * x_k
            xv = x + xx * x_v
            xa = x + xx * x_a
            xg = x + xx * x_g
            r = xr @ Wr
            w = -jax.nn.softplus(-(w0 + jnp.tanh(xw @ w1) @ w2)) - 0.5
            k = xk @ Wk
            v = xv @ Wv
            v_first = jax.lax.stop_gradient(v)
            v = v + (v_first - v) * jax.nn.sigmoid(v0 + xv @ v1 @ v2)
            a = jax.nn.sigmoid(a0 + xa @ a1 @ a2)
            g = jax.nn.sigmoid(xg @ g1) @ g2
            kk = k * k_k
            kkh = kk.reshape(Bv, Tv, H, HS)
            kkh = kkh / jnp.maximum(jnp.linalg.norm(kkh, axis=-1, keepdims=True), 1e-12)
            kk = kkh.reshape(Bv, Tv, Cv)
            k = k * (1 + (a - 1) * k_a)
            y = _wkv(r, w, k, v, -kk, kk * a)
            yh = y.reshape(Bv, Tv, H, HS)
            mu = jnp.mean(yh, axis=-1, keepdims=True)
            var = jnp.var(yh, axis=-1, keepdims=True)
            y = ((yh - mu) / jnp.sqrt(var + EPS)).reshape(Bv, Tv, Cv) * ln_w + ln_b
            rt = (r.reshape(Bv, Tv, H, HS) * k.reshape(Bv, Tv, H, HS) * r_k).sum(-1, keepdims=True) * v.reshape(Bv, Tv, H, HS)
            y = y + rt.reshape(Bv, Tv, Cv)
            return y * g @ Wo
        key = jax.random.key(seed)
        ks = jax.random.split(key, 28)
        it = iter(range(28))
        n = lambda shape, std: jax.random.normal(ks[next(it)], shape, jnp.float32) * std
        s = C ** (-0.5)
        return {'x': n((B, T, C), 1.0), 'x_r': n((1, 1, C), 0.01), 'x_w': n((1, 1, C), 0.01), 'x_k': n((1, 1, C), 0.01), 'x_v': n((1, 1, C), 0.01), 'x_a': n((1, 1, C), 0.01), 'x_g': n((1, 1, C), 0.01), 'w0': n((1, 1, C), 0.02), 'w1': n((C, D_W), 0.04), 'w2': n((D_W, C), 0.04), 'a0': n((1, 1, C), 0.02), 'a1': n((C, D_A), 0.04), 'a2': n((D_A, C), 0.04), 'v0': n((1, 1, C), 0.02), 'v1': n((C, D_V), 0.04), 'v2': n((D_V, C), 0.04), 'g1': n((C, D_G), 0.04), 'g2': n((D_G, C), 0.04), 'k_k': n((1, 1, C), 0.02), 'k_a': n((1, 1, C), 0.02), 'r_k': n((H, HS), 0.1) + 0.1 * jnp.arange(H, dtype=jnp.float32)[:, None], 'Wr': n((C, C), s), 'Wk': n((C, C), s), 'Wv': n((C, C), s), 'Wo': n((C, C), s), 'ln_w': jnp.ones((C,), jnp.float32), 'ln_b': jnp.zeros((C,), jnp.float32)}
    _L0_attn_all = _L0_attn_setup()
    _L0_attn_in = {k: v for k, v in _L0_attn_all.items() if k in ('x_r', 'x_w', 'x_k', 'x_v', 'x_a', 'x_g', 'w0', 'w1', 'w2', 'a0', 'a1', 'a2', 'v0', 'v1', 'v2', 'g1', 'g2', 'k_k', 'k_a', 'r_k', 'Wr', 'Wk', 'Wv', 'Wo', 'ln_w', 'ln_b')}
    del _L0_attn_all

    def _L0_ffn_setup():
        import jax, jax.numpy as jnp
        import numpy as np
        B, T, E, C, H, G = (2, 512, 8, 256, 512, 16)
        key = jax.random.key(seed)
        ks = jax.random.split(key, 7)
        return {'hidden_states': jax.random.normal(ks[0], (B, T, C), jnp.float32), 'w_red': jax.random.normal(ks[1], (C, G), jnp.float32) * 0.02, 'wg': jax.random.normal(ks[2], (E, G), jnp.float32), 'W1': jax.random.normal(ks[3], (E, C, H), jnp.float32) * 0.02, 'b1': jax.random.normal(ks[4], (E, H), jnp.float32) * 0.02, 'W2': jax.random.normal(ks[5], (E, H, C), jnp.float32) * 0.02, 'b2': jax.random.normal(ks[6], (E, C), jnp.float32) * 0.02}
    _L0_ffn_all = _L0_ffn_setup()
    _L0_ffn_in = {k: v for k, v in _L0_ffn_all.items() if k in ('w_red', 'wg', 'W1', 'b1', 'W2', 'b2')}
    del _L0_ffn_all
    return {'x': x, 'L0_tok_weight': _L0_tok_in['weight'], 'L0_tok_bias': _L0_tok_in['bias'], 'L0_attn_x_r': _L0_attn_in['x_r'], 'L0_attn_x_w': _L0_attn_in['x_w'], 'L0_attn_x_k': _L0_attn_in['x_k'], 'L0_attn_x_v': _L0_attn_in['x_v'], 'L0_attn_x_a': _L0_attn_in['x_a'], 'L0_attn_x_g': _L0_attn_in['x_g'], 'L0_attn_w0': _L0_attn_in['w0'], 'L0_attn_w1': _L0_attn_in['w1'], 'L0_attn_w2': _L0_attn_in['w2'], 'L0_attn_a0': _L0_attn_in['a0'], 'L0_attn_a1': _L0_attn_in['a1'], 'L0_attn_a2': _L0_attn_in['a2'], 'L0_attn_v0': _L0_attn_in['v0'], 'L0_attn_v1': _L0_attn_in['v1'], 'L0_attn_v2': _L0_attn_in['v2'], 'L0_attn_g1': _L0_attn_in['g1'], 'L0_attn_g2': _L0_attn_in['g2'], 'L0_attn_k_k': _L0_attn_in['k_k'], 'L0_attn_k_a': _L0_attn_in['k_a'], 'L0_attn_r_k': _L0_attn_in['r_k'], 'L0_attn_Wr': _L0_attn_in['Wr'], 'L0_attn_Wk': _L0_attn_in['Wk'], 'L0_attn_Wv': _L0_attn_in['Wv'], 'L0_attn_Wo': _L0_attn_in['Wo'], 'L0_attn_ln_w': _L0_attn_in['ln_w'], 'L0_attn_ln_b': _L0_attn_in['ln_b'], 'L0_ffn_w_red': _L0_ffn_in['w_red'], 'L0_ffn_wg': _L0_ffn_in['wg'], 'L0_ffn_W1': _L0_ffn_in['W1'], 'L0_ffn_b1': _L0_ffn_in['b1'], 'L0_ffn_W2': _L0_ffn_in['W2'], 'L0_ffn_b2': _L0_ffn_in['b2']}

def reference(x, L0_tok_weight, L0_tok_bias, L0_attn_x_r, L0_attn_x_w, L0_attn_x_k, L0_attn_x_v, L0_attn_x_a, L0_attn_x_g, L0_attn_w0, L0_attn_w1, L0_attn_w2, L0_attn_a0, L0_attn_a1, L0_attn_a2, L0_attn_v0, L0_attn_v1, L0_attn_v2, L0_attn_g1, L0_attn_g2, L0_attn_k_k, L0_attn_k_a, L0_attn_r_k, L0_attn_Wr, L0_attn_Wk, L0_attn_Wv, L0_attn_Wo, L0_attn_ln_w, L0_attn_ln_b, L0_ffn_w_red, L0_ffn_wg, L0_ffn_W1, L0_ffn_b1, L0_ffn_W2, L0_ffn_b2):
    import jax
    import jax.numpy as jnp

    def _L0_tok_ref(tokens, weight, bias):
        import jax, jax.numpy as jnp
        import numpy as np
        VOCAB = 50257
        NUM_DIM = 256
        BATCH = 4
        SEQ = 1024
        table = weight.T
        return jnp.take(table, tokens, axis=0) + bias

    def _L0_attn_ref(x, x_r, x_w, x_k, x_v, x_a, x_g, w0, w1, w2, a0, a1, a2, v0, v1, v2, g1, g2, k_k, k_a, r_k, Wr, Wk, Wv, Wo, ln_w, ln_b):
        import jax, jax.numpy as jnp
        import numpy as np
        B, T, C = (4, 256, 256)
        HS = 64
        H = C // HS
        D_W, D_A, D_V, D_G = (64, 64, 32, 128)
        EPS = 0.00064

        def _wkv(r, w, k, v, a, b):
            Bv, Tv, Cv = r.shape
            rs = lambda t: t.reshape(Bv, Tv, H, HS)
            r, k, v, a, b = (rs(r), rs(k), rs(v), rs(a), rs(b))
            wd = jnp.exp(-jnp.exp(rs(w)))

            def step(S, xs):
                r_, w_, k_, v_, a_, b_ = xs
                sa = jnp.einsum('bhij,bhj->bhi', S, a_)
                S = S * w_[:, :, None, :] + sa[..., None] * b_[:, :, None, :] + v_[..., None] * k_[:, :, None, :]
                y = jnp.einsum('bhij,bhj->bhi', S, r_)
                return (S, y)
            xs = tuple((jnp.swapaxes(t, 0, 1) for t in (r, wd, k, v, a, b)))
            S0 = jnp.zeros((Bv, H, HS, HS), r.dtype)
            _, ys = jax.lax.scan(step, S0, xs)
            return jnp.swapaxes(ys, 0, 1).reshape(Bv, Tv, Cv)

        def _forward(x, x_r, x_w, x_k, x_v, x_a, x_g, w0, w1, w2, a0, a1, a2, v0, v1, v2, g1, g2, k_k, k_a, r_k, Wr, Wk, Wv, Wo, ln_w, ln_b):
            Bv, Tv, Cv = x.shape
            xx = jnp.concatenate([jnp.zeros_like(x[:, :1]), x[:, :-1]], axis=1) - x
            xr = x + xx * x_r
            xw = x + xx * x_w
            xk = x + xx * x_k
            xv = x + xx * x_v
            xa = x + xx * x_a
            xg = x + xx * x_g
            r = xr @ Wr
            w = -jax.nn.softplus(-(w0 + jnp.tanh(xw @ w1) @ w2)) - 0.5
            k = xk @ Wk
            v = xv @ Wv
            v_first = jax.lax.stop_gradient(v)
            v = v + (v_first - v) * jax.nn.sigmoid(v0 + xv @ v1 @ v2)
            a = jax.nn.sigmoid(a0 + xa @ a1 @ a2)
            g = jax.nn.sigmoid(xg @ g1) @ g2
            kk = k * k_k
            kkh = kk.reshape(Bv, Tv, H, HS)
            kkh = kkh / jnp.maximum(jnp.linalg.norm(kkh, axis=-1, keepdims=True), 1e-12)
            kk = kkh.reshape(Bv, Tv, Cv)
            k = k * (1 + (a - 1) * k_a)
            y = _wkv(r, w, k, v, -kk, kk * a)
            yh = y.reshape(Bv, Tv, H, HS)
            mu = jnp.mean(yh, axis=-1, keepdims=True)
            var = jnp.var(yh, axis=-1, keepdims=True)
            y = ((yh - mu) / jnp.sqrt(var + EPS)).reshape(Bv, Tv, Cv) * ln_w + ln_b
            rt = (r.reshape(Bv, Tv, H, HS) * k.reshape(Bv, Tv, H, HS) * r_k).sum(-1, keepdims=True) * v.reshape(Bv, Tv, H, HS)
            y = y + rt.reshape(Bv, Tv, Cv)
            return y * g @ Wo
        return _forward(x, x_r, x_w, x_k, x_v, x_a, x_g, w0, w1, w2, a0, a1, a2, v0, v1, v2, g1, g2, k_k, k_a, r_k, Wr, Wk, Wv, Wo, ln_w, ln_b)

    def _L0_ffn_ref(hidden_states, w_red, wg, W1, b1, W2, b2):
        import jax, jax.numpy as jnp
        import numpy as np
        B, T, E, C, H, G = (2, 512, 8, 256, 512, 16)
        b, t, c = hidden_states.shape
        x = hidden_states.reshape(-1, c)
        x_red = x @ w_red
        wg_n = wg / jnp.maximum(jnp.linalg.norm(wg, axis=1, keepdims=True), 0.0001)
        logits = x_red @ wg_n.T
        gates = jax.nn.softmax(logits, axis=1)
        scores = jnp.max(gates, axis=1)
        idx = jnp.argmax(gates, axis=1)
        h = jnp.einsum('nc,ech->neh', x, W1) + b1[None]
        h = jnp.take_along_axis(h, idx[:, None, None], axis=1)[:, 0, :]
        h = jax.nn.gelu(h, approximate=False)
        o = jnp.einsum('nh,ehc->nec', h, W2) + b2[None]
        o = jnp.take_along_axis(o, idx[:, None, None], axis=1)[:, 0, :]
        o = o * scores[:, None]
        return o.reshape(b, t, c)
    h = _L0_tok_ref(x, L0_tok_weight, L0_tok_bias)
    h = h + _L0_attn_ref(_layernorm(h, axis=-1), L0_attn_x_r, L0_attn_x_w, L0_attn_x_k, L0_attn_x_v, L0_attn_x_a, L0_attn_x_g, L0_attn_w0, L0_attn_w1, L0_attn_w2, L0_attn_a0, L0_attn_a1, L0_attn_a2, L0_attn_v0, L0_attn_v1, L0_attn_v2, L0_attn_g1, L0_attn_g2, L0_attn_k_k, L0_attn_k_a, L0_attn_r_k, L0_attn_Wr, L0_attn_Wk, L0_attn_Wv, L0_attn_Wo, L0_attn_ln_w, L0_attn_ln_b)
    h = h + _L0_ffn_ref(_layernorm(h, axis=-1), L0_ffn_w_red, L0_ffn_wg, L0_ffn_W1, L0_ffn_b1, L0_ffn_W2, L0_ffn_b2)
    return h

_drawn_inputs = setup_inputs


def setup_inputs(seed=0):
    import zlib

    import numpy as np

    out = dict(_drawn_inputs(seed))
    spreads = {'L0_attn_ln_w': (1.0, 0.2), 'L0_attn_ln_b': (0.0, 0.1)}
    factors = {'L0_attn_x_r': 4.498,
     'L0_attn_x_w': 200.0,
     'L0_attn_x_k': 5.493,
     'L0_attn_x_v': 6.302,
     'L0_attn_x_a': 35.297,
     'L0_attn_x_g': 8.0,
     'L0_attn_w0': 8.0,
     'L0_attn_a0': 180.963,
     'L0_attn_a1': 8.0,
     'L0_attn_a2': 8.0,
     'L0_attn_k_a': 4.886,
     'L0_ffn_b1': 33.272,
     'L0_ffn_b2': 8.0}
    for name, (base, spread) in spreads.items():
        noise = np.random.default_rng([zlib.crc32(name.encode()), seed]).standard_normal(out[name].shape)
        drawn = base * np.exp(spread * noise) if base else spread * noise
        out[name] = jnp.asarray(drawn.astype(out[name].dtype))
    for name, factor in factors.items():
        out[name] = (out[name] * factor).astype(out[name].dtype)
    return out
```

```python
from contextlib import ExitStack

import concourse.bass as bass
from concourse import mybir

F32 = mybir.dt.float32
U32 = mybir.dt.uint32
ALU = mybir.AluOpType
ACT = mybir.ActivationFunctionType
AX = mybir.AxisListType

B, T, C = 4, 512, 256
H, HS = 4, 64
L = 32
TILES = T // L
CH = 4
SLABS = TILES // CH
BLK = CH * B
NT = BLK * L
UN = 2 * CH * 2
E, HID, G = 8, 512, 16
HC = HID // 128
DECAY = -0.6065306597126334
LN_EPS, GN_EPS = 1e-5, 0.00064
VECS = ["x_r", "x_w", "x_k", "x_v", "x_a", "x_g", "w0", "a0", "v0", "k_k", "k_a", "r_k", "ln_w", "ln_b"]
CONSTS = [("ident", 128), ("ones_bd", 128), ("mean_bd", 128), ("strict_bd", 128), ("upto", L), ("pairs", L),
          ("eye", L), ("low", 4 * L), ("half", 2), ("iota", E)]


def build(nc, table, tokens, tok_bias, cvec, consts, W, w1, w2, a1, a2, v1, v2, g1, g2, w_red, wg, W1, b1, W2, b2, out):
    ctx = ExitStack()
    with ctx:
        def sem(name):
            return ctx.enter_context(nc.semaphore(name))

        at = [0]
        WORDS = 52000
        arena = ctx.enter_context(nc.sbuf_tensor("arena", [128, WORDS], F32))

        def carve(*dims):
            n = 1
            for d in dims:
                n *= d
            flat = arena[:, at[0]:at[0] + n]
            at[0] += n
            assert at[0] <= WORDS, at[0]
            if len(dims) == 1:
                return flat
            names = "abcdef"[:len(dims)]
            return flat.rearrange(f"p ({' '.join(names)}) -> p {' '.join(names)}",
                                  **{k: d for k, d in zip(names[:-1], dims[:-1])})

        res = carve(TILES, C)
        cst = {}
        for name, width in CONSTS:
            cst[name] = carve(width)
        cv = carve(2 * len(VECS))
        vec = {name: cv[:, 2 * k:2 * k + 2] for k, name in enumerate(VECS)}
        stats = carve(TILES, 6)
        moments = carve(TILES, 2)
        stdev = carve(TILES)
        rstd = carve(TILES)
        eps_ln = carve(1)
        eps_gn = carve(1)
        ids = carve(TILES).bitcast(U32)
        ident = cst["ident"]
        shared = at[0]

        bias_rows = carve(C)
        w_sb = {k: carve(2, C) for k in "rkvo"}
        w1_sb, a1_sb, v1_sb, g1_sb = carve(2, 64), carve(2, 64), carve(2, 32), carve(2, 128)
        w2_sb, a2_sb, v2_sb, g2_sb = carve(C), carve(C), carve(C), carve(C)
        xT = carve(2, CH + 1, B * L)

        def over(start, *dims):
            keep = at[0]
            at[0] = start
            buf = carve(*dims)
            at[0] = keep
            return buf

        xn_at = at[0]
        xn = carve(CH, C)
        v_cmp = over(xn_at, UN, HS)
        xx_at = at[0]
        xx, v = carve(2, BLK, L), carve(2, NT)
        n_bd = over(xx_at, UN, 128)
        mix = [carve(2, NT) for _ in range(3)]
        rtv, yT, yd = mix
        k_at = at[0]
        k, r = carve(2, NT), carve(2, NT)
        v_tok = over(k_at, UN, 128)
        low_at = at[0]
        low_v, low_w, low_a, low_g = carve(NT), carve(NT), carve(NT), carve(NT)
        k_tok = over(low_at, UN, 128)
        gate_at = at[0]
        vgate, sig_w = carve(2, NT), carve(2, NT)
        b_tok = over(gate_at, UN, 128)
        iclr_at = at[0]
        iclr, kk = carve(2, NT), carve(2, NT)
        mak_bd = over(iclr_at, UN, 128)
        tmp2_at = at[0]
        tmp2 = carve(2, NT)
        t_c, u_c = over(tmp2_at, UN, L), over(tmp2_at + UN * L, UN, L)
        gate, tmp, inv, v2nd = carve(2, NT), carve(2, NT), carve(2, NT), carve(2, NT)
        prod = carve(2, BLK, L + 1)
        invp = carve(2, BLK, L)
        scan_keep = carve(2 * NT)
        ar = carve(2, BLK, 2 * L)
        a_bd, b_bd, k_bd, v_bd = (carve(2, BLK, 2 * L) for _ in range(4))
        u_bd = carve(UN, 128)
        x_c = carve(UN, L)
        mrb, mrk = carve(UN, L), carve(UN, L)
        state = carve(2, 4, HS)
        state_bd = carve(2, 4, 128)
        w_s = carve(4, HS)
        sa_c = carve(4, HS)
        sa_bd = carve(4, 128)
        attn_end = at[0]

        at[0] = shared
        xn2 = carve(TILES, C)
        xT2 = carve(2, TILES * 128)
        red = carve(TILES * 128)
        logits, ex, onehot, picked = carve(TILES, E), carve(TILES, E), carve(TILES, E), carve(TILES, E)
        top, topf = carve(TILES, E), carve(TILES, E)
        topi = carve(TILES, E).bitcast(U32)
        esum, score = carve(TILES), carve(TILES)
        pickedT = carve(TILES * 128)
        wred_sb = carve(2, G)
        wg_sb, wgn, wgsq, wgT = carve(G), carve(G), carve(G), carve(E)
        wgs = carve(2)
        b1_sb = carve(E, HC)
        b2_sb = carve(C)
        W1_sb = [carve(2, HID) for _ in range(2)]
        W2_sb = [carve(HC, C) for _ in range(2)]
        hT = [carve(HC, NT) for _ in range(2)]

        ps = ctx.enter_context(nc.psum_tensor("ps", [128, 8, 512], F32))

        names = """consts_in weights_in ids_in rows_in ffn_in wexp_in0 wexp_in1 biased stats1_ok mom1_ok sd1_ok zeroed rstd1_ok
        xn_ok xT_ps xT_carry xT_ok xx_ok mix_ok  k_ps r_ps v_ps lv_ps lw_ps vg_ps la_ps w_ps lg_ps a_ps g_ps
        k_ok r_ok v_ok lv_ok lw_ok vg_ok la_ok w_ok lg_ok a_ok g_ok
        kk_ok sq_ok nrm_ps nrm_ok nmax_ok ninv_ok kkn_ok scan_ok prod_ok invp_ok t1_ok k2_ok rkr_ok rt_ps rtv_ok
        vd_ok vs_ok v2_ok vbd_ok ar_ok abd_ok bn_ok bbd_ok kbd_ok m_ps tok_ps tok_ok vcmp_ok
        masks_ok u0_ok x_ps x_ok t_ps t_ok u_ok ubd_ok
        w_ps_c w_ok_c sa_ps sa_ok sabd_ok s_ps y_ps s_sum s_ok sbd_ok yT_ok mean_ps yd_ok ysq_ok var_ps ysd_ok
        yinv_ok yz1 yz2 yz3 z_ok o_ps slab_ok
        stats2_ok mom2_ok sd2_ok rstd2_ok xn2_ok xT2_ps xT2_ok red_ps red_ok wgsq_ok wgsum_ok wgsd_ok wgmax_ok wginv_ok wgn_ok
        wgT_ps wgT_ok lg2_ps lg2_ok topv_ok topi_ok topf_ok onehot_ok dif_ok exp_ok esum_ok score_ok picked_ok
        pT_ps pT_ok b2_ps b2_ok h_ps h_ok o2_ps o2_ok  out_done""".split()
        s = {n: sem(n) for n in names}

        block = ctx.enter_context(nc.Block())

        def unit(p, c, b):
            return (p * CH + c) * 2 + b // 2

        @block.sync
        def _(sp):
            at_c = 0
            for name, width in CONSTS:
                sp.dma_start(cst[name], consts[:, at_c:at_c + width]).then_inc(s["consts_in"], 16)
                at_c += width
            sp.dma_start(cv, cvec[:, :]).then_inc(s["consts_in"], 16)
            sp.dma_start(bias_rows, tok_bias[:, :]).then_inc(s["consts_in"], 16)
            for n, key in enumerate("rkvo"):
                sp.dma_start(w_sb[key], W[n]).then_inc(s["weights_in"], 16)
            for dst, src in ((w1_sb, w1), (a1_sb, a1), (v1_sb, v1), (g1_sb, g1)):
                sp.dma_start(dst, src[:, :, :]).then_inc(s["weights_in"], 16)
            for dst, src, rows in ((w2_sb, w2, 64), (a2_sb, a2, 64), (v2_sb, v2, 32), (g2_sb, g2, 128)):
                sp.dma_start(dst[0:rows, :], src[:, :]).then_inc(s["weights_in"], 16)
            sp.wait_ge(s["slab_ok"], SLABS + 1)
            sp.dma_start(wred_sb, w_red[:, :, :]).then_inc(s["ffn_in"], 16)
            sp.dma_start(wg_sb[0:E, :], wg[:, :]).then_inc(s["ffn_in"], 16)
            sp.dma_start(b1_sb, b1[:, :, :]).then_inc(s["ffn_in"], 16)
            sp.dma_start(b2_sb[0:E, :], b2[:, :]).then_inc(s["ffn_in"], 16)
            for e in range(E):
                if e >= 2:
                    sp.wait_ge(s["o2_ps"], (e - 1) * TILES)
                sp.dma_start(W1_sb[e % 2], W1[e]).then_inc(s[f"wexp_in{e % 2}"], 16)
                sp.dma_start(W2_sb[e % 2], W2[e]).then_inc(s[f"wexp_in{e % 2}"], 16)
            for t in range(TILES):
                sp.wait_ge(s["o2_ok"], (E - 1) * TILES + t + 1)
                sp.dma_start(out[t], res[:, t, :]).then_inc(s["out_done"], 16)
            sp.wait_ge(s["out_done"], 16 * TILES)

        @block.gpsimd
        def _(pool):
            pool.dma_start(ids, tokens[:, :]).then_inc(s["ids_in"], 16)
            pool.wait_ge(s["ids_in"], 16)
            for t in range(TILES):
                pool.indirect_dma_start(out=res[:, t, :], out_offset=None, in_=table[:, :],
                                        in_offset=bass.IndirectOffsetOnAxis(ap=ids[:, t:t + 1], axis=0)
                                        ).then_inc(s["rows_in"], 16)
            with pool.Fori(0, SLABS) as i:
                n = i + 1
                pool.wait_ge(s["v_ok"], n)
                pool.wait_ge(s["slab_ok"], n)
                nc.gpsimd.tensor_tensor(v2nd, v, v, ALU.subtract).then_inc(s["vd_ok"], 1)
                pool.wait_ge(s["vd_ok"], n)
                pool.wait_ge(s["vg_ok"], n)
                nc.gpsimd.tensor_tensor(v2nd, v2nd, vgate, ALU.mult).then_inc(s["vs_ok"], 1)
                pool.wait_ge(s["vs_ok"], n)
                nc.gpsimd.tensor_tensor(v2nd, v2nd, v, ALU.add).then_inc(s["v2_ok"], 1)

        @block.scalar
        def _(act):
            act.wait_ge(s["mom1_ok"], 1)
            nc.scalar.activation(stdev, moments[:, :, 1], ACT.Sqrt, bias=eps_ln).then_inc(s["sd1_ok"], 1)
            act.wait_ge(s["zeroed"], 1)
            act.wait_ge(s["consts_in"], 16 * (len(CONSTS) + 2))
            with act.Fori(0, SLABS) as i:
                n = i + 1
                act.wait_ge(s["xT_ps"], n)
                nc.scalar.copy(xT[:, :, 0, :], xT[:, :, CH, :]).then_inc(s["xT_carry"], 1)
                act.wait_ge(s["xT_carry"], n)
                nc.scalar.copy(xT[:, :, 1:CH + 1, :], ps[:, 0:2, :].rearrange("p a (c t) -> p a c t", c=CH)).then_inc(s["xT_ok"], 1)
                act.wait_ge(s["k_ps"], n)
                nc.scalar.copy(k, ps[:, 0:2, :]).then_inc(s["k_ok"], 1)
                act.wait_ge(s["r_ps"], n)
                nc.scalar.copy(r, ps[:, 2:4, :]).then_inc(s["r_ok"], 1)
                act.wait_ge(s["v_ps"], n)
                nc.scalar.copy(v, ps[:, 4:6, :]).then_inc(s["v_ok"], 1)
                act.wait_ge(s["lv_ps"], n)
                nc.scalar.copy(low_v[0:32, :], ps[0:32, 6, :]).then_inc(s["lv_ok"], 1)
                act.wait_ge(s["lw_ps"], n)
                nc.scalar.activation(low_w[0:64, :], ps[0:64, 7, :], ACT.Tanh).then_inc(s["lw_ok"], 1)

                def sigmoid2(dst, bank, bias, ready, done):
                    act.wait_ge(s[ready], n)
                    nc.scalar.activation(dst[:, 0, :], ps[:, bank, :], ACT.Sigmoid, bias=vec[bias][:, 0:1])
                    nc.scalar.activation(dst[:, 1, :], ps[:, bank + 1, :], ACT.Sigmoid, bias=vec[bias][:, 1:2]).then_inc(s[done], 1)

                sigmoid2(vgate, 0, "v0", "vg_ps", "vg_ok")
                act.wait_ge(s["la_ps"], n)
                nc.scalar.copy(low_a[0:64, :], ps[0:64, 6, :]).then_inc(s["la_ok"], 1)
                sigmoid2(sig_w, 2, "w0", "w_ps", "w_ok")
                act.wait_ge(s["lg_ps"], n)
                nc.scalar.activation(low_g, ps[:, 7, :], ACT.Sigmoid).then_inc(s["lg_ok"], 1)
                sigmoid2(iclr, 4, "a0", "a_ps", "a_ok")
                act.wait_ge(s["g_ps"], n)
                nc.scalar.copy(gate, ps[:, 0:2, :]).then_inc(s["g_ok"], 1)
                act.wait_ge(s["nrm_ps"], n)
                nc.scalar.activation(inv, ps[:, 2:4, :], ACT.Sqrt).then_inc(s["nrm_ok"], 1)
                act.wait_ge(s["scan_ok"], n)
                nc.scalar.activation(prod[:, :, :, 1:L + 1], tmp2[:, :, :].rearrange("p a (b t) -> p a b t", b=BLK), ACT.Exp,
                                     scale=DECAY).then_inc(s["prod_ok"], 1)
                act.wait_ge(s["v2_ok"], n)
                for h in range(2):
                    q = slice(64 * h, 64 * h + 64)
                    last = nc.scalar.copy(v_bd[q, :, :, L * h:L * h + L], v2nd[q].rearrange("p a (b t) -> p a b t", b=BLK))
                last.then_inc(s["vbd_ok"], 1)
                act.wait_ge(s["ar_ok"], n)
                for h in range(2):
                    q = slice(64 * h, 64 * h + 64)
                    last = nc.scalar.copy(a_bd[q, :, :, L * h:L * h + L], ar[q, :, :, 0:L])
                last.then_inc(s["abd_ok"], 1)
                for j, dst in enumerate((b_tok, b_tok, k_tok, k_tok, v_tok, v_tok)):
                    act.wait_ge(s["tok_ps"], 6 * i + j + 1)
                    bank = 4 + 2 * (j % 2)
                    nc.scalar.copy(dst[:, 8 * (j % 2):8 * (j % 2) + 8, :],
                                   ps[:, bank:bank + 2, :].rearrange("p a (u t) -> p (a u) t", u=4)).then_inc(s["tok_ok"], 1)
                for lvl in range(5):
                    act.wait_ge(s["u_ok"], 5 * i + lvl + 1)
                    for q in range(4):
                        rows = slice(32 * q, 32 * q + 32)
                        last = nc.scalar.copy(u_bd[rows, :, L * q:L * q + L], u_c[rows])
                    last.then_inc(s["ubd_ok"], 1)
                for c in range(CH):
                    act.wait_ge(s["w_ps_c"], 4 * i + c + 1)
                    nc.scalar.copy(w_s, ps[:, 2, 0:256].rearrange("p (u t) -> p u t", u=4)).then_inc(s["w_ok_c"], 1)
                    act.wait_ge(s["sa_ok"], 4 * i + c + 1)
                    if c:
                        act.wait_ge(s["y_ps"], 4 * i + c)
                    for h in range(2):
                        last = nc.scalar.activation(sa_bd[:, :, HS * h:HS * h + HS], sa_c, ACT.Copy,
                                                    scale=cst["half"][:, h:h + 1])
                    last.then_inc(s["sabd_ok"], 1)
                    act.wait_ge(s["s_ok"], 4 * i + c + 1)
                    act.wait_ge(s["y_ps"], 4 * i + c + 1)
                    for h in range(2):
                        q = slice(64 * h, 64 * h + 64)
                        last = nc.scalar.copy(state_bd[q, :, :, HS * h:HS * h + HS], state[q])
                    last.then_inc(s["sbd_ok"], 1)
                for b2 in range(2):
                    last = nc.scalar.copy(yT.rearrange("p a (c d e t) -> p (a c) d e t", c=CH, d=2, e=2)[:, :, :, b2, :],
                                          ps[:, 6 + b2, :].rearrange("p (u d t) -> p u d t", d=2, t=L))
                last.then_inc(s["yT_ok"], 1)
                act.wait_ge(s["var_ps"], n)
                nc.scalar.activation(inv, ps[:, 2:4, :], ACT.Sqrt, bias=eps_gn).then_inc(s["ysd_ok"], 1)
            act.wait_ge(s["mom2_ok"], 1)
            nc.scalar.activation(stdev, moments[:, :, 1], ACT.Sqrt, bias=eps_ln).then_inc(s["sd2_ok"], 1)
            act.wait_ge(s["wgsum_ok"], 1)
            nc.scalar.activation(wgs[0:E, 1:2], wgs[0:E, 0:1], ACT.Sqrt).then_inc(s["wgsd_ok"], 1)
            for t in range(0, TILES, CH):
                act.wait_ge(s["xT2_ps"], t // CH + 1)
                nc.scalar.copy(xT2[:, :, t * 128:(t + CH) * 128], ps[:, 0:2, :]).then_inc(s["xT2_ok"], 1)
            for t in range(SLABS):
                act.wait_ge(s["red_ps"], t + 1)
                nc.scalar.copy(red[0:G, t * NT:(t + 1) * NT], ps[0:G, 2 + t % 2, :]).then_inc(s["red_ok"], 1)
            act.wait_ge(s["dif_ok"], 1)
            nc.scalar.activation(ex, ex, ACT.Exp).then_inc(s["exp_ok"], 1)
            for e in range(E):
                for sl in range(SLABS):
                    g = e * SLABS + sl
                    if g >= 2:
                        act.wait_ge(s["o2_ps"], CH * (g - 1))
                    for m in range(HC):
                        act.wait_ge(s["h_ps"], g * HC + m + 1)
                        nc.scalar.activation(hT[g % 2][:, m, :], ps[:, m % 4, :], ACT.Gelu,
                                             bias=b1_sb[:, e, m:m + 1]).then_inc(s["h_ok"], 1)

        @block.vector
        def _(dve):
            V = nc.vector
            V.memset(eps_ln, LN_EPS)
            V.memset(eps_gn, GN_EPS).then_inc(s["slab_ok"], 1)
            V.memset(scan_keep, 1.0)
            V.memset(state, 0.0)
            V.memset(state_bd, 0.0)
            V.memset(xT, 0.0)
            V.memset(prod, 1.0)
            for buf in (a_bd, b_bd, k_bd, v_bd, u_bd):
                last = V.memset(buf, 0.0)
            last.then_inc(s["zeroed"], 1)
            dve.wait_ge(s["zeroed"], 1)
            V.memset(scan_keep.rearrange("p (b t) -> p b t", t=L)[:, :, 0:1], 0.0).then_inc(s["zeroed"], 1)
            dve.wait_ge(s["zeroed"], 2)
            dve.wait_ge(s["consts_in"], 16 * (len(CONSTS) + 2))
            dve.wait_ge(s["rows_in"], 16 * TILES)
            for t in range(TILES):
                V.tensor_tensor(res[:, t, :], res[:, t, :], bias_rows, ALU.add).then_inc(s["biased"], 1)
            for t in range(TILES):
                dve.wait_ge(s["biased"], t + 1)
                V.bn_stats(stats[:, t, :], res[:, t, :]).then_inc(s["stats1_ok"], 1)
            for t in range(TILES):
                dve.wait_ge(s["stats1_ok"], t + 1)
                last = V.bn_aggr(moments[:, t, :], stats[:, t, :])
            last.then_inc(s["mom1_ok"], 1)
            dve.wait_ge(s["sd1_ok"], 1)
            V.reciprocal(rstd, stdev).then_inc(s["rstd1_ok"], 1)
            dve.wait_ge(s["rstd1_ok"], 1)
            with dve.Fori(0, SLABS) as i:
                n = i + 1
                for c in range(CH):
                    t = i * CH + c
                    last = V.tensor_scalar(xn[:, c, :], res[:, t, :], moments[:, t, 0:1], rstd[:, bass.ds(t, 1)],
                                           ALU.subtract, ALU.mult)
                last.then_inc(s["xn_ok"], 1)
                dve.wait_ge(s["xT_ok"], n)
                xb = xT.rearrange("p a c (b t) -> p a (c b) t", t=L)
                V.tensor_tensor(xx[:, :, :, 1:L], xb[:, :, B:B + BLK, 0:L - 1], xb[:, :, B:B + BLK, 1:L], ALU.subtract)
                V.tensor_tensor(xx[:, :, :, 0:1], xb[:, :, 0:BLK, L - 1:L], xb[:, :, B:B + BLK, 0:1],
                                ALU.subtract).then_inc(s["xx_ok"], 1)
                dve.wait_ge(s["xx_ok"], n)
                for j, name in enumerate(["x_k", "x_r", "x_v", "x_w", "x_a", "x_g"]):
                    if j >= 3:
                        dve.wait_ge(s[("k_ps", "r_ps", "lv_ps")[j - 3]], n)
                    for p in range(2):
                        last = V.scalar_tensor_tensor(out=mix[j % 3][:, p, :], in0=xx[:, p].rearrange("p b t -> p (b t)"),
                                                      scalar=vec[name][:, p:p + 1],
                                                      in1=xT[:, p, 1:CH + 1, :].rearrange("p c t -> p (c t)"),
                                                      op0=ALU.mult, op1=ALU.add)
                    last.then_inc(s["mix_ok"], 1)
                dve.wait_ge(s["k_ok"], n)
                for p in range(2):
                    last = V.tensor_scalar(kk[:, p, :], k[:, p, :], vec["k_k"][:, p:p + 1], None, ALU.mult)
                last.then_inc(s["kk_ok"], 1)
                dve.wait_ge(s["kk_ok"], n)
                V.tensor_tensor(tmp, kk, kk, ALU.mult).then_inc(s["sq_ok"], 1)
                dve.wait_ge(s["w_ok"], n)
                V.tensor_tensor_scan(tmp2.rearrange("p a t -> p (a t)"), scan_keep, sig_w.rearrange("p a t -> p (a t)"), 0.0, ALU.mult,
                                     ALU.add).then_inc(s["scan_ok"], 1)
                dve.wait_ge(s["nrm_ok"], n)
                V.tensor_scalar(inv, inv, 1e-12, None, ALU.max).then_inc(s["nmax_ok"], 1)
                dve.wait_ge(s["nmax_ok"], n)
                V.reciprocal(inv, inv).then_inc(s["ninv_ok"], 1)
                dve.wait_ge(s["ninv_ok"], n)
                V.tensor_tensor(kk, kk, inv, ALU.mult).then_inc(s["kkn_ok"], 1)
                dve.wait_ge(s["a_ok"], n)
                dve.wait_ge(s["prod_ok"], n)
                for p in range(2):
                    last = V.tensor_scalar(tmp2[:, p, :], iclr[:, p, :], 1.0, vec["k_a"][:, p:p + 1], ALU.subtract, ALU.mult)
                last.then_inc(s["t1_ok"], 1)
                V.reciprocal(invp, prod[:, :, :, 1:L + 1]).then_inc(s["invp_ok"], 1)
                dve.wait_ge(s["t1_ok"], n)
                V.scalar_tensor_tensor(out=k, in0=tmp2, scalar=1.0, in1=k, op0=ALU.add, op1=ALU.mult).then_inc(s["k2_ok"], 1)
                dve.wait_ge(s["k2_ok"], n)
                for p in range(2):
                    last = V.scalar_tensor_tensor(out=tmp[:, p, :], in0=r[:, p, :], scalar=vec["r_k"][:, p:p + 1], in1=k[:, p, :],
                                                  op0=ALU.mult, op1=ALU.mult)
                last.then_inc(s["rkr_ok"], 1)
                kb = kk.rearrange("p a (b t) -> p a b t", b=BLK)
                dve.wait_ge(s["kkn_ok"], n)
                V.tensor_tensor(ar[:, :, :, 0:L], kb, prod[:, :, :, 0:L], ALU.mult)
                V.tensor_tensor(ar[:, :, :, L:2 * L], r.rearrange("p a (b t) -> p a b t", b=BLK), prod[:, :, :, 1:L + 1],
                                ALU.mult).then_inc(s["ar_ok"], 1)
                V.scalar_tensor_tensor(out=tmp2, in0=kk, scalar=-1.0, in1=iclr, op0=ALU.mult, op1=ALU.mult).then_inc(s["bn_ok"], 1)
                dve.wait_ge(s["invp_ok"], n)
                for h in range(2):
                    q = slice(64 * h, 64 * h + 64)
                    last = V.tensor_tensor(k_bd[q, :, :, L * h:L * h + L], k[q].rearrange("p a (b t) -> p a b t", b=BLK), invp[q],
                                           ALU.mult)
                last.then_inc(s["kbd_ok"], 1)
                dve.wait_ge(s["bn_ok"], n)
                for h in range(2):
                    q = slice(64 * h, 64 * h + 64)
                    last = V.tensor_tensor(b_bd[q, :, :, L * h:L * h + L], tmp2[q].rearrange("p a (b t) -> p a b t", b=BLK), invp[q],
                                           ALU.mult)
                last.then_inc(s["bbd_ok"], 1)
                dve.wait_ge(s["rt_ps"], n)
                dve.wait_ge(s["v2_ok"], n)
                V.tensor_tensor(rtv, ps[:, 4:6, :], v2nd, ALU.mult).then_inc(s["rtv_ok"], 1)
                dve.wait_ge(s["m_ps"], n)
                m1 = ps[:, 0:2, :].rearrange("p a (u x) -> p (a u) x", x=2 * L)
                m2 = ps[:, 2:4, :].rearrange("p a (u x) -> p (a u) x", x=2 * L)

                def per_unit(mask):
                    return mask.unsqueeze(1).broadcast_to([128, UN, L])

                V.tensor_tensor(u_c, m1[:, :, 0:L], per_unit(cst["pairs"]), ALU.mult).then_inc(s["u0_ok"], 1)
                strict4 = cst["strict_bd"].rearrange("p (q t) -> p q t", q=4)
                for q in range(4):
                    V.tensor_tensor(n_bd[:, :, L * q:L * q + L], m1[:, :, 0:L], per_unit(strict4[:, q, :]), ALU.mult)
                    V.tensor_tensor(mak_bd[:, :, L * q:L * q + L], m2[:, :, 0:L], per_unit(strict4[:, q, :]), ALU.mult)
                V.tensor_tensor(mrb, m1[:, :, L:2 * L], per_unit(cst["upto"]), ALU.mult)
                V.tensor_tensor(mrk, m2[:, :, L:2 * L], per_unit(cst["upto"]), ALU.mult).then_inc(s["masks_ok"], 1)
                dve.wait_ge(s["u0_ok"], n)
                V.tensor_tensor(u_c, u_c, per_unit(cst["eye"]), ALU.add).then_inc(s["u_ok"], 1)
                dve.wait_ge(s["u_ok"], 5 * i + 1)
                V.transpose(t_c.rearrange("p u t -> p (u t)"), u_c.rearrange("p u t -> p (u t)")).then_inc(s["t_ok"], 1)
                for lvl in range(4):
                    dve.wait_ge(s["x_ps"], 4 * i + lvl + 1)
                    V.tensor_tensor(x_c, ps[:, 0, :].rearrange("p (u t) -> p u t", u=UN),
                                    per_unit(cst["low"][:, L * lvl:L * lvl + L]), ALU.mult).then_inc(s["x_ok"], 1)
                    dve.wait_ge(s["t_ps"], 4 * i + lvl + 1)
                    V.tensor_tensor(t_c, ps[:, 1, :].rearrange("p (u t) -> p u t", u=UN), t_c, ALU.add).then_inc(s["t_ok"], 1)
                    dve.wait_ge(s["t_ok"], 5 * i + lvl + 2)
                    dve.wait_ge(s["ubd_ok"], 5 * i + lvl + 1)
                    V.transpose(u_c.rearrange("p u t -> p (u t)"), t_c.rearrange("p u t -> p (u t)")).then_inc(s["u_ok"], 1)
                dve.wait_ge(s["tok_ok"], 6 * n)
                V.tensor_tensor(v_cmp, v_tok[:, :, 0:HS], v_tok[:, :, HS:2 * HS], ALU.add).then_inc(s["vcmp_ok"], 1)
                pr = prod.rearrange("p a (c d e) t -> p a c d e t", c=CH, d=2)
                for c in range(CH):
                    dve.wait_ge(s["sa_ps"], 4 * i + c + 1)
                    V.tensor_copy(sa_c, ps[:, 3, 0:256].rearrange("p (u t) -> p u t", u=4)).then_inc(s["sa_ok"], 1)
                    dve.wait_ge(s["s_ps"], 4 * i + c + 1)
                    V.tensor_tensor(state.rearrange("p e u t -> p e (u t)"), ps[:, 4:6, 0:256],
                                    state.rearrange("p e u t -> p e (u t)"), ALU.add).then_inc(s["s_sum"], 1)
                    dve.wait_ge(s["s_sum"], 4 * i + c + 1)
                    for e in range(2):
                        last = V.tensor_tensor(state[:, e].rearrange("p (a d) t -> p a d t", a=2),
                                               state[:, e].rearrange("p (a d) t -> p a d t", a=2),
                                               pr[:, :, c, :, e, L:L + 1].broadcast_to([128, 2, 2, HS]), ALU.mult)
                    last.then_inc(s["s_ok"], 1)
                dve.wait_ge(s["mean_ps"], n)
                V.tensor_tensor(yd, yT, ps[:, 0:2, :], ALU.subtract).then_inc(s["yd_ok"], 1)
                dve.wait_ge(s["yd_ok"], n)
                V.tensor_tensor(tmp, yd, yd, ALU.mult).then_inc(s["ysq_ok"], 1)
                dve.wait_ge(s["ysd_ok"], n)
                V.reciprocal(inv, inv).then_inc(s["yinv_ok"], 1)
                dve.wait_ge(s["yinv_ok"], n)
                V.tensor_tensor(yd, yd, inv, ALU.mult).then_inc(s["yz1"], 1)
                dve.wait_ge(s["yz1"], n)
                for p in range(2):
                    last = V.tensor_scalar(yd[:, p, :], yd[:, p, :], vec["ln_w"][:, p:p + 1], vec["ln_b"][:, p:p + 1], ALU.mult, ALU.add)
                last.then_inc(s["yz2"], 1)
                dve.wait_ge(s["yz2"], n)
                V.tensor_tensor(yd, yd, rtv, ALU.add).then_inc(s["yz3"], 1)
                dve.wait_ge(s["yz3"], n)
                V.tensor_tensor(tmp, yd, gate, ALU.mult).then_inc(s["z_ok"], 1)
                dve.wait_ge(s["o_ps"], n)
                rows = res[:, bass.ds(i * CH, CH), :].rearrange("p t c -> p (t c)")
                V.tensor_tensor(rows, ps[:, 4:6, :].rearrange("p a x -> p (a x)"), rows, ALU.add).then_inc(s["slab_ok"], 1)
            dve.wait_ge(s["slab_ok"], SLABS + 1)
            for t in range(TILES):
                V.bn_stats(stats[:, t, :], res[:, t, :]).then_inc(s["stats2_ok"], 1)
            for t in range(TILES):
                dve.wait_ge(s["stats2_ok"], t + 1)
                last = V.bn_aggr(moments[:, t, :], stats[:, t, :])
            last.then_inc(s["mom2_ok"], 1)
            dve.wait_ge(s["ffn_in"], 64)
            V.tensor_tensor(wgsq[0:E, :], wg_sb[0:E, :], wg_sb[0:E, :], ALU.mult).then_inc(s["wgsq_ok"], 1)
            dve.wait_ge(s["wgsq_ok"], 1)
            V.reduce_sum(wgs[0:E, 0:1], wgsq[0:E, :], axis=AX.X).then_inc(s["wgsum_ok"], 1)
            dve.wait_ge(s["sd2_ok"], 1)
            V.reciprocal(rstd, stdev).then_inc(s["rstd2_ok"], 1)
            dve.wait_ge(s["rstd2_ok"], 1)
            for t in range(TILES):
                V.tensor_scalar(xn2[:, t, :], res[:, t, :], moments[:, t, 0:1], rstd[:, t:t + 1],
                                ALU.subtract, ALU.mult).then_inc(s["xn2_ok"], 1)
            dve.wait_ge(s["wgsd_ok"], 1)
            V.tensor_scalar(wgs[0:E, 1:2], wgs[0:E, 1:2], 1e-4, None, ALU.max).then_inc(s["wgmax_ok"], 1)
            dve.wait_ge(s["wgmax_ok"], 1)
            V.reciprocal(wgs[0:E, 0:1], wgs[0:E, 1:2]).then_inc(s["wginv_ok"], 1)
            dve.wait_ge(s["wginv_ok"], 1)
            V.tensor_scalar(wgn[0:E, :], wg_sb[0:E, :], wgs[0:E, 0:1], None, ALU.mult).then_inc(s["wgn_ok"], 1)
            dve.wait_ge(s["wgT_ps"], 1)
            V.tensor_copy(wgT[0:G, :], ps[0:G, 4, 0:E]).then_inc(s["wgT_ok"], 1)
            dve.wait_ge(s["lg2_ps"], 1)
            V.tensor_copy(logits, ps[:, 5, 0:TILES * E].rearrange("p (t e) -> p t e", e=E)).then_inc(s["lg2_ok"], 1)
            dve.wait_ge(s["lg2_ok"], 1)
            for t in range(TILES):
                V.max(top[:, t, :], logits[:, t, :]).then_inc(s["topv_ok"], 1)
            for t in range(TILES):
                dve.wait_ge(s["topv_ok"], t + 1)
                last = V.max_index(topi[:, t, :], top[:, t, :], logits[:, t, :])
            last.then_inc(s["topi_ok"], 1)
            V.tensor_tensor(ex, logits, top[:, :, 0:1].broadcast_to([128, TILES, E]), ALU.subtract).then_inc(s["dif_ok"], 1)
            dve.wait_ge(s["topi_ok"], 1)
            V.tensor_copy(topf[:, :, 0:1], topi[:, :, 0:1]).then_inc(s["topf_ok"], 1)
            dve.wait_ge(s["topf_ok"], 1)
            V.tensor_tensor(onehot, cst["iota"].unsqueeze(1).broadcast_to([128, TILES, E]),
                            topf[:, :, 0:1].broadcast_to([128, TILES, E]), ALU.is_equal).then_inc(s["onehot_ok"], 1)
            dve.wait_ge(s["exp_ok"], 1)
            V.reduce_sum(esum, ex, axis=AX.X).then_inc(s["esum_ok"], 1)
            dve.wait_ge(s["esum_ok"], 1)
            V.reciprocal(score, esum).then_inc(s["score_ok"], 1)
            dve.wait_ge(s["score_ok"], 1)
            dve.wait_ge(s["onehot_ok"], 1)
            V.tensor_tensor(picked, onehot, score.unsqueeze(2).broadcast_to([128, TILES, E]), ALU.mult).then_inc(s["picked_ok"], 1)
            dve.wait_ge(s["picked_ok"], 1)
            for t in range(0, TILES, CH):
                dve.wait_ge(s["pT_ps"], t // CH + 1)
                V.tensor_copy(pickedT[0:E, t * 128:(t + CH) * 128], ps[0:E, 6, :]).then_inc(s["pT_ok"], 1)
            for t in range(TILES):
                dve.wait_ge(s["b2_ps"], t + 1)
                V.tensor_tensor(res[:, t, :], ps[:, 4 + t % 2, 0:C], res[:, t, :], ALU.add).then_inc(s["b2_ok"], 1)
            for e in range(E):
                for t in range(TILES):
                    g = e * TILES + t
                    dve.wait_ge(s["o2_ps"], g + 1)
                    if e == 0:
                        dve.wait_ge(s["b2_ok"], t + 1)
                    else:
                        dve.wait_ge(s["o2_ok"], g - TILES + 1)
                    V.scalar_tensor_tensor(out=res[:, t, :], in0=ps[:, 4 + g % 4, 0:C], scalar=picked[:, t, e:e + 1],
                                           in1=res[:, t, :], op0=ALU.mult, op1=ALU.add).then_inc(s["o2_ok"], 1)

        @block.tensor
        def _(pe):
            mm = nc.tensor.matmul
            pe.wait_ge(s["consts_in"], 16 * (len(CONSTS) + 2))
            pe.wait_ge(s["weights_in"], 16 * 12)
            pe.wait_ge(s["zeroed"], 1)
            with pe.Fori(0, SLABS) as i:
                n = i + 1
                pe.wait_ge(s["xn_ok"], n)
                for p in range(2):
                    for c in range(CH):
                        last = nc.tensor.transpose(ps[:, p, c * 128:(c + 1) * 128], xn[:, c, p * 128:(p + 1) * 128], ident)
                last.then_inc(s["xT_ps"], 1)

                def full(w, src, bank):
                    for m in range(2):
                        for kt in range(2):
                            last = mm(ps[:, bank + m, :], w[:, kt, m * 128:(m + 1) * 128], src[:, kt, :], start=kt == 0, stop=kt == 1)
                    return last

                def down(w, src, bank, rows):
                    for kt in range(2):
                        last = mm(ps[0:rows, bank, :], w[:, kt, :], src[:, kt, :], start=kt == 0, stop=kt == 1)
                    return last

                def up(w, src, bank, rows):
                    for m in range(2):
                        last = mm(ps[:, bank + m, :], w[0:rows, m * 128:(m + 1) * 128], src[0:rows, :], start=True, stop=True)
                    return last

                pe.wait_ge(s["xT_ok"], n)
                pe.wait_ge(s["mix_ok"], 6 * i + 1)
                full(w_sb["k"], mix[0], 0).then_inc(s["k_ps"], 1)
                pe.wait_ge(s["mix_ok"], 6 * i + 2)
                full(w_sb["r"], mix[1], 2).then_inc(s["r_ps"], 1)
                pe.wait_ge(s["mix_ok"], 6 * i + 3)
                full(w_sb["v"], mix[2], 4).then_inc(s["v_ps"], 1)
                down(v1_sb, mix[2], 6, 32).then_inc(s["lv_ps"], 1)
                pe.wait_ge(s["mix_ok"], 6 * i + 4)
                down(w1_sb, mix[0], 7, 64).then_inc(s["lw_ps"], 1)
                pe.wait_ge(s["k_ok"], n)
                pe.wait_ge(s["lv_ok"], n)
                up(v2_sb, low_v, 0, 32).then_inc(s["vg_ps"], 1)
                pe.wait_ge(s["mix_ok"], 6 * i + 5)
                down(a1_sb, mix[1], 6, 64).then_inc(s["la_ps"], 1)
                pe.wait_ge(s["r_ok"], n)
                pe.wait_ge(s["lw_ok"], n)
                up(w2_sb, low_w, 2, 64).then_inc(s["w_ps"], 1)
                pe.wait_ge(s["mix_ok"], 6 * i + 6)
                down(g1_sb, mix[2], 7, 128).then_inc(s["lg_ps"], 1)
                pe.wait_ge(s["v_ok"], n)
                pe.wait_ge(s["la_ok"], n)
                up(a2_sb, low_a, 4, 64).then_inc(s["a_ps"], 1)
                pe.wait_ge(s["vg_ok"], n)
                pe.wait_ge(s["lg_ok"], n)
                up(g2_sb, low_g, 0, 128).then_inc(s["g_ps"], 1)
                pe.wait_ge(s["sq_ok"], n)
                pe.wait_ge(s["w_ok"], n)
                for p in range(2):
                    last = mm(ps[:, 2 + p, :], cst["ones_bd"], tmp[:, p, :], start=True, stop=True)
                last.then_inc(s["nrm_ps"], 1)
                pe.wait_ge(s["rkr_ok"], n)
                pe.wait_ge(s["a_ok"], n)
                for p in range(2):
                    last = mm(ps[:, 4 + p, :], cst["ones_bd"], tmp[:, p, :], start=True, stop=True)
                last.then_inc(s["rt_ps"], 1)
                pe.wait_ge(s["kbd_ok"], n)
                pe.wait_ge(s["bbd_ok"], n)
                pe.wait_ge(s["ar_ok"], n)
                pe.wait_ge(s["g_ok"], n)
                pe.wait_ge(s["nrm_ok"], n)
                for src, bank in ((b_bd, 0), (k_bd, 2)):
                    for p in range(2):
                        for u in range(BLK):
                            q, col = 64 * (u % 2), ((p * BLK + u) // 2) * 2 * L
                            last = mm(ps[q:q + 64, bank + col // 512, col % 512:col % 512 + 2 * L], src[:, p, u, :], ar[:, p, u, :],
                                      start=True, stop=True)
                last.then_inc(s["m_ps"], 1)
                pe.wait_ge(s["rtv_ok"], n)
                pe.wait_ge(s["vbd_ok"], n)
                for j, src in enumerate((b_bd, b_bd, k_bd, k_bd, v_bd, v_bd)):
                    if j >= 2:
                        pe.wait_ge(s["tok_ok"], 6 * i + j - 1)
                    for w in range(8):
                        last = nc.tensor.transpose(ps[:, 4 + 2 * (j % 2) + w // 4, (w % 4) * 128:(w % 4 + 1) * 128],
                                                   src[:, j % 2, 2 * w:2 * w + 2, :].rearrange("p a b -> p (a b)"), ident)
                    last.then_inc(s["tok_ps"], 1)
                pe.wait_ge(s["masks_ok"], n)
                for lvl in range(4):
                    pe.wait_ge(s["t_ok"], 5 * i + lvl + 1)
                    for u in range(UN):
                        last = mm(ps[:, 0, u * L:(u + 1) * L], n_bd[:, u, :], t_c[:, u, :], start=True, stop=True)
                    last.then_inc(s["x_ps"], 1)
                    pe.wait_ge(s["x_ok"], 4 * i + lvl + 1)
                    pe.wait_ge(s["ubd_ok"], 5 * i + lvl + 1)
                    for u in range(UN):
                        last = mm(ps[:, 1, u * L:(u + 1) * L], u_bd[:, u, :], x_c[:, u, :], start=True, stop=True)
                    last.then_inc(s["t_ps"], 1)
                pe.wait_ge(s["ubd_ok"], 5 * n)
                pe.wait_ge(s["vcmp_ok"], n)
                pe.wait_ge(s["abd_ok"], n)
                for c in range(CH):
                    if c:
                        pe.wait_ge(s["s_ok"], 4 * i + c)
                        pe.wait_ge(s["w_ok_c"], 4 * i + c)
                    for p in range(2):
                        for d in range(2):
                            u, x = unit(p, c, 2 * d), (2 * p + d) * HS
                            mm(ps[:, 2, x:x + HS], mak_bd[:, u, :], v_cmp[:, u, :], start=True, stop=False, skip_group_check=True)
                            for e in range(2):
                                last = mm(ps[64 * e:64 * e + 64, 2, x:x + HS], a_bd[:, p, c * B + 2 * d + e, :], state[:, e, 2 * p + d, :],
                                          start=False, stop=True, skip_group_check=True)
                    last.then_inc(s["w_ps_c"], 1)
                    pe.wait_ge(s["w_ok_c"], 4 * i + c + 1)
                    if c:
                        pe.wait_ge(s["sabd_ok"], 4 * i + c)
                        pe.wait_ge(s["sa_ok"], 4 * i + c)
                    for p in range(2):
                        for d in range(2):
                            last = mm(ps[:, 3, (2 * p + d) * HS:(2 * p + d + 1) * HS], u_bd[:, unit(p, c, 2 * d), :], w_s[:, 2 * p + d, :],
                                      start=True, stop=True)
                    last.then_inc(s["sa_ps"], 1)
                    pe.wait_ge(s["sa_ok"], 4 * i + c + 1)
                    for e in range(2):
                        q = slice(64 * e, 64 * e + 64)
                        for p in range(2):
                            for d in range(2):
                                u, x = unit(p, c, 2 * d), (2 * p + d) * HS
                                mm(ps[:, 4 + e, x:x + HS], k_tok[q, u, :], v_cmp[q, u, :], start=True, stop=False)
                                last = mm(ps[:, 4 + e, x:x + HS], b_tok[q, u, :], sa_c[q, 2 * p + d, :], start=False, stop=True)
                    last.then_inc(s["s_ps"], 1)
                    pe.wait_ge(s["sabd_ok"], 4 * i + c + 1)
                    if c:
                        pe.wait_ge(s["sbd_ok"], 4 * i + c)
                    for e in range(2):
                        q = slice(64 * e, 64 * e + 64)
                        for p in range(2):
                            for d in range(2):
                                u, x = unit(p, c, 2 * d), unit(p, c, 2 * d) * L
                                mm(ps[:, 6 + e, x:x + L], state_bd[:, e, 2 * p + d, :], ar[:, p, c * B + 2 * d + e, L:2 * L],
                                   start=True, stop=False)
                                mm(ps[:, 6 + e, x:x + L], v_tok[q, u, :], mrk[q, u, :], start=False, stop=False)
                                last = mm(ps[:, 6 + e, x:x + L], sa_bd[q, 2 * p + d, :], mrb[q, u, :], start=False, stop=True)
                    last.then_inc(s["y_ps"], 1)
                pe.wait_ge(s["yT_ok"], n)
                for p in range(2):
                    last = mm(ps[:, p, :], cst["mean_bd"], yT[:, p, :], start=True, stop=True)
                last.then_inc(s["mean_ps"], 1)
                pe.wait_ge(s["ysq_ok"], n)
                for p in range(2):
                    last = mm(ps[:, 2 + p, :], cst["mean_bd"], tmp[:, p, :], start=True, stop=True)
                last.then_inc(s["var_ps"], 1)
                pe.wait_ge(s["z_ok"], n)
                for c in range(CH):
                    for p in range(2):
                        last = mm(ps[:, 4 + c // 2, (c % 2) * C:(c % 2 + 1) * C], tmp[:, p, c * 128:(c + 1) * 128], w_sb["o"][:, p, :],
                                  start=p == 0, stop=p == 1)
                last.then_inc(s["o_ps"], 1)
            pe.wait_ge(s["slab_ok"], SLABS + 1)
            for t in range(0, TILES, CH):
                pe.wait_ge(s["xn2_ok"], t + CH)
                if t:
                    pe.wait_ge(s["xT2_ok"], t // CH)
                for p in range(2):
                    for c in range(CH):
                        last = nc.tensor.transpose(ps[:, p, c * 128:(c + 1) * 128], xn2[:, t + c, p * 128:(p + 1) * 128], ident)
                last.then_inc(s["xT2_ps"], 1)
            pe.wait_ge(s["ffn_in"], 64)
            for t in range(SLABS):
                pe.wait_ge(s["xT2_ok"], t + 1)
                if t >= 2:
                    pe.wait_ge(s["red_ok"], t - 1)
                for p in range(2):
                    last = mm(ps[0:G, 2 + t % 2, :], wred_sb[:, p, :], xT2[:, p, t * NT:(t + 1) * NT], start=p == 0, stop=p == 1)
                last.then_inc(s["red_ps"], 1)
            pe.wait_ge(s["wgn_ok"], 1)
            nc.tensor.transpose(ps[0:G, 4, 0:E], wgn[0:E, :], ident[0:E, 0:E]).then_inc(s["wgT_ps"], 1)
            pe.wait_ge(s["wgT_ok"], 1)
            pe.wait_ge(s["red_ok"], SLABS)
            for t in range(TILES):
                last = mm(ps[:, 5, t * E:(t + 1) * E], red[0:G, t * 128:(t + 1) * 128], wgT[0:G, :], start=True, stop=True)
            last.then_inc(s["lg2_ps"], 1)
            pe.wait_ge(s["picked_ok"], 1)
            for t in range(0, TILES, CH):
                if t:
                    pe.wait_ge(s["pT_ok"], t // CH)
                for c in range(CH):
                    last = nc.tensor.transpose(ps[0:E, 6, c * 128:(c + 1) * 128], picked[:, t + c, :], ident)
                last.then_inc(s["pT_ps"], 1)
            for t in range(TILES):
                pe.wait_ge(s["pT_ok"], t // CH + 1)
                if t >= 2:
                    pe.wait_ge(s["b2_ok"], t - 1)
                mm(ps[:, 4 + t % 2, 0:C], pickedT[0:E, t * 128:(t + 1) * 128], b2_sb[0:E, :], start=True, stop=True).then_inc(s["b2_ps"], 1)
            pe.wait_ge(s["b2_ok"], TILES)
            GROUPS = E * SLABS

            def hidden(g):
                e, sl = g // SLABS, g % SLABS
                if sl == 0:
                    pe.wait_ge(s[f"wexp_in{e % 2}"], 32 * (e // 2 + 1))
                for m in range(HC):
                    if g:
                        pe.wait_ge(s["h_ok"], (g - 1) * HC + m + 1)
                    for kt in range(2):
                        last = mm(ps[:, m, :], W1_sb[e % 2][:, kt, m * 128:(m + 1) * 128], xT2[:, kt, sl * NT:(sl + 1) * NT],
                                  start=kt == 0, stop=kt == 1)
                    last.then_inc(s["h_ps"], 1)

            def project(g):
                e, sl = g // SLABS, g % SLABS
                pe.wait_ge(s["h_ok"], (g + 1) * HC)
                for c in range(CH):
                    t = g * CH + c
                    if t >= 4:
                        pe.wait_ge(s["o2_ok"], t - 3)
                    for m in range(HC):
                        last = mm(ps[:, 4 + t % 4, 0:C], hT[g % 2][:, m, c * 128:(c + 1) * 128], W2_sb[e % 2][:, m, :],
                                  start=m == 0, stop=m == HC - 1)
                    last.then_inc(s["o2_ps"], 1)

            hidden(0)
            for g in range(1, GROUPS):
                hidden(g)
                project(g - 1)
            project(GROUPS - 1)


def kernel(**inputs):
    import numpy as np
    import concourse.bacc as bacc
    from concourse.bass_utils import run_bass_kernel_spmd

    a = {name: np.asarray(value) for name, value in inputs.items()}
    P = "L0_attn_"

    def two(w):
        return np.ascontiguousarray(w.reshape(2, 128, -1).transpose(1, 0, 2))

    row = np.arange(128)
    t = row % L
    col = np.arange(L)
    f = np.float32
    bd64 = (row[:, None] // 64 == row[None, :] // 64).astype(f)
    strict = (t[:, None] < col[None, :]).astype(f)
    low = [((t[:, None] // w == col[None, :] // w) & (t[:, None] % w >= w // 2) & (col[None, :] % w < w // 2)).astype(f)
           for w in (4, 8, 16, 32)]
    made = {
        "ident": np.eye(128, dtype=f), "ones_bd": bd64, "mean_bd": bd64 / f(HS),
        "strict_bd": ((row[:, None] // L == row[None, :] // L) & (t[:, None] < row[None, :] % L)).astype(f),
        "upto": (t[:, None] <= col[None, :]).astype(f),
        "pairs": strict * (t[:, None] // 2 == col[None, :] // 2).astype(f),
        "eye": (t[:, None] == col[None, :]).astype(f),
        "low": np.concatenate(low, axis=1),
        "half": (row[:, None] // L % 2 == np.arange(2)[None, :]).astype(f),
        "iota": np.broadcast_to(np.arange(E, dtype=f), (128, E)),
    }
    arrays = {
        "table": np.ascontiguousarray(a["L0_tok_weight"].T),
        "tokens": np.ascontiguousarray(a["x"].reshape(B, TILES, L).transpose(0, 2, 1).reshape(128, TILES)).view(np.uint32),
        "tok_bias": np.ascontiguousarray(np.broadcast_to(a["L0_tok_bias"], (128, C))),
        "cvec": np.ascontiguousarray(np.concatenate([a[P + v].reshape(2, 128).T for v in VECS], axis=1)),
        "consts": np.ascontiguousarray(np.concatenate([made[name] for name, _ in CONSTS], axis=1)),
        "W": np.stack([two(a[P + "W" + c]) for c in "rkvo"]),
        "w1": two(a[P + "w1"]), "w2": a[P + "w2"], "a1": two(a[P + "a1"]), "a2": a[P + "a2"],
        "v1": two(a[P + "v1"]), "v2": a[P + "v2"], "g1": two(a[P + "g1"]), "g2": a[P + "g2"],
        "w_red": two(a["L0_ffn_w_red"]), "wg": a["L0_ffn_wg"],
        "W1": np.ascontiguousarray(a["L0_ffn_W1"].reshape(E, 2, 128, HID).transpose(0, 2, 1, 3)),
        "b1": np.ascontiguousarray(a["L0_ffn_b1"].reshape(E, HC, 128).transpose(2, 0, 1)),
        "W2": np.ascontiguousarray(a["L0_ffn_W2"].reshape(E, HC, 128, C).transpose(0, 2, 1, 3)),
        "b2": a["L0_ffn_b2"],
    }
    arrays = {name: np.ascontiguousarray(value) for name, value in arrays.items()}
    nc = bacc.Bacc("TRN2", target_bir_lowering=False, num_devices=1)
    args = [nc.dram_tensor(name, value.shape, mybir.dt.from_np(value.dtype), kind="ExternalInput").ap()
            for name, value in arrays.items()]
    args.append(nc.dram_tensor("out", (TILES, 128, C), F32, kind="ExternalOutput").ap())
    build(nc, *args)
    got = run_bass_kernel_spmd(nc, [arrays], core_ids=[0]).results[0]["out"]
    return np.ascontiguousarray(np.asarray(got).reshape(TILES, B, L, C).transpose(1, 0, 2, 3).reshape(B, T, C))
```

```python
from contextlib import ExitStack

import concourse.bass as bass
from concourse import mybir

F32 = mybir.dt.float32
U32 = mybir.dt.uint32
ALU = mybir.AluOpType
ACT = mybir.ActivationFunctionType
AX = mybir.AxisListType

B, T, C = 4, 512, 256
H, HS = 4, 64
L = 32
TILES = T // L
CH = 2
SLABS = TILES // CH
BLK = CH * B
NT = BLK * L
UN = 2 * CH * 2
E, HID, G = 8, 512, 16
HC = HID // 128
FT = 4
FN = FT * 128
ROUTE = """wgsq wgmax wginv lg2 topi topf count scan_t more start tiles end base passed start2 place place2 place3 owner owner2 esum""".split()
SORTED = TILES + E
DECAY = -0.6065306597126334
LN_EPS, GN_EPS = 1e-5, 0.00064
LIFT = 20
LN2 = 0.6931471805599453

ORDER = """Q.start P.k Q.X0 P.r Q.T0 P.v Q.X1 P.lw Q.T1 P.vg P.la Q.X2 P.w P.lg Q.T2 P.a P.g Q.X3 P.norm Q.T3 Q.W0 P.decay
Q.A0 P.key Q.S0 P.ar Q.W1 P.kbd Q.A1 P.bonus P.tok0 P.tok1 P.bbd Q.S1 P.tok2 P.tok3 Q.mean P.M P.tok4 P.tok5 F.xT Q.var
P.masks F.xx Q.out Q.add""".split()
AHEAD = {"Q": 0, "P": 1, "F": 2}
VECS = ["x_r", "x_w", "x_k", "x_v", "x_a", "x_g", "w0", "a0", "v0", "k_k", "k_a", "r_k", "ln_w", "ln_b"]
CONSTS = [("ident", 128), ("ones_bd", 128), ("mean_bd", 128), ("strict_bd", 128), ("upto", 2 * L), ("pairs", L),
          ("eye", L), ("low", 4 * L), ("half", 2), ("iota", E),
          ("blocks", 128), ("before", 128), ("tile_rows", TILES), ("tile_no", SORTED)]


def after(step):
    return ROUTE.index(step) + 1


def build(nc, table, tokens, tok_bias, cvec, consts, W, w1, w2, a1, a2, v1, v2, g1, g2, w_red, wg, W1, b1, W2, b2, sorted_x, sorted_o, out):
    ctx = ExitStack()
    with ctx:
        def sem(name):
            return ctx.enter_context(nc.semaphore(name))

        at = [0]
        WORDS = 52000
        arena = ctx.enter_context(nc.sbuf_tensor("arena", [128, WORDS], F32))

        def carve(*dims):
            n = 1
            for d in dims:
                n *= d
            flat = arena[:, at[0]:at[0] + n]
            at[0] += n
            assert at[0] <= WORDS, at[0]
            if len(dims) == 1:
                return flat
            names = "abcdef"[:len(dims)]
            return flat.rearrange(f"p ({' '.join(names)}) -> p {' '.join(names)}",
                                  **{k: d for k, d in zip(names[:-1], dims[:-1])})

        res = carve(TILES, C)
        cst = {}
        for name, width in CONSTS:
            cst[name] = carve(width)
        cv = carve(2 * len(VECS))
        vec = {name: cv[:, 2 * k:2 * k + 2] for k, name in enumerate(VECS)}
        stats = carve(TILES, 6)
        moments = carve(TILES, 2)
        stdev = carve(TILES)
        rstd = carve(TILES)
        eps_ln = carve(1)
        eps_gn = carve(1)
        lift = carve(1)
        ids = carve(TILES).bitcast(U32)
        zero_row = carve(C)
        ident = cst["ident"]
        shared = at[0]

        bias_rows = carve(C)
        w_sb = {k: carve(2, C) for k in "rkvo"}
        w1_sb, a1_sb, v1_sb, g1_sb = carve(2, 64), carve(2, 64), carve(2, 32), carve(2, 128)
        w2_sb, a2_sb, v2_sb, g2_sb = carve(C), carve(C), carve(C), carve(C)

        xT = carve(2, CH + 1, B * L)
        scan_keep = carve(2 * NT)
        mix = [carve(2, NT) for _ in range(3)]
        r, k, v = carve(2, NT), carve(2, NT), carve(2, NT)
        low_v, low_w, low_a, low_g = carve(NT), carve(NT), carve(NT), carve(NT)
        vgate, sig_w, iclr, kk = carve(2, NT), carve(2, NT), carve(2, NT), carve(2, NT)
        inv, v2nd = carve(2, NT), carve(2, NT)
        at_tmp = at[0]
        tmp, tmp2 = carve(2, NT), carve(2, NT)
        at[0] = at_tmp
        xn, xx = carve(CH, C), carve(2, BLK, L)
        invp = carve(2, BLK, L)
        b_bd, k_bd, v_bd = (carve(2, BLK, 2 * L) for _ in range(3))
        prod = [carve(2, BLK, L + 1) for _ in range(2)]
        ar = [carve(2, BLK, 2 * L) for _ in range(2)]
        a_bd = [carve(2, BLK, 2 * L) for _ in range(2)]
        gate, rtv = [carve(2, NT) for _ in range(2)], [carve(2, NT) for _ in range(2)]
        n_bd, mak_bd = [carve(UN, 128) for _ in range(2)], [carve(UN, 128) for _ in range(2)]
        b_tok, k_tok, v_tok = ([carve(UN, 128) for _ in range(2)] for _ in range(3))
        v_cmp, v_e = [carve(UN, HS) for _ in range(2)], [carve(UN, 2 * HS) for _ in range(2)]
        mrb, mrk = ([carve(UN, 2 * L) for _ in range(2)] for _ in range(2))
        u_0 = [carve(UN, L) for _ in range(2)]
        u_bd = carve(UN, 128)
        t_c, u_c, x_c = carve(UN, L), carve(UN, L), carve(UN, L)
        state = carve(2 * B, HS)
        state_bd = carve(2 * B, 128)
        w_s, sa_e, sa_bd = carve(4, HS), carve(4, 128), carve(4, 128)
        yT, yd, ysq = carve(2, NT), carve(2, NT), carve(2, NT)
        yinv = inv
        attn_end = at[0]

        at[0] = shared
        xn2 = carve(TILES, C)
        xT2 = carve(2, TILES * 128)
        red = carve(TILES * 128)
        logits, ex, onehot, picked = carve(TILES, E), carve(TILES, E), carve(TILES, E), carve(TILES, E)
        top, topf = carve(TILES, E), carve(TILES, E)
        topi = carve(TILES, E).bitcast(U32)
        esum, score = carve(TILES), carve(TILES)
        pickedT = carve(TILES * 128)
        wred_sb = carve(2, G)
        wg_sb, wgn, wgsq, wgT = carve(G), carve(G), carve(G), carve(E)
        wgs = carve(2)
        b2_sb = carve(C)
        W1_sb = carve(E * 2 * HID)
        W2_sb = carve(E * HC * C)
        b1_sb = carve(E * HID)
        ones_sb = carve(128)
        keep_e = carve(E * TILES)
        count, upto_t, start_t = carve(E, TILES), carve(E, TILES), carve(E, TILES)
        more, tiles_e, end_e, base_e = carve(E, TILES), carve(E), carve(E), carve(E)
        place_e, place_f = carve(TILES, E), carve(TILES)
        place = carve(TILES).bitcast(U32)
        passed, owner_f = carve(SORTED, E), carve(SORTED)
        owner = carve(SORTED).bitcast(U32)
        x_s = [carve(C) for _ in range(2)]
        x_sT = [carve(2, 128) for _ in range(2)]
        h_pre = [carve(HID) for _ in range(2)]
        h_act = [carve(HID) for _ in range(2)]
        hT = [carve(HC, 128) for _ in range(2)]
        o_s = [carve(C) for _ in range(2)]
        back = carve(TILES, C)

        ps = ctx.enter_context(nc.psum_tensor("ps", [128, 8, 512], F32))

        names = """route consts_in weights_in ids_in rows_in ffn_in wexp_in0 wexp_in1 biased stats1_ok mom1_ok sd1_ok zeroed rstd1_ok
        xn_ok xT_ps xT_carry xT_ok xx_ok mix_ok  k_ps r_ps v_ps lv_ps lw_ps vg_ps la_ps w_ps lg_ps a_ps g_ps
        k_ok r_ok v_ok lv_ok lw_ok vg_ok la_ok w_ok lg_ok a_ok g_ok
        kk_ok sq_ok nrm_ps nrm_ok nmax_ok kkn_ok scan_ok prod_ok invp_ok t1_ok k2_ok rkr_ok rt_ps rtv_ok
        lnk_ok ubd2_ok vd_ok vs_ok v2_ok vbd_ok ar_ok abd_ok bn_ok bbd_ok kbd_ok m_ps tok_ps tok_ok vcmp_ok
        masks_ok pairs_ok u0_ok x_ps x_ok t_ps t_ok u_ok ubd_ok
        w_ps_c w_ok_c sa_ps sa_ok sabd_ok s_ps y_ps s_sum s_ok sbd_ok yT_ok mean_ps yd_ok ysq_ok var_ps ysd_ok
        lny_ok ve_ok yz1 yz2 yz3 z_ok o_ps slab_ok
        stats2_ok mom2_ok sd2_ok rstd2_ok xn2_ok xT2_ps xT2_ok red_ps red_ok  wgsum_ok wgsd_ok   wgn_ok
        wgT_ps wgT_ok lg2_ps  topv_ok   onehot_ok dif_ok exp_ok  score_ok picked_ok
        pT_ps pT_ok b2_ps b2_ok zero_ok cleared ffn_set wexp_in tot_ps   
                place_u    owner_u
        scattered xs_in0 xs_in1 xsT_ps xsT_ok h_ps pre_ok act_ok hT_ps hT_ok o2_ps o2_ok o_out0 o_out1 back_in0 back_in1 back_in2 back_in3 final_ok out_done""".split()
        s = {n: sem(n) for n in names}

        block = ctx.enter_context(nc.Block())

        def unit(p, c, b):
            return (p * CH + c) * 2 + b // 2

        UPDATES = ["Q.start", "Q.T0", "Q.T1", "Q.T2", "Q.T3"]

        def pipeline(engine, emit):
            for turn in (-2, -1):
                for step in ORDER:
                    slab = turn + AHEAD[step[0]]
                    if slab >= 0:
                        emit(step, slab, slab % 2)
            with engine.Fori(0, SLABS // 2 - 1) as j:
                for half in range(2):
                    for step in ORDER:
                        ahead = half + AHEAD[step[0]]
                        emit(step, 2 * j + ahead, ahead % 2)
            for turn in (SLABS - 2, SLABS - 1):
                for step in ORDER:
                    slab = turn + AHEAD[step[0]]
                    if slab < SLABS:
                        emit(step, slab, slab % 2)

        @block.sync
        def _(sp):
            at_c = 0
            for name, width in CONSTS:
                sp.dma_start(cst[name], consts[:, at_c:at_c + width]).then_inc(s["consts_in"], 16)
                at_c += width
            sp.dma_start(cv, cvec[:, :]).then_inc(s["consts_in"], 16)
            sp.dma_start(bias_rows, tok_bias[:, :]).then_inc(s["consts_in"], 16)
            for n, key in enumerate("rkvo"):
                sp.dma_start(w_sb[key], W[n]).then_inc(s["weights_in"], 16)
            for dst, src in ((w1_sb, w1), (a1_sb, a1), (v1_sb, v1), (g1_sb, g1)):
                sp.dma_start(dst, src[:, :, :]).then_inc(s["weights_in"], 16)
            sp.wait_ge(s["zero_ok"], 1)
            sp.dma_start(sorted_x.rearrange("(q p) c -> p q c", p=128),
                         zero_row.unsqueeze(1).broadcast_to([128, SORTED, C])).then_inc(s["cleared"], 16)
            for dst, src, rows in ((w2_sb, w2, 64), (a2_sb, a2, 64), (v2_sb, v2, 32), (g2_sb, g2, 128)):
                sp.dma_start(dst[0:rows, :], src[:, :]).then_inc(s["weights_in"], 16)
            sp.wait_ge(s["slab_ok"], SLABS + 1)
            sp.dma_start(wred_sb, w_red[:, :, :]).then_inc(s["ffn_in"], 16)
            sp.dma_start(wg_sb[0:E, :], wg[:, :]).then_inc(s["ffn_in"], 16)
            sp.dma_start(b2_sb[0:E, :], b2[:, :]).then_inc(s["ffn_in"], 16)
            for e in range(E):
                sp.dma_start(W1_sb[:, e * 2 * HID:(e + 1) * 2 * HID], W1[e]).then_inc(s["wexp_in"], 16)
                sp.dma_start(W2_sb[:, e * HC * C:(e + 1) * HC * C], W2[e]).then_inc(s["wexp_in"], 16)
            sp.dma_start(b1_sb, b1[:, :]).then_inc(s["wexp_in"], 16)
            sp.wait_ge(s["scattered"], 16 * TILES)
            for q in range(2):
                sp.dma_start(x_s[q], sorted_x[q * 128:(q + 1) * 128, :]).then_inc(s[f"xs_in{q}"], 16)
            with sp.Fori(0, SORTED // 2 - 1) as j:
                for b in range(2):
                    q = 2 * j + b
                    sp.wait_ge(s["xsT_ps"], q + 1)
                    sp.dma_start(x_s[b], sorted_x[bass.ds((q + 2) * 128, 128), :]).then_inc(s[f"xs_in{b}"], 16)
                for b in range(2):
                    q = 2 * j + b
                    sp.wait_ge(s["o2_ok"], q + 1)
                    sp.dma_start(sorted_o[bass.ds(q * 128, 128), :], o_s[b]).then_inc(s[f"o_out{b}"], 16)
            for b in range(2):
                q = SORTED - 2 + b
                sp.wait_ge(s["o2_ok"], q + 1)
                sp.dma_start(sorted_o[q * 128:(q + 1) * 128, :], o_s[b]).then_inc(s[f"o_out{b}"], 16)
            for t in range(TILES):
                sp.wait_ge(s["final_ok"], t + 1)
                sp.dma_start(out[t], res[:, t, :]).then_inc(s["out_done"], 16)
            sp.wait_ge(s["out_done"], 16 * TILES)

        @block.gpsimd
        def _(pool):
            pool.dma_start(ids, tokens[:, :]).then_inc(s["ids_in"], 16)
            pool.wait_ge(s["ids_in"], 16)
            for t in range(TILES):
                pool.indirect_dma_start(out=res[:, t, :], out_offset=None, in_=table[:, :],
                                        in_offset=bass.IndirectOffsetOnAxis(ap=ids[:, t:t + 1], axis=0)
                                        ).then_inc(s["rows_in"], 16)

            def emit(step, i, par):
                n = i + 1
                if step == "P.v":
                    pool.wait_ge(s["v_ok"], n)
                    if not (isinstance(i, int) and i == 0):
                        pool.wait_ge(s["vbd_ok"], i)
                        pool.wait_ge(s["rtv_ok"], i)
                        pool.wait_ge(s["ubd2_ok"], 5 * i - 3)
                    nc.gpsimd.tensor_tensor(v2nd, v, v, ALU.subtract).then_inc(s["vd_ok"], 1)
                elif step == "P.vg":
                    pool.wait_ge(s["vd_ok"], n)
                    if not (isinstance(i, int) and i == 0):
                        pool.wait_ge(s["ubd2_ok"], 5 * i - 2)
                    pool.wait_ge(s["vg_ok"], n)
                    nc.gpsimd.tensor_tensor(v2nd, v2nd, vgate, ALU.mult).then_inc(s["vs_ok"], 1)
                    pool.wait_ge(s["vs_ok"], n)
                    nc.gpsimd.tensor_tensor(v2nd, v2nd, v, ALU.add).then_inc(s["v2_ok"], 1)
                elif step in ("Q.start", "Q.T0", "Q.T1", "Q.T2", "Q.T3"):
                    lvl = UPDATES.index(step)
                    last_slab = isinstance(i, int) and i == SLABS - 1
                    if lvl == 0:
                        pool.wait_ge(s["v2_ok"], n)
                    elif lvl == 2 and not last_slab:
                        pool.wait_ge(s["vd_ok"], n + 1)
                    elif lvl == 3 and not last_slab:
                        pool.wait_ge(s["v2_ok"], n + 1)
                    if lvl:
                        pool.wait_ge(s["u_ok"], 4 * i + lvl)
                    else:
                        pool.wait_ge(s["u0_ok"], n)
                    low = slice(64, 128)
                    nc.gpsimd.tensor_tensor(u_bd[low, :, 64:128].rearrange("p u (q t) -> p u q t", q=2),
                                            (u_c if lvl else u_0[par])[low].unsqueeze(2).broadcast_to([64, UN, 2, L]),
                                            cst["blocks"][low, 64:128].rearrange("p (q t) -> p q t", q=2).unsqueeze(1)
                                            .broadcast_to([64, UN, 2, L]), ALU.mult).then_inc(s["ubd2_ok"], 1)

            pool.wait_ge(s["zeroed"], 1)
            pool.wait_ge(s["consts_in"], 16 * (len(CONSTS) + 2))
            pipeline(pool, emit)
            pool.wait_ge(s["ubd2_ok"], 5 * SLABS)
            pool.wait_ge(s["cleared"], 16)
            pool.wait_ge(s["place_u"], 1)
            pool.wait_ge(s["xn2_ok"], TILES)
            for t in range(TILES):
                pool.indirect_dma_start(out=sorted_x[:, :], out_offset=bass.IndirectOffsetOnAxis(ap=place[:, t:t + 1], axis=0),
                                        in_=xn2[:, t, :], in_offset=None).then_inc(s["scattered"], 16)
            for b in range(2):
                pool.wait_ge(s[f"o_out{b}"], 16 * (SORTED // 2))
            for t in range(TILES):
                pool.indirect_dma_start(out=back[:, t, :], out_offset=None, in_=sorted_o[:, :],
                                        in_offset=bass.IndirectOffsetOnAxis(ap=place[:, t:t + 1], axis=0)
                                        ).then_inc(s[f"back_in{t // FT}"], 16)

        @block.scalar
        def _(act):
            act.wait_ge(s["mom1_ok"], 1)
            nc.scalar.activation(stdev, moments[:, :, 1], ACT.Sqrt, bias=eps_ln).then_inc(s["sd1_ok"], 1)
            act.wait_ge(s["zeroed"], 1)
            act.wait_ge(s["consts_in"], 16 * (len(CONSTS) + 2))

            def copy2(dst, bank, ready, done, n):
                act.wait_ge(s[ready], n)
                nc.scalar.copy(dst, ps[:, bank, :].rearrange("p (a t) -> p a t", a=2)).then_inc(s[done], 1)

            def sigmoid2(dst, bank, bias, ready, done, n):
                act.wait_ge(s[ready], n)
                for p in range(2):
                    last = nc.scalar.activation(dst[:, p, :], ps[:, bank, p * NT:(p + 1) * NT], ACT.Sigmoid, bias=vec[bias][:, p:p + 1])
                last.then_inc(s[done], 1)

            def halves(dst, src, done):
                for h in range(2):
                    q = slice(64 * h, 64 * h + 64)
                    last = nc.scalar.copy(dst[q, :, :, L * h:L * h + L], src[q])
                last.then_inc(s[done], 1)

            def emit(step, i, par):
                n = i + 1
                if step == "F.xT":
                    act.wait_ge(s["xT_ps"], n)
                    nc.scalar.copy(xT[:, :, 0, :], xT[:, :, CH, :]).then_inc(s["xT_carry"], 1)
                    act.wait_ge(s["xT_carry"], n)
                    nc.scalar.copy(xT[:, :, 1:CH + 1, :], ps[:, 0, :].rearrange("p (a c t) -> p a c t", a=2, c=CH)).then_inc(s["xT_ok"], 1)
                elif step == "P.k":
                    copy2(k, 1, "k_ps", "k_ok", n)
                elif step == "P.r":
                    copy2(r, 2, "r_ps", "r_ok", n)
                elif step == "P.v":
                    copy2(v, 3, "v_ps", "v_ok", n)
                    act.wait_ge(s["lv_ps"], n)
                    nc.scalar.copy(low_v[0:32, :], ps[0:32, 0, 0:NT]).then_inc(s["lv_ok"], 1)
                elif step == "P.lw":
                    nc.scalar.preload_act_table_set("sigmoid_and_others")
                    act.wait_ge(s["lw_ps"], n)
                    nc.scalar.activation(low_w[0:64, :], ps[0:64, 1, 0:NT], ACT.Tanh).then_inc(s["lw_ok"], 1)
                elif step == "P.vg":
                    sigmoid2(vgate, 2, "v0", "vg_ps", "vg_ok", n)
                elif step == "P.la":
                    act.wait_ge(s["la_ps"], n)
                    nc.scalar.copy(low_a[0:64, :], ps[0:64, 3, 0:NT]).then_inc(s["la_ok"], 1)
                elif step == "P.w":
                    sigmoid2(sig_w, 0, "w0", "w_ps", "w_ok", n)
                elif step == "P.lg":
                    act.wait_ge(s["lg_ps"], n)
                    nc.scalar.activation(low_g, ps[:, 1, 0:NT], ACT.Sigmoid).then_inc(s["lg_ok"], 1)
                elif step == "P.a":
                    sigmoid2(iclr, 2, "a0", "a_ps", "a_ok", n)
                elif step == "P.g":
                    copy2(gate[par], 3, "g_ps", "g_ok", n)
                elif step == "P.decay":
                    nc.scalar.preload_act_table_set("natural_log_exp_and_others")
                    act.wait_ge(s["scan_ok"], n)
                    logs = tmp2.rearrange("p a (b t) -> p a b t", b=BLK)
                    nc.scalar.activation(prod[par][:, :, :, 1:L + 1], logs, ACT.Exp, scale=DECAY).then_inc(s["prod_ok"], 1)
                    nc.scalar.activation(invp, logs, ACT.Exp, scale=-DECAY).then_inc(s["invp_ok"], 1)
                    act.wait_ge(s["nmax_ok"], n)
                    nc.scalar.activation(inv, inv, ACT.Ln, scale=float(2 ** LIFT)).then_inc(s["lnk_ok"], 1)
                    act.wait_ge(s["lnk_ok"], n)
                    nc.scalar.activation(inv, inv, ACT.Exp, scale=-0.5, bias=lift).then_inc(s["nrm_ok"], 1)
                elif step == "P.key":
                    act.wait_ge(s["v2_ok"], n)
                    halves(v_bd, v2nd.rearrange("p a (b t) -> p a b t", b=BLK), "vbd_ok")
                elif step == "P.ar":
                    act.wait_ge(s["ar_ok"], n)
                    halves(a_bd[par], ar[par][:, :, :, 0:L], "abd_ok")
                elif step[:5] == "P.tok":
                    j = int(step[5])
                    act.wait_ge(s["tok_ps"], 6 * i + j + 1)
                    nc.scalar.copy((k_tok, b_tok, v_tok)[j // 2][par][:, 4 * (j % 2):4 * (j % 2) + 4, :],
                                   ps[:, j % 2, :].rearrange("p (u t) -> p u t", u=4)).then_inc(s["tok_ok"], 1)
                elif step in UPDATES:
                    lvl = UPDATES.index(step)
                    if lvl:
                        act.wait_ge(s["u_ok"], 4 * i + lvl)
                    else:
                        act.wait_ge(s["u0_ok"], n)
                    for q in (0, 1):
                        rows = slice(32 * q, 32 * q + 32)
                        last = nc.scalar.copy(u_bd[rows, :, L * q:L * q + L], (u_c if lvl else u_0[par])[rows])
                    last.then_inc(s["ubd_ok"], 1)
                elif step[:3] == "Q.W":
                    act.wait_ge(s["w_ps_c"], 2 * i + int(step[3]) + 1)
                    nc.scalar.copy(w_s, ps[:, 4, 0:256].rearrange("p (u t) -> p u t", u=4)).then_inc(s["w_ok_c"], 1)
                elif step[:3] == "Q.A":
                    act.wait_ge(s["sa_ok"], 2 * i + int(step[3]) + 1)
                    for h in range(2):
                        last = nc.scalar.activation(sa_bd[:, :, HS * h:HS * h + HS], ps[:, 5, 0:256].rearrange("p (u t) -> p u t", u=4),
                                                    ACT.Copy, scale=cst["half"][:, h:h + 1])
                    last.then_inc(s["sabd_ok"], 1)
                elif step[:3] == "Q.S":
                    c = int(step[3])
                    act.wait_ge(s["y_ps"], 2 * i + c + 1)
                    act.wait_ge(s["s_ok"], 2 * i + c + 1)
                    for h in range(2):
                        q = slice(64 * h, 64 * h + 64)
                        last = nc.scalar.copy(state_bd[q, :, HS * h:HS * h + HS], state[q])
                    last.then_inc(s["sbd_ok"], 1)
                elif step == "Q.mean":
                    nc.scalar.copy(yT.rearrange("p a (c x) -> p c a x", c=CH),
                                   ps[:, 7, :].rearrange("p (c a x) -> p c a x", c=CH, a=2)).then_inc(s["yT_ok"], 1)
                elif step == "P.masks":
                    act.wait_ge(s["vcmp_ok"], n)
                    for e in range(2):
                        q = slice(64 * e, 64 * e + 64)
                        last = nc.scalar.copy(v_e[par][q, :, HS * e:HS * e + HS], v_cmp[par][q])
                    last.then_inc(s["ve_ok"], 1)
                elif step == "Q.var":
                    act.wait_ge(s["var_ps"], n)
                    nc.scalar.activation(yinv, ps[:, 5, :].rearrange("p (a t) -> p a t", a=2), ACT.Ln, bias=eps_gn).then_inc(s["lny_ok"], 1)
                    act.wait_ge(s["lny_ok"], n)
                    nc.scalar.activation(yinv, yinv, ACT.Exp, scale=-0.5).then_inc(s["ysd_ok"], 1)

            pipeline(act, emit)
            act.wait_ge(s["mom2_ok"], 1)
            nc.scalar.activation(stdev, moments[:, :, 1], ACT.Sqrt, bias=eps_ln).then_inc(s["sd2_ok"], 1)
            act.wait_ge(s["wgsum_ok"], 1)
            nc.scalar.activation(wgs[0:E, 1:2], wgs[0:E, 0:1], ACT.Sqrt).then_inc(s["wgsd_ok"], 1)
            for t in range(0, TILES, FT):
                act.wait_ge(s["xT2_ps"], t // FT + 1)
                nc.scalar.copy(xT2[:, :, t * 128:(t + FT) * 128], ps[:, 0:2, :]).then_inc(s["xT2_ok"], 1)
            for t in range(TILES // FT):
                act.wait_ge(s["red_ps"], t + 1)
                nc.scalar.copy(red[0:G, t * FN:(t + 1) * FN], ps[0:G, 2 + t % 2, :]).then_inc(s["red_ok"], 1)
            act.wait_ge(s["dif_ok"], 1)
            nc.scalar.activation(ex, ex, ACT.Exp).then_inc(s["exp_ok"], 1)

            def copy_x(q, b):
                act.wait_ge(s["xsT_ps"], q + 1)
                if not isinstance(q, int) or q >= 2:
                    act.wait_ge(s["h_ps"], q - 1 if isinstance(q, int) else q + 0 - 1)
                nc.scalar.copy(x_sT[b], ps[:, b, 0:256].rearrange("p (a t) -> p a t", a=2)).then_inc(s["xsT_ok"], 1)

            def gelu_h(q, b):
                act.wait_ge(s["pre_ok"], q + 1)
                nc.scalar.activation(h_act[b], h_pre[b], ACT.Gelu).then_inc(s["act_ok"], 1)

            def copy_h(q, b):
                act.wait_ge(s["hT_ps"], q + 1)
                nc.scalar.copy(hT[b], ps[:, 4 + b, :].rearrange("p (a t) -> p a t", a=HC)).then_inc(s["hT_ok"], 1)

            copy_x(0, 0)
            gelu_h(0, 0)
            copy_x(1, 1)
            copy_h(0, 0)
            gelu_h(1, 1)
            with act.Fori(0, SORTED // 2 - 1) as j:
                for b in range(2):
                    q = 2 * j + b + 1
                    copy_x(q + 1, b)
                    copy_h(q, 1 - b)
                    gelu_h(q + 1, b)
            copy_h(SORTED - 1, 1)

        @block.vector
        def _(dve):
            V = nc.vector
            V.memset(zero_row, 0.0).then_inc(s["zero_ok"], 1)
            V.memset(eps_ln, LN_EPS)
            V.memset(lift, 0.5 * LIFT * LN2)
            V.memset(eps_gn, GN_EPS).then_inc(s["slab_ok"], 1)
            V.memset(scan_keep, 1.0)
            V.memset(state, 0.0)
            V.memset(state_bd, 0.0)
            V.memset(xT, 0.0)
            for par in range(2):
                V.memset(prod[par], 1.0)
            for buf in (a_bd[0], a_bd[1], v_e[0], v_e[1], sa_e, b_bd, k_bd, v_bd, u_bd):
                last = V.memset(buf, 0.0)
            last.then_inc(s["zeroed"], 1)
            dve.wait_ge(s["zeroed"], 1)
            V.memset(scan_keep.rearrange("p (b t) -> p b t", t=L)[:, :, 0:1], 0.0).then_inc(s["zeroed"], 1)
            dve.wait_ge(s["zeroed"], 2)
            dve.wait_ge(s["consts_in"], 16 * (len(CONSTS) + 2))
            dve.wait_ge(s["rows_in"], 16 * TILES)
            for t in range(TILES):
                V.tensor_tensor(res[:, t, :], res[:, t, :], bias_rows, ALU.add).then_inc(s["biased"], 1)
            for t in range(TILES):
                dve.wait_ge(s["biased"], t + 1)
                V.bn_stats(stats[:, t, :], res[:, t, :]).then_inc(s["stats1_ok"], 1)
            for t in range(TILES):
                dve.wait_ge(s["stats1_ok"], t + 1)
                last = V.bn_aggr(moments[:, t, :], stats[:, t, :])
            last.then_inc(s["mom1_ok"], 1)
            dve.wait_ge(s["sd1_ok"], 1)
            V.reciprocal(rstd, stdev).then_inc(s["rstd1_ok"], 1)
            dve.wait_ge(s["rstd1_ok"], 1)

            def per_unit(mask):
                return mask.unsqueeze(1).broadcast_to([128, UN, L])

            def blocks(x):
                return x.rearrange("p a (b t) -> p a b t", b=BLK)

            def two(bank):
                return ps[:, bank, :].rearrange("p (a t) -> p a t", a=2)

            def mixed(i, j, name):
                if j >= 3:
                    dve.wait_ge(s[("k_ps", "r_ps", "lv_ps")[j - 3]], i + 1)
                for p in range(2):
                    last = V.scalar_tensor_tensor(out=mix[j % 3][:, p, :], in0=xx[:, p].rearrange("p b t -> p (b t)"),
                                                  scalar=vec[name][:, p:p + 1],
                                                  in1=xT[:, p, 1:CH + 1, :].rearrange("p c t -> p (c t)"),
                                                  op0=ALU.mult, op1=ALU.add)
                last.then_inc(s["mix_ok"], 1)

            def spread(dst, x, done):
                for h in range(2):
                    q = slice(64 * h, 64 * h + 64)
                    last = V.tensor_tensor(dst[q, :, :, L * h:L * h + L], blocks(x[q]), invp[q], ALU.mult)
                last.then_inc(s[done], 1)

            def emit(step, i, par):
                n = i + 1
                if step == "F.xT":
                    for c in range(CH):
                        t = i * CH + c
                        last = V.tensor_scalar(xn[:, c, :], res[:, t, :], moments[:, t, 0:1], rstd[:, bass.ds(t, 1)],
                                               ALU.subtract, ALU.mult)
                    last.then_inc(s["xn_ok"], 1)
                elif step == "F.xx":
                    dve.wait_ge(s["xT_ok"], n)
                    xb = xT.rearrange("p a c (b t) -> p a (c b) t", t=L)
                    V.tensor_tensor(xx[:, :, :, 1:L], xb[:, :, B:B + BLK, 0:L - 1], xb[:, :, B:B + BLK, 1:L], ALU.subtract)
                    V.tensor_tensor(xx[:, :, :, 0:1], xb[:, :, 0:BLK, L - 1:L], xb[:, :, B:B + BLK, 0:1],
                                    ALU.subtract).then_inc(s["xx_ok"], 1)
                    dve.wait_ge(s["xx_ok"], n)
                    mixed(i, 0, "x_k")
                    mixed(i, 1, "x_r")
                elif step == "P.k":
                    mixed(i, 2, "x_v")
                elif step == "P.r":
                    mixed(i, 3, "x_w")
                elif step == "P.v":
                    mixed(i, 4, "x_a")
                elif step == "P.lw":
                    mixed(i, 5, "x_g")
                elif step == "P.vg":
                    dve.wait_ge(s["k_ok"], n)
                    for p in range(2):
                        last = V.tensor_scalar(kk[:, p, :], k[:, p, :], vec["k_k"][:, p:p + 1], None, ALU.mult)
                    last.then_inc(s["kk_ok"], 1)
                elif step == "P.la":
                    dve.wait_ge(s["kk_ok"], n)
                    V.tensor_tensor(tmp, kk, kk, ALU.mult).then_inc(s["sq_ok"], 1)
                elif step == "P.g":
                    dve.wait_ge(s["w_ok"], n)
                    V.tensor_tensor_scan(tmp2.rearrange("p a t -> p (a t)"), scan_keep, sig_w.rearrange("p a t -> p (a t)"), 0.0,
                                         ALU.mult, ALU.add).then_inc(s["scan_ok"], 1)
                elif step == "P.norm":
                    dve.wait_ge(s["nrm_ps"], n)
                    V.tensor_scalar(inv, two(0), 1e-24, None, ALU.max).then_inc(s["nmax_ok"], 1)
                elif step == "P.decay":
                    dve.wait_ge(s["a_ok"], n)
                    dve.wait_ge(s["invp_ok"], n)
                    for p in range(2):
                        last = V.tensor_scalar(tmp2[:, p, :], iclr[:, p, :], 1.0, vec["k_a"][:, p:p + 1], ALU.subtract, ALU.mult)
                    last.then_inc(s["t1_ok"], 1)
                elif step == "P.key":
                    dve.wait_ge(s["t1_ok"], n)
                    V.scalar_tensor_tensor(out=k, in0=tmp2, scalar=1.0, in1=k, op0=ALU.add, op1=ALU.mult).then_inc(s["k2_ok"], 1)
                    dve.wait_ge(s["k2_ok"], n)
                    dve.wait_ge(s["r_ok"], n)
                    for p in range(2):
                        last = V.scalar_tensor_tensor(out=tmp[:, p, :], in0=r[:, p, :], scalar=vec["r_k"][:, p:p + 1],
                                                      in1=k[:, p, :], op0=ALU.mult, op1=ALU.mult)
                    last.then_inc(s["rkr_ok"], 1)
                    dve.wait_ge(s["nrm_ok"], n)
                    V.tensor_tensor(kk, kk, inv, ALU.mult).then_inc(s["kkn_ok"], 1)
                elif step == "P.ar":
                    dve.wait_ge(s["kkn_ok"], n)
                    V.tensor_tensor(ar[par][:, :, :, 0:L], blocks(kk), prod[par][:, :, :, 0:L], ALU.mult)
                    V.tensor_tensor(ar[par][:, :, :, L:2 * L], blocks(r), prod[par][:, :, :, 1:L + 1],
                                    ALU.mult).then_inc(s["ar_ok"], 1)
                    V.scalar_tensor_tensor(out=tmp2, in0=kk, scalar=-1.0, in1=iclr, op0=ALU.mult, op1=ALU.mult).then_inc(s["bn_ok"], 1)
                elif step == "P.kbd":
                    spread(k_bd, k, "kbd_ok")
                elif step == "P.bbd":
                    dve.wait_ge(s["bn_ok"], n)
                    spread(b_bd, tmp2, "bbd_ok")
                elif step == "P.bonus":
                    dve.wait_ge(s["rt_ps"], n)
                    dve.wait_ge(s["v2_ok"], n)
                    V.tensor_tensor(rtv[par], two(1), v2nd, ALU.mult).then_inc(s["rtv_ok"], 1)
                elif step == "P.masks":
                    dve.wait_ge(s["m_ps"], n)
                    m1 = ps[:, 2, :].rearrange("p (u x) -> p u x", x=2 * L)
                    m2 = ps[:, 3, :].rearrange("p (u x) -> p u x", x=2 * L)
                    V.tensor_tensor(u_0[par], m1[:, :, 0:L], per_unit(cst["pairs"]), ALU.mult).then_inc(s["pairs_ok"], 1)
                    strict = cst["strict_bd"].rearrange("p (q t) -> p q t", q=4).unsqueeze(1).broadcast_to([128, UN, 4, L])
                    for dst, src in ((n_bd[par], m1), (mak_bd[par], m2)):
                        V.tensor_tensor(dst.rearrange("p u (q t) -> p u q t", q=4),
                                        src[:, :, 0:L].unsqueeze(2).broadcast_to([128, UN, 4, L]), strict, ALU.mult)
                    upto = cst["upto"].rearrange("p (e t) -> p e t", e=2).unsqueeze(1).broadcast_to([128, UN, 2, L])
                    for dst, src in ((mrb[par], m1), (mrk[par], m2)):
                        last = V.tensor_tensor(dst.rearrange("p u (e t) -> p u e t", e=2),
                                               src[:, :, L:2 * L].unsqueeze(2).broadcast_to([128, UN, 2, L]), upto, ALU.mult)
                    last.then_inc(s["masks_ok"], 1)
                    dve.wait_ge(s["pairs_ok"], n)
                    V.tensor_tensor(u_0[par], u_0[par], per_unit(cst["eye"]), ALU.add).then_inc(s["u0_ok"], 1)
                elif step == "P.tok5":
                    dve.wait_ge(s["tok_ok"], 6 * n)
                    V.tensor_tensor(v_cmp[par], v_tok[par][:, :, 0:HS], v_tok[par][:, :, HS:2 * HS], ALU.add).then_inc(s["vcmp_ok"], 1)
                elif step == "Q.start":
                    dve.wait_ge(s["u0_ok"], n)
                    V.transpose(t_c.rearrange("p u t -> p (u t)"), u_0[par].rearrange("p u t -> p (u t)")).then_inc(s["t_ok"], 1)
                elif step[:3] == "Q.X":
                    lvl = int(step[3])
                    dve.wait_ge(s["x_ps"], 4 * i + lvl + 1)
                    V.tensor_tensor(x_c, ps[:, 4, 0:UN * L].rearrange("p (u t) -> p u t", u=UN),
                                    per_unit(cst["low"][:, L * lvl:L * lvl + L]), ALU.mult).then_inc(s["x_ok"], 1)
                elif step[:3] == "Q.T":
                    lvl = int(step[3])
                    dve.wait_ge(s["t_ps"], 4 * i + lvl + 1)
                    V.tensor_tensor(t_c, ps[:, 5, 0:UN * L].rearrange("p (u t) -> p u t", u=UN), t_c, ALU.add).then_inc(s["t_ok"], 1)
                    dve.wait_ge(s["t_ok"], 5 * i + lvl + 2)
                    dve.wait_ge(s["ubd_ok"], 5 * i + lvl + 1)
                    dve.wait_ge(s["ubd2_ok"], 5 * i + lvl + 1)
                    V.transpose(u_c.rearrange("p u t -> p (u t)"), t_c.rearrange("p u t -> p (u t)")).then_inc(s["u_ok"], 1)
                elif step[:3] == "Q.A":
                    dve.wait_ge(s["sa_ps"], 2 * i + int(step[3]) + 1)
                    for e in range(2):
                        q = slice(64 * e, 64 * e + 64)
                        last = V.tensor_copy(sa_e[q, :, HS * e:HS * e + HS], ps[q, 5, 0:256].rearrange("p (u t) -> p u t", u=4))
                    last.then_inc(s["sa_ok"], 1)
                elif step[:3] == "Q.S":
                    c = int(step[3])
                    dve.wait_ge(s["s_ps"], 2 * i + c + 1)
                    V.tensor_tensor(state.rearrange("p u t -> p (u t)"), ps[:, 6, :], state.rearrange("p u t -> p (u t)"),
                                    ALU.add).then_inc(s["s_sum"], 1)
                    dve.wait_ge(s["s_sum"], 2 * i + c + 1)
                    whole = prod[par].rearrange("p a (c b) t -> p a c b t", c=CH)[:, :, c, :, L:L + 1].broadcast_to([128, 2, B, HS])
                    last = V.tensor_tensor(state.rearrange("p (a b) t -> p a b t", a=2), state.rearrange("p (a b) t -> p a b t", a=2),
                                           whole, ALU.mult)
                    last.then_inc(s["s_ok"], 1)
                elif step == "Q.mean":
                    dve.wait_ge(s["mean_ps"], n)
                    V.tensor_tensor(yd, yT, two(6), ALU.subtract).then_inc(s["yd_ok"], 1)
                    dve.wait_ge(s["yd_ok"], n)
                    V.tensor_tensor(ysq, yd, yd, ALU.mult).then_inc(s["ysq_ok"], 1)
                elif step == "Q.out":
                    dve.wait_ge(s["ysd_ok"], n)
                    V.tensor_tensor(yd, yd, yinv, ALU.mult).then_inc(s["yz1"], 1)
                    dve.wait_ge(s["yz1"], n)
                    for p in range(2):
                        last = V.tensor_scalar(yd[:, p, :], yd[:, p, :], vec["ln_w"][:, p:p + 1], vec["ln_b"][:, p:p + 1],
                                               ALU.mult, ALU.add)
                    last.then_inc(s["yz2"], 1)
                    dve.wait_ge(s["yz2"], n)
                    V.tensor_tensor(yd, yd, rtv[par], ALU.add).then_inc(s["yz3"], 1)
                    dve.wait_ge(s["yz3"], n)
                    V.tensor_tensor(ysq, yd, gate[par], ALU.mult).then_inc(s["z_ok"], 1)
                elif step == "Q.add":
                    dve.wait_ge(s["o_ps"], n)
                    rows = res[:, bass.ds(i * CH, CH), :].rearrange("p t c -> p (t c)")
                    V.tensor_tensor(rows, ps[:, 4, :], rows, ALU.add).then_inc(s["slab_ok"], 1)

            pipeline(dve, emit)
            dve.wait_ge(s["slab_ok"], SLABS + 1)
            V.memset(ones_sb, 1.0)
            V.memset(keep_e, 1.0).then_inc(s["ffn_set"], 1)
            dve.wait_ge(s["ffn_set"], 1)
            V.memset(keep_e.rearrange("p (e t) -> p e t", t=TILES)[:, :, 0:1], 0.0).then_inc(s["ffn_set"], 1)
            for t in range(TILES):
                V.bn_stats(stats[:, t, :], res[:, t, :]).then_inc(s["stats2_ok"], 1)
            for t in range(TILES):
                dve.wait_ge(s["stats2_ok"], t + 1)
                last = V.bn_aggr(moments[:, t, :], stats[:, t, :])
            last.then_inc(s["mom2_ok"], 1)
            dve.wait_ge(s["ffn_in"], 48)
            V.tensor_tensor(wgsq[0:E, :], wg_sb[0:E, :], wg_sb[0:E, :], ALU.mult).then_inc(s["route"], 1)
            dve.wait_ge(s["route"], after("wgsq"))
            V.reduce_sum(wgs[0:E, 0:1], wgsq[0:E, :], axis=AX.X).then_inc(s["wgsum_ok"], 1)
            dve.wait_ge(s["sd2_ok"], 1)
            V.reciprocal(rstd, stdev).then_inc(s["rstd2_ok"], 1)
            dve.wait_ge(s["rstd2_ok"], 1)
            for t in range(TILES):
                V.tensor_scalar(xn2[:, t, :], res[:, t, :], moments[:, t, 0:1], rstd[:, t:t + 1],
                                ALU.subtract, ALU.mult).then_inc(s["xn2_ok"], 1)
            dve.wait_ge(s["wgsd_ok"], 1)
            V.tensor_scalar(wgs[0:E, 1:2], wgs[0:E, 1:2], 1e-4, None, ALU.max).then_inc(s["route"], 1)
            dve.wait_ge(s["route"], after("wgmax"))
            V.reciprocal(wgs[0:E, 0:1], wgs[0:E, 1:2]).then_inc(s["route"], 1)
            dve.wait_ge(s["route"], after("wginv"))
            V.tensor_scalar(wgn[0:E, :], wg_sb[0:E, :], wgs[0:E, 0:1], None, ALU.mult).then_inc(s["wgn_ok"], 1)
            dve.wait_ge(s["wgT_ps"], 1)
            V.tensor_copy(wgT[0:G, :], ps[0:G, 4, 0:E]).then_inc(s["wgT_ok"], 1)
            dve.wait_ge(s["lg2_ps"], 1)
            V.tensor_copy(logits, ps[:, 5, 0:TILES * E].rearrange("p (t e) -> p t e", e=E)).then_inc(s["route"], 1)
            dve.wait_ge(s["route"], after("lg2"))
            for t in range(TILES):
                V.max(top[:, t, :], logits[:, t, :]).then_inc(s["topv_ok"], 1)
            for t in range(TILES):
                dve.wait_ge(s["topv_ok"], t + 1)
                last = V.max_index(topi[:, t, :], top[:, t, :], logits[:, t, :])
            last.then_inc(s["route"], 1)
            V.tensor_tensor(ex, logits, top[:, :, 0:1].broadcast_to([128, TILES, E]), ALU.subtract).then_inc(s["dif_ok"], 1)
            dve.wait_ge(s["route"], after("topi"))
            V.tensor_copy(topf[:, :, 0:1], topi[:, :, 0:1]).then_inc(s["route"], 1)
            dve.wait_ge(s["route"], after("topf"))
            V.tensor_tensor(onehot, cst["iota"].unsqueeze(1).broadcast_to([128, TILES, E]),
                            topf[:, :, 0:1].broadcast_to([128, TILES, E]), ALU.is_equal).then_inc(s["onehot_ok"], 1)
            dve.wait_ge(s["ffn_set"], 2)
            dve.wait_ge(s["tot_ps"], 1)
            V.tensor_copy(count, ps[:, 4, 128:256].rearrange("p (t e) -> p e t", e=E)).then_inc(s["route"], 1)
            dve.wait_ge(s["route"], after("count"))
            V.tensor_tensor_scan(upto_t.rearrange("p e t -> p (e t)"), keep_e, count.rearrange("p e t -> p (e t)"), 0.0,
                                 ALU.mult, ALU.add).then_inc(s["route"], 1)
            dve.wait_ge(s["route"], after("scan_t"))
            V.tensor_tensor(more, cst["tile_rows"].unsqueeze(1).broadcast_to([128, E, TILES]),
                            upto_t[:, :, TILES - 1:TILES].broadcast_to([128, E, TILES]), ALU.is_lt).then_inc(s["route"], 1)
            V.tensor_tensor(start_t, upto_t, count, ALU.subtract).then_inc(s["route"], 1)
            dve.wait_ge(s["route"], after("more"))
            V.reduce_sum(tiles_e, more, axis=AX.X).then_inc(s["route"], 1)
            dve.wait_ge(s["route"], after("tiles"))
            V.tensor_tensor_scan(end_e, ones_sb[:, 0:E], tiles_e, 0.0, ALU.mult, ALU.add).then_inc(s["route"], 1)
            dve.wait_ge(s["route"], after("end"))
            V.tensor_tensor(base_e, end_e, tiles_e, ALU.subtract).then_inc(s["route"], 1)
            V.tensor_tensor(passed, end_e.unsqueeze(1).broadcast_to([128, SORTED, E]),
                            cst["tile_no"].unsqueeze(2).broadcast_to([128, SORTED, E]), ALU.is_le).then_inc(s["route"], 1)
            dve.wait_ge(s["route"], after("base"))
            V.scalar_tensor_tensor(out=start_t, in0=base_e.unsqueeze(2).broadcast_to([128, E, TILES]), scalar=128.0, in1=start_t,
                                   op0=ALU.mult, op1=ALU.add).then_inc(s["route"], 1)
            dve.wait_ge(s["route"], after("start2"))
            V.tensor_tensor(place_e, ps[:, 4, 0:128].rearrange("p (t e) -> p t e", e=E), start_t.rearrange("p e t -> p t e"),
                            ALU.add).then_inc(s["route"], 1)
            dve.wait_ge(s["route"], after("place"))
            V.tensor_tensor(place_e, place_e, onehot, ALU.mult).then_inc(s["route"], 1)
            dve.wait_ge(s["route"], after("place2"))
            V.reduce_sum(place_f, place_e, axis=AX.X).then_inc(s["route"], 1)
            dve.wait_ge(s["route"], after("place3"))
            V.tensor_copy(place, place_f).then_inc(s["place_u"], 1)
            dve.wait_ge(s["route"], after("passed"))
            V.reduce_sum(owner_f, passed, axis=AX.X).then_inc(s["route"], 1)
            dve.wait_ge(s["route"], after("owner"))
            V.tensor_scalar(owner_f, owner_f, float(E - 1), None, ALU.min).then_inc(s["route"], 1)
            dve.wait_ge(s["route"], after("owner2"))
            V.tensor_copy(owner, owner_f).then_inc(s["owner_u"], 1)
            dve.wait_ge(s["exp_ok"], 1)
            V.reduce_sum(esum, ex, axis=AX.X).then_inc(s["route"], 1)
            dve.wait_ge(s["route"], after("esum"))
            V.reciprocal(score, esum).then_inc(s["score_ok"], 1)
            dve.wait_ge(s["score_ok"], 1)
            dve.wait_ge(s["onehot_ok"], 1)
            V.tensor_tensor(picked, onehot, score.unsqueeze(2).broadcast_to([128, TILES, E]), ALU.mult).then_inc(s["picked_ok"], 1)
            dve.wait_ge(s["picked_ok"], 1)
            for t in range(0, TILES, FT):
                dve.wait_ge(s["pT_ps"], t // FT + 1)
                V.tensor_copy(pickedT[0:E, t * 128:(t + FT) * 128], ps[0:E, 6, :]).then_inc(s["pT_ok"], 1)
            for t in range(TILES):
                dve.wait_ge(s["b2_ps"], t + 1)
                V.tensor_tensor(res[:, t, :], ps[:, 4 + t % 2, 0:C], res[:, t, :], ALU.add).then_inc(s["b2_ok"], 1)

            def pre(q, b):
                e = dve.value_load(owner[0:1, bass.ds(q, 1)], min_val=0, max_val=E - 1)
                dve.wait_ge(s["h_ps"], q + 1)
                V.tensor_tensor(h_pre[b], ps[:, 2 + b, :], b1_sb[:, bass.ds(e * HID, HID)], ALU.add).then_inc(s["pre_ok"], 1)

            def result(q, b):
                dve.wait_ge(s["o2_ps"], q + 1)
                if not isinstance(q, int) or q >= 2:
                    dve.wait_ge(s[f"o_out{b}"], 16 * (q // 2) if isinstance(q, int) else (q - b) * 8)
                V.tensor_copy(o_s[b], ps[:, 6 + b, 0:C]).then_inc(s["o2_ok"], 1)

            dve.wait_ge(s["wexp_in"], 16 * (2 * E + 1))
            dve.wait_ge(s["owner_u"], 1)
            pre(0, 0)
            pre(1, 1)
            result(0, 0)
            pre(2, 0)
            result(1, 1)
            with dve.Fori(1, SORTED // 2 - 1) as j:
                for b in range(2):
                    q = 2 * j + b
                    pre(q + 1, 1 - b)
                    result(q, b)
            pre(SORTED - 1, 1)
            result(SORTED - 2, 0)
            result(SORTED - 1, 1)
            for t in range(TILES):
                dve.wait_ge(s[f"back_in{t // FT}"], 16 * FT)
                V.scalar_tensor_tensor(out=res[:, t, :], in0=back[:, t, :], scalar=score[:, t:t + 1], in1=res[:, t, :],
                                       op0=ALU.mult, op1=ALU.add).then_inc(s["final_ok"], 1)

        @block.tensor
        def _(pe):
            mm = nc.tensor.matmul
            pe.wait_ge(s["consts_in"], 16 * (len(CONSTS) + 2))
            pe.wait_ge(s["weights_in"], 16 * 12)
            pe.wait_ge(s["zeroed"], 1)

            def full(w, src, bank):
                for m in range(2):
                    for kt in range(2):
                        last = mm(ps[:, bank, m * NT:(m + 1) * NT], w[:, kt, m * 128:(m + 1) * 128], src[:, kt, :],
                                  start=kt == 0, stop=kt == 1)
                return last

            def down(w, src, bank, rows):
                for kt in range(2):
                    last = mm(ps[0:rows, bank, 0:NT], w[:, kt, :], src[:, kt, :], start=kt == 0, stop=kt == 1)
                return last

            def up(w, src, bank, rows):
                for m in range(2):
                    last = mm(ps[:, bank, m * NT:(m + 1) * NT], w[0:rows, m * 128:(m + 1) * 128], src[0:rows, :], start=True, stop=True)
                return last

            def over_heads(w, src, bank):
                for p in range(2):
                    last = mm(ps[:, bank, p * NT:(p + 1) * NT], w, src[:, p, :], start=True, stop=True)
                return last

            def emit(step, i, par):
                n = i + 1
                if step == "F.xT":
                    pe.wait_ge(s["xn_ok"], n)
                    if not (isinstance(i, int) and i == 0):
                        pe.wait_ge(s["tok_ok"], 6 * i)
                    for p in range(2):
                        for c in range(CH):
                            last = nc.tensor.transpose(ps[:, 0, p * NT + c * 128:p * NT + (c + 1) * 128],
                                                       xn[:, c, p * 128:(p + 1) * 128], ident)
                    last.then_inc(s["xT_ps"], 1)
                elif step == "P.k":
                    pe.wait_ge(s["mix_ok"], 6 * i + 1)
                    full(w_sb["k"], mix[0], 1).then_inc(s["k_ps"], 1)
                elif step == "P.r":
                    pe.wait_ge(s["mix_ok"], 6 * i + 2)
                    if not (isinstance(i, int) and i == 0):
                        pe.wait_ge(s["masks_ok"], i)
                    full(w_sb["r"], mix[1], 2).then_inc(s["r_ps"], 1)
                elif step == "P.v":
                    pe.wait_ge(s["mix_ok"], 6 * i + 3)
                    full(w_sb["v"], mix[2], 3).then_inc(s["v_ps"], 1)
                    pe.wait_ge(s["xT_ok"], n)
                    down(v1_sb, mix[2], 0, 32).then_inc(s["lv_ps"], 1)
                elif step == "P.lw":
                    pe.wait_ge(s["mix_ok"], 6 * i + 4)
                    pe.wait_ge(s["k_ok"], n)
                    down(w1_sb, mix[0], 1, 64).then_inc(s["lw_ps"], 1)
                elif step == "P.vg":
                    pe.wait_ge(s["lv_ok"], n)
                    pe.wait_ge(s["r_ok"], n)
                    up(v2_sb, low_v, 2, 32).then_inc(s["vg_ps"], 1)
                elif step == "P.la":
                    pe.wait_ge(s["mix_ok"], 6 * i + 5)
                    pe.wait_ge(s["v_ok"], n)
                    down(a1_sb, mix[1], 3, 64).then_inc(s["la_ps"], 1)
                elif step == "P.w":
                    pe.wait_ge(s["lw_ok"], n)
                    up(w2_sb, low_w, 0, 64).then_inc(s["w_ps"], 1)
                elif step == "P.lg":
                    pe.wait_ge(s["mix_ok"], 6 * i + 6)
                    down(g1_sb, mix[2], 1, 128).then_inc(s["lg_ps"], 1)
                elif step == "P.a":
                    pe.wait_ge(s["vg_ok"], n)
                    pe.wait_ge(s["la_ok"], n)
                    up(a2_sb, low_a, 2, 64).then_inc(s["a_ps"], 1)
                elif step == "P.g":
                    pe.wait_ge(s["lg_ok"], n)
                    up(g2_sb, low_g, 3, 128).then_inc(s["g_ps"], 1)
                elif step == "P.norm":
                    pe.wait_ge(s["sq_ok"], n)
                    pe.wait_ge(s["w_ok"], n)
                    over_heads(cst["ones_bd"], tmp, 0).then_inc(s["nrm_ps"], 1)
                elif step == "P.ar":
                    pe.wait_ge(s["rkr_ok"], n)
                    over_heads(cst["ones_bd"], tmp, 1).then_inc(s["rt_ps"], 1)
                elif step == "P.M":
                    pe.wait_ge(s["bbd_ok"], n)
                    pe.wait_ge(s["a_ok"], n)
                    pe.wait_ge(s["g_ok"], n)
                    for src, bank in ((b_bd, 2), (k_bd, 3)):
                        for p in range(2):
                            for u in range(BLK):
                                q, col = 64 * (u % 2), ((p * BLK + u) // 2) * 2 * L
                                last = mm(ps[q:q + 64, bank, col:col + 2 * L], src[:, p, u, :], ar[par][:, p, u, :],
                                          start=True, stop=True)
                    last.then_inc(s["m_ps"], 1)
                elif step[:5] == "P.tok":
                    j = int(step[5])
                    if j == 0:
                        pe.wait_ge(s["kbd_ok"], n)
                        pe.wait_ge(s["nmax_ok"], n)
                    elif j == 1:
                        pe.wait_ge(s["rtv_ok"], n)
                    else:
                        pe.wait_ge(s["tok_ok"], 6 * i + j - 1)
                        if j == 2:
                            pe.wait_ge(s["bbd_ok"], n)
                        if j == 4:
                            pe.wait_ge(s["vbd_ok"], n)
                    for w in range(4):
                        last = nc.tensor.transpose(ps[:, j % 2, w * 128:(w + 1) * 128],
                                                   (k_bd, b_bd, v_bd)[j // 2][:, j % 2, 2 * w:2 * w + 2, :].rearrange("p a b -> p (a b)"),
                                                   ident)
                    last.then_inc(s["tok_ps"], 1)
                elif step[:3] == "Q.X":
                    lvl = int(step[3])
                    if lvl == 0:
                        pe.wait_ge(s["slab_ok"], n)
                        pe.wait_ge(s["masks_ok"], n)
                    pe.wait_ge(s["t_ok"], 5 * i + lvl + 1)
                    for u in range(UN):
                        last = mm(ps[:, 4, u * L:(u + 1) * L], n_bd[par][:, u, :], t_c[:, u, :], start=True, stop=True)
                    last.then_inc(s["x_ps"], 1)
                elif step[:3] == "Q.T":
                    lvl = int(step[3])
                    pe.wait_ge(s["x_ok"], 4 * i + lvl + 1)
                    pe.wait_ge(s["ubd_ok"], 5 * i + lvl + 1)
                    pe.wait_ge(s["ubd2_ok"], 5 * i + lvl + 1)
                    for u in range(UN):
                        last = mm(ps[:, 5, u * L:(u + 1) * L], u_bd[:, u, :], x_c[:, u, :], start=True, stop=True)
                    last.then_inc(s["t_ps"], 1)
                elif step[:3] == "Q.W":
                    c = int(step[3])
                    if c:
                        pe.wait_ge(s["s_ok"], 2 * i + c)
                    else:
                        pe.wait_ge(s["vcmp_ok"], n)
                        pe.wait_ge(s["ve_ok"], n)
                        pe.wait_ge(s["abd_ok"], n)
                    for k in range(4):
                        mm(ps[:, 4, k * HS:(k + 1) * HS], mak_bd[par][:, unit(k // 2, c, 2 * (k % 2)), :],
                           v_cmp[par][:, unit(k // 2, c, 2 * (k % 2)), :], start=k == 0, stop=False, skip_group_check=True)
                    for k in range(4):
                        for e in range(2):
                            last = mm(ps[64 * e:64 * e + 64, 4, k * HS:(k + 1) * HS], a_bd[par][:, k // 2, c * B + 2 * (k % 2) + e, :],
                                      state[:, 2 * k + e, :], start=False, stop=k == 3, skip_group_check=True)
                    last.then_inc(s["w_ps_c"], 1)
                elif step[:3] == "Q.A":
                    c = int(step[3])
                    pe.wait_ge(s["w_ok_c"], 2 * i + c + 1)
                    pe.wait_ge(s["ubd_ok"], 5 * n)
                    pe.wait_ge(s["ubd2_ok"], 5 * n)
                    if c:
                        pe.wait_ge(s["sabd_ok"], 2 * i + c)
                    for k in range(4):
                        last = mm(ps[:, 5, k * HS:(k + 1) * HS], u_bd[:, unit(k // 2, c, 2 * (k % 2)), :], w_s[:, k, :],
                                  start=True, stop=True)
                    last.then_inc(s["sa_ps"], 1)
                elif step[:3] == "Q.S":
                    c = int(step[3])
                    pe.wait_ge(s["sa_ok"], 2 * i + c + 1)
                    for k in range(4):
                        u, x = unit(k // 2, c, 2 * (k % 2)), k * 128
                        mm(ps[:, 6, x:x + 128], k_tok[par][:, u, :], v_e[par][:, u, :], start=True, stop=False)
                        last = mm(ps[:, 6, x:x + 128], b_tok[par][:, u, :], sa_e[:, k, :], start=False, stop=True)
                    last.then_inc(s["s_ps"], 1)
                    pe.wait_ge(s["sabd_ok"], 2 * i + c + 1)
                    if c:
                        pe.wait_ge(s["sbd_ok"], 2 * i + c)
                    for k in range(4):
                        u, x = unit(k // 2, c, 2 * (k % 2)), c * 256 + k * 2 * L
                        mm(ps[:, 7, x:x + 2 * L], v_tok[par][:, u, :], mrk[par][:, u, :], start=True, stop=False, skip_group_check=True)
                        mm(ps[:, 7, x:x + 2 * L], sa_bd[:, k, :], mrb[par][:, u, :], start=False, stop=False, skip_group_check=True)
                        for e in range(2):
                            last = mm(ps[:, 7, x + e * L:x + (e + 1) * L], state_bd[:, 2 * k + e, :],
                                      ar[par][:, k // 2, c * B + 2 * (k % 2) + e, L:2 * L], start=False, stop=e == 1,
                                      skip_group_check=True)
                    last.then_inc(s["y_ps"], 1)
                elif step == "Q.mean":
                    pe.wait_ge(s["yT_ok"], n)
                    pe.wait_ge(s["s_ok"], 2 * n)
                    over_heads(cst["mean_bd"], yT, 6).then_inc(s["mean_ps"], 1)
                elif step == "Q.var":
                    pe.wait_ge(s["ysq_ok"], n)
                    over_heads(cst["mean_bd"], ysq, 5).then_inc(s["var_ps"], 1)
                elif step == "Q.out":
                    pe.wait_ge(s["z_ok"], n)
                    for c in range(CH):
                        for p in range(2):
                            last = mm(ps[:, 4, c * C:(c + 1) * C], ysq[:, p, c * 128:(c + 1) * 128], w_sb["o"][:, p, :],
                                      start=p == 0, stop=p == 1)
                    last.then_inc(s["o_ps"], 1)

            pipeline(pe, emit)
            pe.wait_ge(s["slab_ok"], SLABS + 1)
            for t in range(0, TILES, FT):
                pe.wait_ge(s["xn2_ok"], t + FT)
                if t:
                    pe.wait_ge(s["xT2_ok"], t // FT)
                for p in range(2):
                    for c in range(FT):
                        last = nc.tensor.transpose(ps[:, p, c * 128:(c + 1) * 128], xn2[:, t + c, p * 128:(p + 1) * 128], ident)
                last.then_inc(s["xT2_ps"], 1)
            pe.wait_ge(s["ffn_in"], 48)
            for t in range(TILES // FT):
                pe.wait_ge(s["xT2_ok"], t + 1)
                if t >= 2:
                    pe.wait_ge(s["red_ok"], t - 1)
                for p in range(2):
                    last = mm(ps[0:G, 2 + t % 2, :], wred_sb[:, p, :], xT2[:, p, t * FN:(t + 1) * FN], start=p == 0, stop=p == 1)
                last.then_inc(s["red_ps"], 1)
            pe.wait_ge(s["wgn_ok"], 1)
            nc.tensor.transpose(ps[0:G, 4, 0:E], wgn[0:E, :], ident[0:E, 0:E]).then_inc(s["wgT_ps"], 1)
            pe.wait_ge(s["wgT_ok"], 1)
            pe.wait_ge(s["red_ok"], TILES // FT)
            for t in range(TILES):
                last = mm(ps[:, 5, t * E:(t + 1) * E], red[0:G, t * 128:(t + 1) * 128], wgT[0:G, :], start=True, stop=True)
            last.then_inc(s["lg2_ps"], 1)
            pe.wait_ge(s["onehot_ok"], 1)
            pe.wait_ge(s["wgT_ok"], 1)
            mm(ps[:, 4, 0:128], cst["before"], onehot.rearrange("p t e -> p (t e)"), start=True, stop=True)
            mm(ps[:, 4, 128:256], ones_sb, onehot.rearrange("p t e -> p (t e)"), start=True, stop=True).then_inc(s["tot_ps"], 1)
            pe.wait_ge(s["route"], after("place"))
            pe.wait_ge(s["picked_ok"], 1)
            for t in range(0, TILES, FT):
                if t:
                    pe.wait_ge(s["pT_ok"], t // FT)
                for c in range(FT):
                    last = nc.tensor.transpose(ps[0:E, 6, c * 128:(c + 1) * 128], picked[:, t + c, :], ident)
                last.then_inc(s["pT_ps"], 1)
            for t in range(TILES):
                pe.wait_ge(s["pT_ok"], t // FT + 1)
                if t >= 2:
                    pe.wait_ge(s["b2_ok"], t - 1)
                mm(ps[:, 4 + t % 2, 0:C], pickedT[0:E, t * 128:(t + 1) * 128], b2_sb[0:E, :], start=True, stop=True).then_inc(s["b2_ps"], 1)
            pe.wait_ge(s["b2_ok"], TILES)
            pe.wait_ge(s["wexp_in"], 16 * (2 * E + 1))

            def up_x(q, b):
                pe.wait_ge(s[f"xs_in{b}"], 16 * (q // 2 + 1) if isinstance(q, int) else (q - b) * 8 + 16)
                if not isinstance(q, int) or q >= 2:
                    pe.wait_ge(s["xsT_ok"], q - 1)
                for p in range(2):
                    last = nc.tensor.transpose(ps[:, b, p * 128:(p + 1) * 128], x_s[b][:, p * 128:(p + 1) * 128], ident)
                last.then_inc(s["xsT_ps"], 1)

            def up_h(q, b):
                e = pe.value_load(owner[0:1, bass.ds(q, 1)], min_val=0, max_val=E - 1)
                pe.wait_ge(s["xsT_ok"], q + 1)
                if not isinstance(q, int) or q >= 2:
                    pe.wait_ge(s["pre_ok"], q - 1)
                for p in range(2):
                    last = mm(ps[:, 2 + b, :], x_sT[b][:, p, :], W1_sb[:, bass.ds(e * (2 * HID) + p * HID, HID)], start=p == 0, stop=p == 1)
                last.then_inc(s["h_ps"], 1)

            def turn_h(q, b):
                pe.wait_ge(s["act_ok"], q + 1)
                if not isinstance(q, int) or q >= 2:
                    pe.wait_ge(s["hT_ok"], q - 1)
                for m in range(HC):
                    last = nc.tensor.transpose(ps[:, 4 + b, m * 128:(m + 1) * 128], h_act[b][:, m * 128:(m + 1) * 128], ident)
                last.then_inc(s["hT_ps"], 1)

            def down_h(q, b):
                e = pe.value_load(owner[0:1, bass.ds(q, 1)], min_val=0, max_val=E - 1)
                pe.wait_ge(s["hT_ok"], q + 1)
                if not isinstance(q, int) or q >= 2:
                    pe.wait_ge(s["o2_ok"], q - 1)
                for m in range(HC):
                    last = mm(ps[:, 6 + b, 0:C], hT[b][:, m, :], W2_sb[:, bass.ds(e * (HC * C) + m * C, C)], start=m == 0, stop=m == HC - 1)
                last.then_inc(s["o2_ps"], 1)

            pe.wait_ge(s["owner_u"], 1)
            up_x(0, 0)
            up_h(0, 0)
            up_x(1, 1)
            up_h(1, 1)
            turn_h(0, 0)
            down_h(0, 0)
            with pe.Fori(0, SORTED // 2 - 1) as j:
                for b in range(2):
                    q = 2 * j + b + 1
                    up_x(q + 1, b)
                    up_h(q + 1, b)
                    turn_h(q, 1 - b)
                    down_h(q, 1 - b)
            turn_h(SORTED - 1, 1)
            down_h(SORTED - 1, 1)


def kernel(**inputs):
    import numpy as np
    import concourse.bacc as bacc
    from concourse.bass_utils import run_bass_kernel_spmd

    a = {name: np.asarray(value) for name, value in inputs.items()}
    P = "L0_attn_"

    def two(w):
        return np.ascontiguousarray(w.reshape(2, 128, -1).transpose(1, 0, 2))

    row = np.arange(128)
    t = row % L
    col = np.arange(L)
    f = np.float32
    bd64 = (row[:, None] // 64 == row[None, :] // 64).astype(f)
    strict = (t[:, None] < col[None, :]).astype(f)
    low = [((t[:, None] // w == col[None, :] // w) & (t[:, None] % w >= w // 2) & (col[None, :] % w < w // 2)).astype(f)
           for w in (4, 8, 16, 32)]
    made = {
        "ident": np.eye(128, dtype=f), "ones_bd": bd64, "mean_bd": bd64 / f(HS),
        "strict_bd": ((row[:, None] // L == row[None, :] // L) & (t[:, None] < row[None, :] % L)).astype(f),
        "upto": np.concatenate([((t[:, None] <= col[None, :]) & (row[:, None] // 64 == e)).astype(f) for e in range(2)], axis=1),
        "pairs": strict * (t[:, None] // 2 == col[None, :] // 2).astype(f),
        "eye": (t[:, None] == col[None, :]).astype(f),
        "low": np.concatenate(low, axis=1),
        "half": (row[:, None] // L % 2 == np.arange(2)[None, :]).astype(f),
        "blocks": (row[:, None] // L == row[None, :] // L).astype(f),
        "before": (row[:, None] < row[None, :]).astype(f),
        "tile_rows": np.broadcast_to(128 * np.arange(TILES, dtype=f), (128, TILES)),
        "tile_no": np.broadcast_to(np.arange(SORTED, dtype=f), (128, SORTED)),
        "iota": np.broadcast_to(np.arange(E, dtype=f), (128, E)),
    }
    arrays = {
        "table": np.ascontiguousarray(a["L0_tok_weight"].T),
        "tokens": np.ascontiguousarray(a["x"].reshape(B, TILES, L).transpose(0, 2, 1).reshape(128, TILES)).view(np.uint32),
        "tok_bias": np.ascontiguousarray(np.broadcast_to(a["L0_tok_bias"], (128, C))),
        "cvec": np.ascontiguousarray(np.concatenate([a[P + v].reshape(2, 128).T for v in VECS], axis=1)),
        "consts": np.ascontiguousarray(np.concatenate([made[name] for name, _ in CONSTS], axis=1)),
        "W": np.stack([two(a[P + "W" + c]) for c in "rkvo"]),
        "w1": two(a[P + "w1"]), "w2": a[P + "w2"], "a1": two(a[P + "a1"]), "a2": a[P + "a2"],
        "v1": two(a[P + "v1"]), "v2": a[P + "v2"], "g1": two(a[P + "g1"]), "g2": a[P + "g2"],
        "w_red": two(a["L0_ffn_w_red"]), "wg": a["L0_ffn_wg"],
        "W1": np.ascontiguousarray(a["L0_ffn_W1"].reshape(E, 2, 128, HID).transpose(0, 2, 1, 3)),
        "b1": np.ascontiguousarray(np.broadcast_to(a["L0_ffn_b1"].reshape(1, E * HID), (128, E * HID))),
        "W2": np.ascontiguousarray(a["L0_ffn_W2"].reshape(E, HC, 128, C).transpose(0, 2, 1, 3)),
        "b2": a["L0_ffn_b2"],
    }
    arrays = {name: np.ascontiguousarray(value) for name, value in arrays.items()}
    nc = bacc.Bacc("TRN2", target_bir_lowering=False, num_devices=1)
    args = [nc.dram_tensor(name, value.shape, mybir.dt.from_np(value.dtype), kind="ExternalInput").ap()
            for name, value in arrays.items()]
    args += [nc.dram_tensor(name, (SORTED * 128, C), F32, kind="Internal").ap() for name in ("sorted_x", "sorted_o")]
    args.append(nc.dram_tensor("out", (TILES, 128, C), F32, kind="ExternalOutput").ap())
    build(nc, *args)
    got = run_bass_kernel_spmd(nc, [arrays], core_ids=[0]).results[0]["out"]
    return np.ascontiguousarray(np.asarray(got).reshape(TILES, B, L, C).transpose(1, 0, 2, 3).reshape(B, T, C))
```

```python
from contextlib import ExitStack

import concourse.bass as bass
from concourse import mybir

F32 = mybir.dt.float32
U32 = mybir.dt.uint32
ALU = mybir.AluOpType
ACT = mybir.ActivationFunctionType
AX = mybir.AxisListType

B, T, C = 4, 512, 256
H, HS = 4, 64
L = 32
TILES = T // L
CH = 2
SLABS = TILES // CH
BLK = CH * B
NT = BLK * L
UN = 2 * CH * 2
E, HID, G = 8, 512, 16
HC = HID // 128
FT = 4
FN = FT * 128
ROUTE = """wgsq wgmax wginv lg2 topi topf count scan_t more start tiles end base passed start2 place place2 place3 owner owner2 esum""".split()
SORTED = TILES + E - 1
PAIRS = (SORTED - 2) // 2
DECAY = -0.6065306597126334
LN_EPS, GN_EPS = 1e-5, 0.00064
LIFT = 20
LN2 = 0.6931471805599453

ORDER = """Q.start P.k O.mean P.r Q.X0 P.v Q.T0 P.lv P.vd O.var Q.X1 P.lw P.vg Q.T1 P.vgate O.z1 P.la P.w Q.X2 O.z2 P.lg P.a Q.T2
P.vbd F.stats P.g O.out0 P.decay F.rstd Q.X3 P.norm F.xn O.out1 P.inv Q.T3 O.add Q.W0 F.xT Q.A0 P.tok0 P.tok1 P.key Q.S0 P.ar Q.W1
P.rt P.kbd P.bonus Q.A1 P.tok2 P.tok3 P.bbd Q.S1 P.vcmp P.tok4 P.tok5 P.M F.xx P.ve Q.yT P.masks""".split()
AHEAD = {"O": -1, "Q": 0, "P": 1, "F": 2}
VECS = ["x_r", "x_w", "x_k", "x_v", "x_a", "x_g", "w0", "a0", "v0", "k_k", "k_a", "r_k", "ln_w", "ln_b"]
CONSTS = [("ident", 128), ("ones_bd", 128), ("mean_bd", 128), ("strict_bd", 128), ("upto", 2 * L), ("pairs", L),
          ("eye", L), ("low", 4 * L), ("half", 2), ("iota", E),
          ("blocks", 128), ("before", 128), ("tile_rows", TILES), ("tile_no", SORTED)]


def after(step):
    return ROUTE.index(step) + 1


def build(nc, table, tokens, tok_bias, cvec, consts, W, w1, w2, a1, a2, v1, v2, g1, g2, w_red, wg, W1, b1, W2, b2, sorted_x, sorted_o, out):
    ctx = ExitStack()
    with ctx:
        def sem(name):
            return ctx.enter_context(nc.semaphore(name))

        at = [0]
        WORDS = 52000
        arena = ctx.enter_context(nc.sbuf_tensor("arena", [128, WORDS], F32))

        def carve(*dims):
            n = 1
            for d in dims:
                n *= d
            flat = arena[:, at[0]:at[0] + n]
            at[0] += n
            assert at[0] <= WORDS, at[0]
            if len(dims) == 1:
                return flat
            names = "abcdef"[:len(dims)]
            return flat.rearrange(f"p ({' '.join(names)}) -> p {' '.join(names)}",
                                  **{k: d for k, d in zip(names[:-1], dims[:-1])})

        res = carve(TILES, C)
        cst = {}
        for name, width in CONSTS:
            cst[name] = carve(width)
        cv = carve(2 * len(VECS))
        vec = {name: cv[:, 2 * k:2 * k + 2] for k, name in enumerate(VECS)}
        stats = carve(TILES, 6)
        moments = carve(TILES, 2)
        stdev = carve(TILES)
        rstd = carve(TILES)
        eps_ln = carve(1)
        eps_gn = carve(1)
        lift = carve(1)
        ids = carve(TILES).bitcast(U32)
        zero_row = carve(C)
        ident = cst["ident"]
        shared = at[0]

        bias_rows = carve(C)
        w_sb = {k: carve(2, C) for k in "rkvo"}
        w1_sb, a1_sb, v1_sb, g1_sb = carve(2, 64), carve(2, 64), carve(2, 32), carve(2, 128)
        w2_sb, a2_sb, v2_sb, g2_sb = carve(C), carve(C), carve(C), carve(C)

        xT = carve(2, CH + 1, B * L)
        scan_keep = carve(2 * NT)
        mix = [carve(2, NT) for _ in range(3)]
        r, k, v = carve(2, NT), carve(2, NT), carve(2, NT)
        low_v, low_w, low_a, low_g = carve(NT), carve(NT), carve(NT), carve(NT)
        vgate, sig_w, iclr, kk = carve(2, NT), carve(2, NT), carve(2, NT), carve(2, NT)
        inv, v2nd = carve(2, NT), carve(2, NT)
        tmp, tmp2 = carve(2, NT), carve(2, NT)
        xx = tmp2.rearrange("p a (b t) -> p a b t", b=BLK)
        invp = carve(2, BLK, L)
        b_bd, k_bd, v_bd = (carve(2, BLK, 2 * L) for _ in range(3))
        prod = [carve(2, BLK, L + 1) for _ in range(2)]
        ar = [carve(2, BLK, 2 * L) for _ in range(2)]
        a_bd = [carve(2, BLK, 2 * L) for _ in range(2)]
        gate, rtv = [carve(2, NT) for _ in range(2)], [carve(2, NT) for _ in range(2)]
        n_bd, mak_bd = [carve(UN, 128) for _ in range(2)], [carve(UN, 128) for _ in range(2)]
        b_tok, k_tok, v_tok = ([carve(UN, 128) for _ in range(2)] for _ in range(3))
        v_cmp, v_e = [carve(UN, HS) for _ in range(2)], [carve(UN, 2 * HS) for _ in range(2)]
        mrb, mrk = ([carve(UN, 2 * L) for _ in range(2)] for _ in range(2))
        u_0 = [carve(UN, L) for _ in range(2)]
        u_bd = carve(UN, 128)
        t_c, u_c, x_c = carve(UN, L), carve(UN, L), carve(UN, L)
        state = carve(2 * B, HS)
        state_bd = carve(2 * B, 128)
        w_s, sa_e, sa_bd = carve(4, HS), carve(4, 128), carve(4, 128)
        yT, yd, ysq = carve(2, NT), carve(2, NT), carve(2, NT)
        yinv = inv
        xn = yd.rearrange("p a (c t) -> p (a c t)", c=CH).rearrange("p (c x) -> p c x", c=CH)
        attn_end = at[0]

        at[0] = shared
        xn2 = carve(TILES, C)
        xT2 = carve(2, TILES * 128)
        red = carve(TILES * 128)
        logits, ex, onehot, picked = carve(TILES, E), carve(TILES, E), carve(TILES, E), carve(TILES, E)
        top, topf = carve(TILES, E), carve(TILES, E)
        topi = carve(TILES, E).bitcast(U32)
        esum, score = carve(TILES), carve(TILES)
        pickedT = carve(TILES * 128)
        wred_sb = carve(2, G)
        wg_sb, wgn, wgsq, wgT = carve(G), carve(G), carve(G), carve(E)
        wgs = carve(2)
        b2_sb = carve(C)
        W1_sb = carve(E * 2 * HID)
        W2_sb = carve(E * HC * C)
        b1_sb = carve(E * HID)
        ones_sb = carve(128)
        keep_e = carve(E * TILES)
        count, upto_t, start_t = carve(E, TILES), carve(E, TILES), carve(E, TILES)
        more, tiles_e, end_e, base_e = carve(E, TILES), carve(E), carve(E), carve(E)
        place_e, place_f = carve(TILES, E), carve(TILES)
        place = carve(TILES).bitcast(U32)
        passed, owner_f = carve(SORTED, E), carve(SORTED)
        owner = carve(SORTED).bitcast(U32)
        x_s = [carve(C) for _ in range(2)]
        x_sT = [carve(2, 128) for _ in range(2)]
        h_pre = [carve(HID) for _ in range(2)]
        h_act = [carve(HID) for _ in range(2)]
        hT = [carve(HC, 128) for _ in range(2)]
        o_s = [carve(C) for _ in range(2)]
        back = carve(TILES, C)

        ps = ctx.enter_context(nc.psum_tensor("ps", [128, 8, 512], F32))

        names = """route consts_in weights_in ids_in rows_in0 rows_in zeroed_q ffn_in biased stats1_ok mom1_ok sd1_ok zeroed rstd1_ok
        xn_ok xT_ps xT_carry xT_ok xx_ok mix_ok  k_ps r_ps v_ps lv_ps lw_ps vg_ps la_ps w_ps lg_ps a_ps g_ps
        k_ok r_ok v_ok lv_ok lw_ok vg_ok la_ok w_ok lg_ok a_ok g_ok
        kk_ok sq_ok nrm_ps nrm_ok nmax_ok kkn_ok scan_ok prod_ok invp_ok t1_ok k2_ok rkr_ok rt_ps rtv_ok
        lnk_ok ubd2_ok vd_ok vs_ok v2_ok vbd_ok ar_ok abd_ok bn_ok bbd_ok kbd_ok m_ps tok_ps tok_ok vcmp_ok
        masks_ok pairs_ok u0_ok x_ps x_ok t_ps t_ok u_ok ubd_ok
        w_ps_c w_ok_c sa_ps sa_ok sabd_ok s_ps y_ps s_sum s_ok sbd_ok yT_ok mean_ps yd_ok ysq_ok var_ps ysd_ok
        lny_ok ve_ok yz1 yz2 yz3 z_ok o_ps slab_ok
        stats2_ok mom2_ok sd2_ok rstd2_ok xn2_ok xT2_ps xT2_ok red_ps red_ok  wgsum_ok wgsd_ok   wgn_ok
        wgT_ps wgT_ok lg2_ps  topv_ok   onehot_ok dif_ok exp_ok  score_ok picked_ok
        pT_ps pT_ok b2_ps b2_ok zero_ok cleared ffn_set wexp_in tot_ps   
                place_u    owner_u
        scattered xs_in0 xs_in1 xsT_ps xsT_ok h_ps pre_ok act_ok hT_ps hT_ok o2_ps o2_ok o_out0 o_out1 back_in0 back_in1 back_in2 back_in3 final_ok out_done""".split()
        s = {n: sem(n) for n in names}

        block = ctx.enter_context(nc.Block())

        def unit(p, c, b):
            return (p * CH + c) * 2 + b // 2

        UPDATES = ["Q.start", "Q.T0", "Q.T1", "Q.T2", "Q.T3"]

        def pipeline(engine, emit):

            def partly(turn):
                for step in ORDER:
                    slab = turn + AHEAD[step[0]]
                    if 0 <= slab < SLABS:
                        emit(step, slab, slab % 2)

            for turn in (-2, -1, 0):
                partly(turn)
            with engine.Fori(0, SLABS // 2 - 2) as j:
                for turn in (1, 2):
                    for step in ORDER:
                        ahead = turn + AHEAD[step[0]]
                        emit(step, 2 * j + ahead, ahead % 2)
            for turn in range(SLABS - 3, SLABS + 1):
                partly(turn)

        @block.sync
        def _(sp):
            at_c = 0
            for name, width in CONSTS:
                sp.dma_start(cst[name], consts[:, at_c:at_c + width]).then_inc(s["consts_in"], 16)
                at_c += width
            sp.dma_start(cv, cvec[:, :]).then_inc(s["consts_in"], 16)
            sp.dma_start(bias_rows, tok_bias[:, :]).then_inc(s["consts_in"], 16)
            for n, key in enumerate("rkvo"):
                sp.dma_start(w_sb[key], W[n]).then_inc(s["weights_in"], 16)
            for dst, src in ((w1_sb, w1), (a1_sb, a1), (v1_sb, v1), (g1_sb, g1)):
                sp.dma_start(dst, src[:, :, :]).then_inc(s["weights_in"], 16)
            for dst, src, rows in ((w2_sb, w2, 64), (a2_sb, a2, 64), (v2_sb, v2, 32), (g2_sb, g2, 128)):
                sp.dma_start(dst[0:rows, :], src[:, :]).then_inc(s["weights_in"], 16)
            sp.wait_ge(s["zero_ok"], 1)
            sp.dma_start(sorted_x.rearrange("(q p) c -> p q c", p=128),
                         zero_row.unsqueeze(1).broadcast_to([128, SORTED, C])).then_inc(s["cleared"], 16)
            sp.wait_ge(s["slab_ok"], SLABS + 1)
            sp.dma_start(wred_sb, w_red[:, :, :]).then_inc(s["ffn_in"], 16)
            sp.dma_start(wg_sb[0:E, :], wg[:, :]).then_inc(s["ffn_in"], 16)
            sp.dma_start(b2_sb[0:E, :], b2[:, :]).then_inc(s["ffn_in"], 16)
            for e in range(E):
                sp.dma_start(W1_sb[:, e * 2 * HID:(e + 1) * 2 * HID], W1[e]).then_inc(s["wexp_in"], 16)
                sp.dma_start(W2_sb[:, e * HC * C:(e + 1) * HC * C], W2[e]).then_inc(s["wexp_in"], 16)
            sp.dma_start(b1_sb, b1[:, :]).then_inc(s["wexp_in"], 16)
            sp.wait_ge(s["scattered"], 16 * TILES)
            for q in range(2):
                sp.dma_start(x_s[q], sorted_x[q * 128:(q + 1) * 128, :]).then_inc(s[f"xs_in{q}"], 16)

            def load(q, b):
                sp.wait_ge(s["xsT_ps"], q - 1)
                sp.dma_start(x_s[b], sorted_x[bass.ds(q * 128, 128), :]).then_inc(s[f"xs_in{b}"], 16)

            def store(q, b):
                sp.wait_ge(s["o2_ok"], q + 1)
                sp.dma_start(sorted_o[bass.ds(q * 128, 128), :], o_s[b]).then_inc(s[f"o_out{b}"], 16)

            load(2, 0)
            load(3, 1)
            with sp.Fori(1, PAIRS) as j:
                for b in range(2):
                    load(2 * j + b + 2, b)
                    store(2 * j + b - 2, b)
            for q in range(2 * PAIRS, SORTED + 2):
                if q + 2 < SORTED:
                    load(q + 2, q % 2)
                store(q - 2, q % 2)
            for t in range(TILES):
                sp.wait_ge(s["final_ok"], t + 1)
                sp.dma_start(out[t], res[:, t, :]).then_inc(s["out_done"], 16)
            sp.wait_ge(s["out_done"], 16 * TILES)

        @block.gpsimd
        def _(pool):
            pool.dma_start(ids, tokens[:, :]).then_inc(s["ids_in"], 16)
            pool.wait_ge(s["ids_in"], 16)
            for t in range(TILES):
                pool.indirect_dma_start(out=res[:, t, :], out_offset=None, in_=table[:, :],
                                        in_offset=bass.IndirectOffsetOnAxis(ap=ids[:, t:t + 1], axis=0)
                                        ).then_inc(s["rows_in0" if t < CH else "rows_in"], 16)
            for buf in (v_e[0], v_e[1], u_bd, sa_e, state_bd):
                last = nc.gpsimd.memset(buf, 0.0)
            last.then_inc(s["zeroed_q"], 1)

            def emit(step, i, par):
                n = i + 1
                if step == "P.vd":
                    pool.wait_ge(s["v_ok"], n)
                    if not (isinstance(i, int) and i == 0):
                        pool.wait_ge(s["vbd_ok"], i)
                        pool.wait_ge(s["rtv_ok"], i)
                        pool.wait_ge(s["ubd2_ok"], 5 * i - 3)
                    nc.gpsimd.tensor_tensor(v2nd, v, v, ALU.subtract).then_inc(s["vd_ok"], 1)
                elif step == "P.vgate":
                    pool.wait_ge(s["vd_ok"], n)
                    if not (isinstance(i, int) and i == 0):
                        pool.wait_ge(s["ubd2_ok"], 5 * i - 2)
                    pool.wait_ge(s["vg_ok"], n)
                    nc.gpsimd.tensor_tensor(v2nd, v2nd, vgate, ALU.mult).then_inc(s["vs_ok"], 1)
                    pool.wait_ge(s["vs_ok"], n)
                    nc.gpsimd.tensor_tensor(v2nd, v2nd, v, ALU.add).then_inc(s["v2_ok"], 1)
                elif step in ("Q.start", "Q.T0", "Q.T1", "Q.T2", "Q.T3"):
                    lvl = UPDATES.index(step)
                    last_slab = isinstance(i, int) and i == SLABS - 1
                    if lvl == 0:
                        pool.wait_ge(s["v2_ok"], n)
                    elif lvl == 2 and not last_slab:
                        pool.wait_ge(s["vd_ok"], n + 1)
                    elif lvl == 3 and not last_slab:
                        pool.wait_ge(s["v2_ok"], n + 1)
                    if lvl:
                        pool.wait_ge(s["u_ok"], 4 * i + lvl)
                    else:
                        pool.wait_ge(s["u0_ok"], n)
                    low = slice(64, 128)
                    nc.gpsimd.tensor_tensor(u_bd[low, :, 64:128].rearrange("p u (q t) -> p u q t", q=2),
                                            (u_c if lvl else u_0[par])[low].unsqueeze(2).broadcast_to([64, UN, 2, L]),
                                            cst["blocks"][low, 64:128].rearrange("p (q t) -> p q t", q=2).unsqueeze(1)
                                            .broadcast_to([64, UN, 2, L]), ALU.mult).then_inc(s["ubd2_ok"], 1)

            pool.wait_ge(s["zeroed_q"], 1)
            pool.wait_ge(s["consts_in"], 16 * (len(CONSTS) + 2))
            pipeline(pool, emit)
            pool.wait_ge(s["ubd2_ok"], 5 * SLABS)
            pool.wait_ge(s["cleared"], 16)
            pool.wait_ge(s["place_u"], 1)
            pool.wait_ge(s["xn2_ok"], TILES)
            for t in range(TILES):
                pool.indirect_dma_start(out=sorted_x[:, :], out_offset=bass.IndirectOffsetOnAxis(ap=place[:, t:t + 1], axis=0),
                                        in_=xn2[:, t, :], in_offset=None).then_inc(s["scattered"], 16)
            for b in range(2):
                pool.wait_ge(s[f"o_out{b}"], 16 * ((SORTED + 1 - b) // 2))
            for t in range(TILES):
                pool.indirect_dma_start(out=back[:, t, :], out_offset=None, in_=sorted_o[:, :],
                                        in_offset=bass.IndirectOffsetOnAxis(ap=place[:, t:t + 1], axis=0)
                                        ).then_inc(s[f"back_in{t // FT}"], 16)

        @block.scalar
        def _(act):
            nc.scalar.preload_act_table_set("natural_log_exp_and_others")
            act.wait_ge(s["zeroed"], 1)
            act.wait_ge(s["consts_in"], 16 * (len(CONSTS) + 2))

            def copy2(dst, bank, ready, done, n):
                act.wait_ge(s[ready], n)
                nc.scalar.copy(dst, ps[:, bank, :].rearrange("p (a t) -> p a t", a=2)).then_inc(s[done], 1)

            def sigmoid2(dst, bank, bias, ready, done, n):
                act.wait_ge(s[ready], n)
                for p in range(2):
                    last = nc.scalar.activation(dst[:, p, :], ps[:, bank, p * NT:(p + 1) * NT], ACT.Sigmoid, bias=vec[bias][:, p:p + 1])
                last.then_inc(s[done], 1)

            def halves(dst, src, done):
                for h in range(2):
                    q = slice(64 * h, 64 * h + 64)
                    last = nc.scalar.copy(dst[q, :, :, L * h:L * h + L], src[q])
                last.then_inc(s[done], 1)

            def emit(step, i, par):
                n = i + 1
                if step == "F.rstd":
                    act.wait_ge(s["mom1_ok"], n)
                    nc.scalar.activation(stdev[:, 0:CH], moments[:, 0:CH, 1], ACT.Ln, bias=eps_ln).then_inc(s["sd1_ok"], 1)
                    act.wait_ge(s["sd1_ok"], n)
                    nc.scalar.activation(rstd[:, 0:CH], stdev[:, 0:CH], ACT.Exp, scale=-0.5).then_inc(s["rstd1_ok"], 1)
                elif step == "F.xT":
                    act.wait_ge(s["xT_ps"], n)
                    nc.scalar.copy(xT[:, :, 0, :], xT[:, :, CH, :]).then_inc(s["xT_carry"], 1)
                    act.wait_ge(s["xT_carry"], n)
                    nc.scalar.copy(xT[:, :, 1:CH + 1, :], ps[:, 0, :].rearrange("p (a c t) -> p a c t", a=2, c=CH)).then_inc(s["xT_ok"], 1)
                elif step == "P.k":
                    copy2(k, 1, "k_ps", "k_ok", n)
                elif step == "P.r":
                    copy2(r, 2, "r_ps", "r_ok", n)
                elif step == "P.v":
                    copy2(v, 3, "v_ps", "v_ok", n)
                elif step == "P.lv":
                    act.wait_ge(s["lv_ps"], n)
                    nc.scalar.copy(low_v[0:32, :], ps[0:32, 0, 0:NT]).then_inc(s["lv_ok"], 1)
                elif step == "P.lw":
                    nc.scalar.preload_act_table_set("sigmoid_and_others")
                    act.wait_ge(s["lw_ps"], n)
                    nc.scalar.activation(low_w[0:64, :], ps[0:64, 1, 0:NT], ACT.Tanh).then_inc(s["lw_ok"], 1)
                elif step == "P.vg":
                    sigmoid2(vgate, 2, "v0", "vg_ps", "vg_ok", n)
                elif step == "P.la":
                    act.wait_ge(s["la_ps"], n)
                    nc.scalar.copy(low_a[0:64, :], ps[0:64, 3, 0:NT]).then_inc(s["la_ok"], 1)
                elif step == "P.w":
                    sigmoid2(sig_w, 0, "w0", "w_ps", "w_ok", n)
                elif step == "P.lg":
                    act.wait_ge(s["lg_ps"], n)
                    nc.scalar.activation(low_g, ps[:, 1, 0:NT], ACT.Sigmoid).then_inc(s["lg_ok"], 1)
                elif step == "P.a":
                    sigmoid2(iclr, 2, "a0", "a_ps", "a_ok", n)
                elif step == "P.g":
                    if not (isinstance(i, int) and i == 0):
                        act.wait_ge(s["z_ok"], i)
                    copy2(gate[par], 3, "g_ps", "g_ok", n)
                elif step == "P.decay":
                    nc.scalar.preload_act_table_set("natural_log_exp_and_others")
                    act.wait_ge(s["scan_ok"], n)
                    logs = tmp2.rearrange("p a (b t) -> p a b t", b=BLK)
                    nc.scalar.activation(prod[par][:, :, :, 1:L + 1], logs, ACT.Exp, scale=DECAY).then_inc(s["prod_ok"], 1)
                    nc.scalar.activation(invp, logs, ACT.Exp, scale=-DECAY).then_inc(s["invp_ok"], 1)
                elif step == "P.inv":
                    act.wait_ge(s["nmax_ok"], n)
                    nc.scalar.activation(inv, inv, ACT.Ln, scale=float(2 ** LIFT)).then_inc(s["lnk_ok"], 1)
                    act.wait_ge(s["lnk_ok"], n)
                    nc.scalar.activation(inv, inv, ACT.Exp, scale=-0.5, bias=lift).then_inc(s["nrm_ok"], 1)
                elif step == "P.vbd":
                    act.wait_ge(s["v2_ok"], n)
                    halves(v_bd, v2nd.rearrange("p a (b t) -> p a b t", b=BLK), "vbd_ok")
                elif step == "P.ar":
                    act.wait_ge(s["ar_ok"], n)
                    halves(a_bd[par], ar[par][:, :, :, 0:L], "abd_ok")
                elif step[:5] == "P.tok":
                    j = int(step[5])
                    act.wait_ge(s["tok_ps"], 6 * i + j + 1)
                    nc.scalar.copy((v_tok, k_tok, b_tok)[j // 2][par][:, 4 * (j % 2):4 * (j % 2) + 4, :],
                                   ps[:, j % 2, :].rearrange("p (u t) -> p u t", u=4)).then_inc(s["tok_ok"], 1)
                elif step in UPDATES:
                    lvl = UPDATES.index(step)
                    if lvl:
                        act.wait_ge(s["u_ok"], 4 * i + lvl)
                    else:
                        act.wait_ge(s["u0_ok"], n)
                    for q in (0, 1):
                        rows = slice(32 * q, 32 * q + 32)
                        last = nc.scalar.copy(u_bd[rows, :, L * q:L * q + L], (u_c if lvl else u_0[par])[rows])
                    last.then_inc(s["ubd_ok"], 1)
                elif step[:3] == "Q.W":
                    act.wait_ge(s["w_ps_c"], 2 * i + int(step[3]) + 1)
                    nc.scalar.copy(w_s, ps[:, 4, 0:256].rearrange("p (u t) -> p u t", u=4)).then_inc(s["w_ok_c"], 1)
                elif step[:3] == "Q.A":
                    act.wait_ge(s["sa_ok"], 2 * i + int(step[3]) + 1)
                    for h in range(2):
                        last = nc.scalar.activation(sa_bd[:, :, HS * h:HS * h + HS], ps[:, 5, 0:256].rearrange("p (u t) -> p u t", u=4),
                                                    ACT.Copy, scale=cst["half"][:, h:h + 1])
                    last.then_inc(s["sabd_ok"], 1)
                elif step[:3] == "Q.S":
                    c = int(step[3])
                    act.wait_ge(s["y_ps"], 2 * i + c + 1)
                    act.wait_ge(s["s_ok"], 2 * i + c + 1)
                    for h in range(2):
                        q = slice(64 * h, 64 * h + 64)
                        last = nc.scalar.copy(state_bd[q, :, HS * h:HS * h + HS], state[q])
                    last.then_inc(s["sbd_ok"], 1)
                elif step == "Q.yT":
                    nc.scalar.copy(yT.rearrange("p a (c x) -> p c a x", c=CH),
                                   ps[:, 7, :].rearrange("p (c a x) -> p c a x", c=CH, a=2)).then_inc(s["yT_ok"], 1)
                elif step == "P.ve":
                    act.wait_ge(s["vcmp_ok"], n)
                    if isinstance(i, int) and i == 0:
                        act.wait_ge(s["zeroed_q"], 1)
                    for e in range(2):
                        q = slice(64 * e, 64 * e + 64)
                        last = nc.scalar.copy(v_e[par][q, :, HS * e:HS * e + HS], v_cmp[par][q])
                    last.then_inc(s["ve_ok"], 1)
                elif step == "O.var":
                    act.wait_ge(s["var_ps"], n)
                    nc.scalar.activation(yinv, ps[:, 7, :].rearrange("p (a t) -> p a t", a=2), ACT.Ln, bias=eps_gn).then_inc(s["lny_ok"], 1)
                    act.wait_ge(s["lny_ok"], n)
                    nc.scalar.activation(yinv, yinv, ACT.Exp, scale=-0.5).then_inc(s["ysd_ok"], 1)

            pipeline(act, emit)
            act.wait_ge(s["mom2_ok"], 1)
            nc.scalar.activation(stdev, moments[:, :, 1], ACT.Sqrt, bias=eps_ln).then_inc(s["sd2_ok"], 1)
            act.wait_ge(s["wgsum_ok"], 1)
            nc.scalar.activation(wgs[0:E, 1:2], wgs[0:E, 0:1], ACT.Sqrt).then_inc(s["wgsd_ok"], 1)
            for t in range(0, TILES, FT):
                act.wait_ge(s["xT2_ps"], t // FT + 1)
                nc.scalar.copy(xT2[:, :, t * 128:(t + FT) * 128], ps[:, 2 * (t // FT % 2):2 * (t // FT % 2) + 2, :]).then_inc(s["xT2_ok"], 1)
            for t in range(TILES // FT):
                act.wait_ge(s["red_ps"], t + 1)
                nc.scalar.copy(red[0:G, t * FN:(t + 1) * FN], ps[0:G, 6 + t % 2, :]).then_inc(s["red_ok"], 1)
            act.wait_ge(s["dif_ok"], 1)
            nc.scalar.activation(ex, ex, ACT.Exp).then_inc(s["exp_ok"], 1)

            def copy_x(q, b):
                act.wait_ge(s["xsT_ps"], q + 1)
                if not isinstance(q, int) or q >= 2:
                    act.wait_ge(s["h_ps"], q - 1)
                nc.scalar.copy(x_sT[b], ps[:, b, 0:256].rearrange("p (a t) -> p a t", a=2)).then_inc(s["xsT_ok"], 1)

            def gelu_h(q, b):
                act.wait_ge(s["pre_ok"], q + 1)
                nc.scalar.activation(h_act[b], h_pre[b], ACT.Gelu).then_inc(s["act_ok"], 1)

            def copy_h(q, b):
                act.wait_ge(s["hT_ps"], q + 1)
                nc.scalar.copy(hT[b], ps[:, 4 + b, :].rearrange("p (a t) -> p a t", a=HC)).then_inc(s["hT_ok"], 1)

            def act_tile(q, b, more=2):
                copy_h(q, b)
                if more == 2:
                    copy_x(q + 2, b)
                if more:
                    gelu_h(q + 1, 1 - b)

            copy_x(0, 0)
            copy_x(1, 1)
            gelu_h(0, 0)
            act_tile(0, 0)
            act_tile(1, 1)
            with act.Fori(1, PAIRS) as j:
                for b in range(2):
                    act_tile(2 * j + b, b)
            for q in range(2 * PAIRS, SORTED):
                act_tile(q, q % 2, min(2, SORTED - 1 - q))

        @block.vector
        def _(dve):
            V = nc.vector
            V.memset(zero_row, 0.0).then_inc(s["zero_ok"], 1)
            V.memset(eps_ln, LN_EPS)
            V.memset(lift, 0.5 * LIFT * LN2).then_inc(s["z_ok"], 1)
            V.memset(eps_gn, GN_EPS).then_inc(s["slab_ok"], 1)
            V.memset(scan_keep, 1.0)
            V.memset(state, 0.0)
            V.memset(xT, 0.0)
            for par in range(2):
                V.memset(prod[par], 1.0)
            for buf in (a_bd[0], a_bd[1], b_bd, k_bd, v_bd):
                last = V.memset(buf, 0.0)
            last.then_inc(s["zeroed"], 1)
            dve.wait_ge(s["zeroed"], 1)
            V.memset(scan_keep.rearrange("p (b t) -> p b t", t=L)[:, :, 0:1], 0.0).then_inc(s["zeroed"], 1)
            dve.wait_ge(s["zeroed"], 2)
            dve.wait_ge(s["consts_in"], 16 * (len(CONSTS) + 2))

            def per_unit(mask):
                return mask.unsqueeze(1).broadcast_to([128, UN, L])

            def blocks(x):
                return x.rearrange("p a (b t) -> p a b t", b=BLK)

            def two(bank):
                return ps[:, bank, :].rearrange("p (a t) -> p a t", a=2)

            def mixed(i, j, name):
                if j >= 3:
                    dve.wait_ge(s[("k_ps", "r_ps", "lv_ps")[j - 3]], i + 1)
                for p in range(2):
                    last = V.scalar_tensor_tensor(out=mix[j % 3][:, p, :], in0=xx[:, p].rearrange("p b t -> p (b t)"),
                                                  scalar=vec[name][:, p:p + 1],
                                                  in1=xT[:, p, 1:CH + 1, :].rearrange("p c t -> p (c t)"),
                                                  op0=ALU.mult, op1=ALU.add)
                last.then_inc(s["mix_ok"], 1)

            def spread(dst, x, done):
                for h in range(2):
                    q = slice(64 * h, 64 * h + 64)
                    last = V.tensor_tensor(dst[q, :, :, L * h:L * h + L], blocks(x[q]), invp[q], ALU.mult)
                last.then_inc(s[done], 1)

            def emit(step, i, par):
                n = i + 1
                if step == "F.stats":
                    if isinstance(i, int):
                        dve.wait_ge(*((s["rows_in"], 16 * (TILES - CH)) if i else (s["rows_in0"], 16 * CH)))
                    if not (isinstance(i, int) and i < 3):
                        dve.wait_ge(s["z_ok"], i - 1)
                    V.tensor_tensor(xn, res[:, bass.ds(i * CH, CH), :], bias_rows.unsqueeze(1).broadcast_to([128, CH, C]),
                                    ALU.add).then_inc(s["biased"], 1)
                    dve.wait_ge(s["biased"], n)
                    V.tensor_tensor(res[:, i * CH, :], res[:, i * CH, :], bias_rows, ALU.add)
                    for c in range(CH):
                        last = V.bn_stats(stats[:, c, :], xn[:, c, :])
                    last.then_inc(s["stats1_ok"], 1)
                    dve.wait_ge(s["stats1_ok"], n)
                    V.tensor_tensor(res[:, i * CH + 1, :], res[:, i * CH + 1, :], bias_rows, ALU.add)
                    for c in range(CH):
                        last = V.bn_aggr(moments[:, c, :], stats[:, c, :])
                    last.then_inc(s["mom1_ok"], 1)
                elif step == "F.xn":
                    dve.wait_ge(s["rstd1_ok"], n)
                    for c in range(CH):
                        last = V.tensor_scalar(xn[:, c, :], xn[:, c, :], moments[:, c, 0:1], rstd[:, c:c + 1], ALU.subtract, ALU.mult)
                    last.then_inc(s["xn_ok"], 1)
                elif step == "F.xx":
                    dve.wait_ge(s["xT_ok"], n)
                    if not (isinstance(i, int) and i == 0):
                        dve.wait_ge(s["bbd_ok"], i)
                    xb = xT.rearrange("p a c (b t) -> p a (c b) t", t=L)
                    V.tensor_tensor(xx[:, :, :, 1:L], xb[:, :, B:B + BLK, 0:L - 1], xb[:, :, B:B + BLK, 1:L], ALU.subtract)
                    V.tensor_tensor(xx[:, :, :, 0:1], xb[:, :, 0:BLK, L - 1:L], xb[:, :, B:B + BLK, 0:1],
                                    ALU.subtract).then_inc(s["xx_ok"], 1)
                    dve.wait_ge(s["xx_ok"], n)
                    mixed(i, 0, "x_k")
                    mixed(i, 1, "x_r")
                elif step == "P.k":
                    mixed(i, 2, "x_v")
                elif step == "P.r":
                    mixed(i, 3, "x_w")
                elif step == "P.v":
                    mixed(i, 4, "x_a")
                elif step == "P.lw":
                    mixed(i, 5, "x_g")
                elif step == "P.vg":
                    dve.wait_ge(s["k_ok"], n)
                    for p in range(2):
                        last = V.tensor_scalar(kk[:, p, :], k[:, p, :], vec["k_k"][:, p:p + 1], None, ALU.mult)
                    last.then_inc(s["kk_ok"], 1)
                elif step == "P.la":
                    dve.wait_ge(s["kk_ok"], n)
                    V.tensor_tensor(tmp, kk, kk, ALU.mult).then_inc(s["sq_ok"], 1)
                elif step == "P.g":
                    dve.wait_ge(s["w_ok"], n)
                    V.tensor_tensor_scan(tmp2.rearrange("p a t -> p (a t)"), scan_keep, sig_w.rearrange("p a t -> p (a t)"), 0.0,
                                         ALU.mult, ALU.add).then_inc(s["scan_ok"], 1)
                elif step == "P.norm":
                    dve.wait_ge(s["nrm_ps"], n)
                    V.tensor_scalar(inv, two(0), 1e-24, None, ALU.max).then_inc(s["nmax_ok"], 1)
                elif step == "P.key":
                    dve.wait_ge(s["a_ok"], n)
                    dve.wait_ge(s["invp_ok"], n)
                    for p in range(2):
                        last = V.tensor_scalar(tmp2[:, p, :], iclr[:, p, :], 1.0, vec["k_a"][:, p:p + 1], ALU.subtract, ALU.mult)
                    last.then_inc(s["t1_ok"], 1)
                    dve.wait_ge(s["t1_ok"], n)
                    V.scalar_tensor_tensor(out=k, in0=tmp2, scalar=1.0, in1=k, op0=ALU.add, op1=ALU.mult).then_inc(s["k2_ok"], 1)
                    dve.wait_ge(s["k2_ok"], n)
                    dve.wait_ge(s["r_ok"], n)
                    for p in range(2):
                        last = V.scalar_tensor_tensor(out=tmp[:, p, :], in0=r[:, p, :], scalar=vec["r_k"][:, p:p + 1],
                                                      in1=k[:, p, :], op0=ALU.mult, op1=ALU.mult)
                    last.then_inc(s["rkr_ok"], 1)
                    dve.wait_ge(s["nrm_ok"], n)
                    V.tensor_tensor(kk, kk, inv, ALU.mult).then_inc(s["kkn_ok"], 1)
                elif step == "P.ar":
                    dve.wait_ge(s["kkn_ok"], n)
                    V.tensor_tensor(ar[par][:, :, :, 0:L], blocks(kk), prod[par][:, :, :, 0:L], ALU.mult)
                    V.tensor_tensor(ar[par][:, :, :, L:2 * L], blocks(r), prod[par][:, :, :, 1:L + 1],
                                    ALU.mult).then_inc(s["ar_ok"], 1)
                    V.scalar_tensor_tensor(out=tmp2, in0=kk, scalar=-1.0, in1=iclr, op0=ALU.mult, op1=ALU.mult).then_inc(s["bn_ok"], 1)
                elif step == "P.kbd":
                    spread(k_bd, k, "kbd_ok")
                elif step == "P.bbd":
                    dve.wait_ge(s["bn_ok"], n)
                    spread(b_bd, tmp2, "bbd_ok")
                elif step == "P.bonus":
                    dve.wait_ge(s["rt_ps"], n)
                    dve.wait_ge(s["v2_ok"], n)
                    V.tensor_tensor(rtv[par], two(1), v2nd, ALU.mult).then_inc(s["rtv_ok"], 1)
                elif step == "P.masks":
                    dve.wait_ge(s["m_ps"], n)
                    m1 = ps[:, 2, :].rearrange("p (u x) -> p u x", x=2 * L)
                    m2 = ps[:, 3, :].rearrange("p (u x) -> p u x", x=2 * L)
                    V.tensor_tensor(u_0[par], m1[:, :, 0:L], per_unit(cst["pairs"]), ALU.mult).then_inc(s["pairs_ok"], 1)
                    strict = cst["strict_bd"].rearrange("p (q t) -> p q t", q=4).unsqueeze(1).broadcast_to([128, UN, 4, L])
                    upto = cst["upto"].rearrange("p (e t) -> p e t", e=2).unsqueeze(1).broadcast_to([128, UN, 2, L])
                    for own, other, src in ((n_bd[par], mrb[par], m1), (mak_bd[par], mrk[par], m2)):
                        V.tensor_tensor(own.rearrange("p u (q t) -> p u q t", q=4),
                                        src[:, :, 0:L].unsqueeze(2).broadcast_to([128, UN, 4, L]), strict, ALU.mult)
                        V.tensor_tensor(other.rearrange("p u (e t) -> p u e t", e=2),
                                        src[:, :, L:2 * L].unsqueeze(2).broadcast_to([128, UN, 2, L]), upto,
                                        ALU.mult).then_inc(s["masks_ok"], 1)
                        if src is m1:
                            dve.wait_ge(s["pairs_ok"], n)
                            V.tensor_tensor(u_0[par], u_0[par], per_unit(cst["eye"]), ALU.add).then_inc(s["u0_ok"], 1)
                            dve.wait_ge(s["u0_ok"], n)
                            V.transpose(t_c.rearrange("p u t -> p (u t)"),
                                        u_0[par].rearrange("p u t -> p (u t)")).then_inc(s["t_ok"], 1)
                elif step == "P.vcmp":
                    dve.wait_ge(s["tok_ok"], 6 * i + 2)
                    V.tensor_tensor(v_cmp[par], v_tok[par][:, :, 0:HS], v_tok[par][:, :, HS:2 * HS], ALU.add).then_inc(s["vcmp_ok"], 1)
                elif step[:3] == "Q.X":
                    lvl = int(step[3])
                    dve.wait_ge(s["x_ps"], 4 * i + lvl + 1)
                    V.tensor_tensor(x_c, ps[:, 4, 0:UN * L].rearrange("p (u t) -> p u t", u=UN),
                                    per_unit(cst["low"][:, L * lvl:L * lvl + L]), ALU.mult).then_inc(s["x_ok"], 1)
                elif step[:3] == "Q.T":
                    lvl = int(step[3])
                    dve.wait_ge(s["t_ps"], 4 * i + lvl + 1)
                    V.tensor_tensor(t_c, ps[:, 5, 0:UN * L].rearrange("p (u t) -> p u t", u=UN), t_c, ALU.add).then_inc(s["t_ok"], 1)
                    dve.wait_ge(s["t_ok"], 5 * i + lvl + 2)
                    dve.wait_ge(s["ubd_ok"], 5 * i + lvl + 1)
                    dve.wait_ge(s["ubd2_ok"], 5 * i + lvl + 1)
                    V.transpose(u_c.rearrange("p u t -> p (u t)"), t_c.rearrange("p u t -> p (u t)")).then_inc(s["u_ok"], 1)
                elif step[:3] == "Q.A":
                    dve.wait_ge(s["sa_ps"], 2 * i + int(step[3]) + 1)
                    if isinstance(i, int) and i == 0:
                        dve.wait_ge(s["zeroed_q"], 1)
                    for e in range(2):
                        q = slice(64 * e, 64 * e + 64)
                        last = V.tensor_copy(sa_e[q, :, HS * e:HS * e + HS], ps[q, 5, 0:256].rearrange("p (u t) -> p u t", u=4))
                    last.then_inc(s["sa_ok"], 1)
                elif step[:3] == "Q.S":
                    c = int(step[3])
                    dve.wait_ge(s["s_ps"], 2 * i + c + 1)
                    V.tensor_tensor(state.rearrange("p u t -> p (u t)"), ps[:, 6, :], state.rearrange("p u t -> p (u t)"),
                                    ALU.add).then_inc(s["s_sum"], 1)
                    dve.wait_ge(s["s_sum"], 2 * i + c + 1)
                    whole = prod[par].rearrange("p a (c b) t -> p a c b t", c=CH)[:, :, c, :, L:L + 1].broadcast_to([128, 2, B, HS])
                    last = V.tensor_tensor(state.rearrange("p (a b) t -> p a b t", a=2), state.rearrange("p (a b) t -> p a b t", a=2),
                                           whole, ALU.mult)
                    last.then_inc(s["s_ok"], 1)
                elif step == "O.mean":
                    dve.wait_ge(s["mean_ps"], n)
                    V.tensor_tensor(yd, yT, two(6), ALU.subtract).then_inc(s["yd_ok"], 1)
                    dve.wait_ge(s["yd_ok"], n)
                    V.tensor_tensor(ysq, yd, yd, ALU.mult).then_inc(s["ysq_ok"], 1)
                elif step == "O.z1":
                    if isinstance(i, int) and i == SLABS - 1:
                        for t in range(TILES - CH):
                            V.bn_stats(stats[:, t, :], res[:, t, :]).then_inc(s["stats2_ok"], 1)
                    dve.wait_ge(s["ysd_ok"], n)
                    V.tensor_tensor(yd, yd, yinv, ALU.mult).then_inc(s["yz1"], 1)
                    dve.wait_ge(s["yz1"], n)
                    for p in range(2):
                        last = V.tensor_scalar(yd[:, p, :], yd[:, p, :], vec["ln_w"][:, p:p + 1], vec["ln_b"][:, p:p + 1],
                                               ALU.mult, ALU.add)
                    last.then_inc(s["yz2"], 1)
                elif step == "O.z2":
                    dve.wait_ge(s["yz2"], n)
                    V.tensor_tensor(yd, yd, rtv[par], ALU.add).then_inc(s["yz3"], 1)
                    dve.wait_ge(s["yz3"], n)
                    V.tensor_tensor(ysq, yd, gate[par], ALU.mult).then_inc(s["z_ok"], 1)
                elif step == "O.add":
                    dve.wait_ge(s["o_ps"], 2 * n)
                    rows = res[:, bass.ds(i * CH, CH), :].rearrange("p t c -> p (t c)")
                    V.tensor_tensor(rows, ps[:, 6, :], rows, ALU.add).then_inc(s["slab_ok"], 1)

            pipeline(dve, emit)
            dve.wait_ge(s["slab_ok"], SLABS + 1)
            V.memset(ones_sb, 1.0)
            V.memset(keep_e, 1.0).then_inc(s["ffn_set"], 1)
            dve.wait_ge(s["ffn_set"], 1)
            V.memset(keep_e.rearrange("p (e t) -> p e t", t=TILES)[:, :, 0:1], 0.0).then_inc(s["ffn_set"], 1)
            for t in range(TILES - CH, TILES):
                V.bn_stats(stats[:, t, :], res[:, t, :]).then_inc(s["stats2_ok"], 1)
            for t in range(TILES):
                dve.wait_ge(s["stats2_ok"], t + 1)
                last = V.bn_aggr(moments[:, t, :], stats[:, t, :])
            last.then_inc(s["mom2_ok"], 1)
            dve.wait_ge(s["ffn_in"], 48)
            V.tensor_tensor(wgsq[0:E, :], wg_sb[0:E, :], wg_sb[0:E, :], ALU.mult).then_inc(s["route"], 1)
            dve.wait_ge(s["route"], after("wgsq"))
            V.reduce_sum(wgs[0:E, 0:1], wgsq[0:E, :], axis=AX.X).then_inc(s["wgsum_ok"], 1)
            dve.wait_ge(s["sd2_ok"], 1)
            V.reciprocal(rstd, stdev).then_inc(s["rstd2_ok"], 1)
            dve.wait_ge(s["rstd2_ok"], 1)
            for t in range(TILES):
                V.tensor_scalar(xn2[:, t, :], res[:, t, :], moments[:, t, 0:1], rstd[:, t:t + 1],
                                ALU.subtract, ALU.mult).then_inc(s["xn2_ok"], 1)
            dve.wait_ge(s["wgsd_ok"], 1)
            V.tensor_scalar(wgs[0:E, 1:2], wgs[0:E, 1:2], 1e-4, None, ALU.max).then_inc(s["route"], 1)
            dve.wait_ge(s["route"], after("wgmax"))
            V.reciprocal(wgs[0:E, 0:1], wgs[0:E, 1:2]).then_inc(s["route"], 1)
            dve.wait_ge(s["route"], after("wginv"))
            V.tensor_scalar(wgn[0:E, :], wg_sb[0:E, :], wgs[0:E, 0:1], None, ALU.mult).then_inc(s["wgn_ok"], 1)
            dve.wait_ge(s["wgT_ps"], 1)
            V.tensor_copy(wgT[0:G, :], ps[0:G, 4, 0:E]).then_inc(s["wgT_ok"], 1)
            dve.wait_ge(s["lg2_ps"], 1)
            V.tensor_copy(logits, ps[:, 5, 0:TILES * E].rearrange("p (t e) -> p t e", e=E)).then_inc(s["route"], 1)
            dve.wait_ge(s["route"], after("lg2"))
            for t in range(TILES):
                V.max(top[:, t, :], logits[:, t, :]).then_inc(s["topv_ok"], 1)
            for t in range(TILES):
                dve.wait_ge(s["topv_ok"], t + 1)
                last = V.max_index(topi[:, t, :], top[:, t, :], logits[:, t, :])
            last.then_inc(s["route"], 1)
            V.tensor_tensor(ex, logits, top[:, :, 0:1].broadcast_to([128, TILES, E]), ALU.subtract).then_inc(s["dif_ok"], 1)
            dve.wait_ge(s["route"], after("topi"))
            V.tensor_copy(topf[:, :, 0:1], topi[:, :, 0:1]).then_inc(s["route"], 1)
            dve.wait_ge(s["route"], after("topf"))
            V.tensor_tensor(onehot, cst["iota"].unsqueeze(1).broadcast_to([128, TILES, E]),
                            topf[:, :, 0:1].broadcast_to([128, TILES, E]), ALU.is_equal).then_inc(s["onehot_ok"], 1)
            dve.wait_ge(s["ffn_set"], 2)
            dve.wait_ge(s["tot_ps"], 1)
            V.tensor_copy(count, ps[:, 4, 128:256].rearrange("p (t e) -> p e t", e=E)).then_inc(s["route"], 1)
            dve.wait_ge(s["route"], after("count"))
            V.tensor_tensor_scan(upto_t.rearrange("p e t -> p (e t)"), keep_e, count.rearrange("p e t -> p (e t)"), 0.0,
                                 ALU.mult, ALU.add).then_inc(s["route"], 1)
            dve.wait_ge(s["route"], after("scan_t"))
            V.tensor_tensor(more, cst["tile_rows"].unsqueeze(1).broadcast_to([128, E, TILES]),
                            upto_t[:, :, TILES - 1:TILES].broadcast_to([128, E, TILES]), ALU.is_lt).then_inc(s["route"], 1)
            V.tensor_tensor(start_t, upto_t, count, ALU.subtract).then_inc(s["route"], 1)
            dve.wait_ge(s["route"], after("more"))
            V.reduce_sum(tiles_e, more, axis=AX.X).then_inc(s["route"], 1)
            dve.wait_ge(s["route"], after("tiles"))
            V.tensor_tensor_scan(end_e, ones_sb[:, 0:E], tiles_e, 0.0, ALU.mult, ALU.add).then_inc(s["route"], 1)
            dve.wait_ge(s["route"], after("end"))
            V.tensor_tensor(base_e, end_e, tiles_e, ALU.subtract).then_inc(s["route"], 1)
            V.tensor_tensor(passed, end_e.unsqueeze(1).broadcast_to([128, SORTED, E]),
                            cst["tile_no"].unsqueeze(2).broadcast_to([128, SORTED, E]), ALU.is_le).then_inc(s["route"], 1)
            dve.wait_ge(s["route"], after("base"))
            V.scalar_tensor_tensor(out=start_t, in0=base_e.unsqueeze(2).broadcast_to([128, E, TILES]), scalar=128.0, in1=start_t,
                                   op0=ALU.mult, op1=ALU.add).then_inc(s["route"], 1)
            dve.wait_ge(s["route"], after("start2"))
            V.tensor_tensor(place_e, ps[:, 4, 0:128].rearrange("p (t e) -> p t e", e=E), start_t.rearrange("p e t -> p t e"),
                            ALU.add).then_inc(s["route"], 1)
            dve.wait_ge(s["route"], after("place"))
            V.tensor_tensor(place_e, place_e, onehot, ALU.mult).then_inc(s["route"], 1)
            dve.wait_ge(s["route"], after("place2"))
            V.reduce_sum(place_f, place_e, axis=AX.X).then_inc(s["route"], 1)
            dve.wait_ge(s["route"], after("place3"))
            V.tensor_copy(place, place_f).then_inc(s["place_u"], 1)
            dve.wait_ge(s["route"], after("passed"))
            V.reduce_sum(owner_f, passed, axis=AX.X).then_inc(s["route"], 1)
            dve.wait_ge(s["route"], after("owner"))
            V.tensor_scalar(owner_f, owner_f, float(E - 1), None, ALU.min).then_inc(s["route"], 1)
            dve.wait_ge(s["route"], after("owner2"))
            V.tensor_copy(owner, owner_f).then_inc(s["owner_u"], 1)
            dve.wait_ge(s["exp_ok"], 1)
            V.reduce_sum(esum, ex, axis=AX.X).then_inc(s["route"], 1)
            dve.wait_ge(s["route"], after("esum"))
            V.reciprocal(score, esum).then_inc(s["score_ok"], 1)
            dve.wait_ge(s["score_ok"], 1)
            dve.wait_ge(s["onehot_ok"], 1)
            V.tensor_tensor(picked, onehot, score.unsqueeze(2).broadcast_to([128, TILES, E]), ALU.mult).then_inc(s["picked_ok"], 1)
            dve.wait_ge(s["picked_ok"], 1)
            for t in range(0, TILES, FT):
                dve.wait_ge(s["pT_ps"], t // FT + 1)
                V.tensor_copy(pickedT[0:E, t * 128:(t + FT) * 128], ps[0:E, 6, :]).then_inc(s["pT_ok"], 1)
            for t in range(TILES):
                dve.wait_ge(s["b2_ps"], t + 1)
                V.tensor_tensor(res[:, t, :], ps[:, 4 + t % 2, 0:C], res[:, t, :], ALU.add).then_inc(s["b2_ok"], 1)

            def pre(q, b):
                e = dve.value_load(owner[0:1, bass.ds(q, 1)], min_val=0, max_val=E - 1)
                dve.wait_ge(s["h_ps"], q + 1)
                V.tensor_tensor(h_pre[b], ps[:, 2 + b, :], b1_sb[:, bass.ds(e * HID, HID)], ALU.add).then_inc(s["pre_ok"], 1)

            def result(q, b):
                dve.wait_ge(s["o2_ps"], q + 1)
                if not isinstance(q, int) or q >= 2:
                    dve.wait_ge(s[f"o_out{b}"], 16 * (q // 2) if isinstance(q, int) else (q - b) * 8)
                V.tensor_copy(o_s[b], ps[:, 6 + b, 0:C]).then_inc(s["o2_ok"], 1)

            dve.wait_ge(s["wexp_in"], 16 * (2 * E + 1))
            dve.wait_ge(s["owner_u"], 1)
            pre(0, 0)
            pre(1, 1)
            result(0, 0)
            pre(2, 0)
            result(1, 1)
            with dve.Fori(1, PAIRS) as j:
                for b in range(2):
                    q = 2 * j + b
                    pre(q + 1, 1 - b)
                    result(q, b)
            for q in range(2 * PAIRS, SORTED):
                if q + 1 < SORTED:
                    pre(q + 1, 1 - q % 2)
                result(q, q % 2)
            for t in range(TILES):
                dve.wait_ge(s[f"back_in{t // FT}"], 16 * FT)
                V.scalar_tensor_tensor(out=res[:, t, :], in0=back[:, t, :], scalar=score[:, t:t + 1], in1=res[:, t, :],
                                       op0=ALU.mult, op1=ALU.add).then_inc(s["final_ok"], 1)

        @block.tensor
        def _(pe):
            mm = nc.tensor.matmul
            pe.wait_ge(s["consts_in"], 16 * (len(CONSTS) + 2))
            pe.wait_ge(s["zeroed"], 1)

            def full(w, src, bank):
                for m in range(2):
                    for kt in range(2):
                        last = mm(ps[:, bank, m * NT:(m + 1) * NT], w[:, kt, m * 128:(m + 1) * 128], src[:, kt, :],
                                  start=kt == 0, stop=kt == 1)
                return last

            def down(w, src, bank, rows):
                for kt in range(2):
                    last = mm(ps[0:rows, bank, 0:NT], w[:, kt, :], src[:, kt, :], start=kt == 0, stop=kt == 1)
                return last

            def up(w, src, bank, rows):
                for m in range(2):
                    last = mm(ps[:, bank, m * NT:(m + 1) * NT], w[0:rows, m * 128:(m + 1) * 128], src[0:rows, :], start=True, stop=True)
                return last

            def over_heads(w, src, bank):
                for p in range(2):
                    last = mm(ps[:, bank, p * NT:(p + 1) * NT], w, src[:, p, :], start=True, stop=True)
                return last

            def idle(i, count):
                if isinstance(i, int) and i == SLABS - 1:
                    pe.wait_ge(s["tok_ok"], 6 * SLABS)
                    for _ in range(count):
                        mm(ps[:, 0, 0:NT], cst["ones_bd"], w_sb["k"][:, 0, :], start=True, stop=True)

            def emit(step, i, par):
                n = i + 1
                if step == "F.xT":
                    pe.wait_ge(s["xn_ok"], n)
                    if not (isinstance(i, int) and i == 0):
                        pe.wait_ge(s["nmax_ok"], i)
                    for p in range(2):
                        for c in range(CH):
                            last = nc.tensor.transpose(ps[:, 0, p * NT + c * 128:p * NT + (c + 1) * 128],
                                                       xn[:, c, p * 128:(p + 1) * 128], ident)
                    last.then_inc(s["xT_ps"], 1)
                elif step == "P.k":
                    if isinstance(i, int) and i == 0:
                        pe.wait_ge(s["weights_in"], 16 * 12)
                    pe.wait_ge(s["mix_ok"], 6 * i + 1)
                    if not (isinstance(i, int) and i == 0):
                        pe.wait_ge(s["tok_ok"], 6 * i)
                    full(w_sb["k"], mix[0], 1).then_inc(s["k_ps"], 1)
                elif step == "P.r":
                    pe.wait_ge(s["mix_ok"], 6 * i + 2)
                    if not (isinstance(i, int) and i == 0):
                        pe.wait_ge(s["masks_ok"], 2 * i - 1)
                    full(w_sb["r"], mix[1], 2).then_inc(s["r_ps"], 1)
                elif step == "P.v":
                    pe.wait_ge(s["mix_ok"], 6 * i + 3)
                    if not (isinstance(i, int) and i == 0):
                        pe.wait_ge(s["masks_ok"], 2 * i)
                    full(w_sb["v"], mix[2], 3).then_inc(s["v_ps"], 1)
                elif step == "P.lv":
                    down(v1_sb, mix[2], 0, 32).then_inc(s["lv_ps"], 1)
                elif step == "P.lw":
                    pe.wait_ge(s["mix_ok"], 6 * i + 4)
                    pe.wait_ge(s["k_ok"], n)
                    down(w1_sb, mix[0], 1, 64).then_inc(s["lw_ps"], 1)
                elif step == "P.vg":
                    pe.wait_ge(s["lv_ok"], n)
                    pe.wait_ge(s["r_ok"], n)
                    up(v2_sb, low_v, 2, 32).then_inc(s["vg_ps"], 1)
                elif step == "P.la":
                    pe.wait_ge(s["mix_ok"], 6 * i + 5)
                    pe.wait_ge(s["v_ok"], n)
                    down(a1_sb, mix[1], 3, 64).then_inc(s["la_ps"], 1)
                elif step == "P.w":
                    pe.wait_ge(s["lw_ok"], n)
                    up(w2_sb, low_w, 0, 64).then_inc(s["w_ps"], 1)
                elif step == "P.lg":
                    pe.wait_ge(s["mix_ok"], 6 * i + 6)
                    down(g1_sb, mix[2], 1, 128).then_inc(s["lg_ps"], 1)
                elif step == "P.a":
                    pe.wait_ge(s["vg_ok"], n)
                    pe.wait_ge(s["la_ok"], n)
                    up(a2_sb, low_a, 2, 64).then_inc(s["a_ps"], 1)
                elif step == "P.g":
                    pe.wait_ge(s["lg_ok"], n)
                    up(g2_sb, low_g, 3, 128).then_inc(s["g_ps"], 1)
                elif step == "P.norm":
                    pe.wait_ge(s["sq_ok"], n)
                    pe.wait_ge(s["w_ok"], n)
                    over_heads(cst["ones_bd"], tmp, 0).then_inc(s["nrm_ps"], 1)
                elif step == "P.rt":
                    pe.wait_ge(s["rkr_ok"], n)
                    pe.wait_ge(s["tok_ok"], 6 * i + 2)
                    over_heads(cst["ones_bd"], tmp, 1).then_inc(s["rt_ps"], 1)
                elif step == "P.M":
                    pe.wait_ge(s["bbd_ok"], n)
                    pe.wait_ge(s["a_ok"], n)
                    pe.wait_ge(s["g_ok"], n)
                    for src, bank in ((b_bd, 2), (k_bd, 3)):
                        for p in range(2):
                            for u in range(BLK):
                                q, col = 64 * (u % 2), ((p * BLK + u) // 2) * 2 * L
                                last = mm(ps[q:q + 64, bank, col:col + 2 * L], src[:, p, u, :], ar[par][:, p, u, :],
                                          start=True, stop=True)
                    last.then_inc(s["m_ps"], 1)
                elif step[:5] == "P.tok":
                    j = int(step[5])
                    if j == 0:
                        pe.wait_ge(s["vbd_ok"], n)
                        pe.wait_ge(s["nmax_ok"], n)
                        pe.wait_ge(s["xT_ok"], min(n + 1, SLABS) if isinstance(n, int) else n + 1)
                    elif j == 1:
                        pe.wait_ge(s["lg_ok"], n)
                    elif j == 3:
                        pe.wait_ge(s["rtv_ok"], n)
                    else:
                        pe.wait_ge(s["tok_ok"], 6 * i + j - 1)
                        if j == 2:
                            pe.wait_ge(s["kbd_ok"], n)
                        if j == 4:
                            pe.wait_ge(s["bbd_ok"], n)
                    for w in range(4):
                        last = nc.tensor.transpose(ps[:, j % 2, w * 128:(w + 1) * 128],
                                                   (v_bd, k_bd, b_bd)[j // 2][:, j % 2, 2 * w:2 * w + 2, :].rearrange("p a b -> p (a b)"),
                                                   ident)
                    last.then_inc(s["tok_ps"], 1)
                elif step[:3] == "Q.X":
                    lvl = int(step[3])
                    if lvl == 0:
                        idle(i, 8)
                        pe.wait_ge(s["masks_ok"], 2 * i + 1)
                    pe.wait_ge(s["t_ok"], 5 * i + lvl + 1)
                    for u in range(UN):
                        last = mm(ps[:, 4, u * L:(u + 1) * L], n_bd[par][:, u, :], t_c[:, u, :], start=True, stop=True)
                    last.then_inc(s["x_ps"], 1)
                    idle(i, 3)
                elif step[:3] == "Q.T":
                    lvl = int(step[3])
                    pe.wait_ge(s["x_ok"], 4 * i + lvl + 1)
                    pe.wait_ge(s["ubd_ok"], 5 * i + lvl + 1)
                    pe.wait_ge(s["ubd2_ok"], 5 * i + lvl + 1)
                    for u in range(UN):
                        last = mm(ps[:, 5, u * L:(u + 1) * L], u_bd[:, u, :], x_c[:, u, :], start=True, stop=True)
                    last.then_inc(s["t_ps"], 1)
                    idle(i, 5)
                elif step[:3] == "Q.W":
                    c = int(step[3])
                    if c:
                        pe.wait_ge(s["s_ok"], 2 * i + c)
                    else:
                        pe.wait_ge(s["masks_ok"], 2 * n)
                        pe.wait_ge(s["vcmp_ok"], n)
                        pe.wait_ge(s["ve_ok"], n)
                        pe.wait_ge(s["abd_ok"], n)
                    for k in range(4):
                        mm(ps[:, 4, k * HS:(k + 1) * HS], mak_bd[par][:, unit(k // 2, c, 2 * (k % 2)), :],
                           v_cmp[par][:, unit(k // 2, c, 2 * (k % 2)), :], start=k == 0, stop=False, skip_group_check=True)
                    for k in range(4):
                        for e in range(2):
                            last = mm(ps[64 * e:64 * e + 64, 4, k * HS:(k + 1) * HS], a_bd[par][:, k // 2, c * B + 2 * (k % 2) + e, :],
                                      state[:, 2 * k + e, :], start=False, stop=k == 3, skip_group_check=True)
                    last.then_inc(s["w_ps_c"], 1)
                    idle(i, 3)
                elif step[:3] == "Q.A":
                    c = int(step[3])
                    pe.wait_ge(s["w_ok_c"], 2 * i + c + 1)
                    pe.wait_ge(s["ubd_ok"], 5 * n)
                    pe.wait_ge(s["ubd2_ok"], 5 * n)
                    if c:
                        pe.wait_ge(s["sabd_ok"], 2 * i + c)
                    for k in range(4):
                        last = mm(ps[:, 5, k * HS:(k + 1) * HS], u_bd[:, unit(k // 2, c, 2 * (k % 2)), :], w_s[:, k, :],
                                  start=True, stop=True)
                    last.then_inc(s["sa_ps"], 1)
                    idle(i, 5)
                elif step[:3] == "Q.S":
                    c = int(step[3])
                    pe.wait_ge(s["sa_ok"], 2 * i + c + 1)
                    if c == 0:
                        pe.wait_ge(s["slab_ok"], n)
                    for k in range(4):
                        u, x = unit(k // 2, c, 2 * (k % 2)), k * 128
                        mm(ps[:, 6, x:x + 128], k_tok[par][:, u, :], v_e[par][:, u, :], start=True, stop=False)
                        last = mm(ps[:, 6, x:x + 128], b_tok[par][:, u, :], sa_e[:, k, :], start=False, stop=True)
                    last.then_inc(s["s_ps"], 1)
                    pe.wait_ge(s["sabd_ok"], 2 * i + c + 1)
                    if c:
                        pe.wait_ge(s["sbd_ok"], 2 * i + c)
                    for k in range(4):
                        u, x = unit(k // 2, c, 2 * (k % 2)), c * 256 + k * 2 * L
                        mm(ps[:, 7, x:x + 2 * L], v_tok[par][:, u, :], mrk[par][:, u, :], start=True, stop=False, skip_group_check=True)
                        mm(ps[:, 7, x:x + 2 * L], sa_bd[:, k, :], mrb[par][:, u, :], start=False, stop=False, skip_group_check=True)
                        for e in range(2):
                            last = mm(ps[:, 7, x + e * L:x + (e + 1) * L], state_bd[:, 2 * k + e, :],
                                      ar[par][:, k // 2, c * B + 2 * (k % 2) + e, L:2 * L], start=False, stop=e == 1,
                                      skip_group_check=True)
                    last.then_inc(s["y_ps"], 1)
                elif step == "O.mean":
                    pe.wait_ge(s["yT_ok"], n)
                    pe.wait_ge(s["s_ok"], 2 * n)
                    over_heads(cst["mean_bd"], yT, 6).then_inc(s["mean_ps"], 1)
                elif step == "O.var":
                    pe.wait_ge(s["ysq_ok"], n)
                    over_heads(cst["mean_bd"], ysq, 7).then_inc(s["var_ps"], 1)
                elif step[:5] == "O.out":
                    c = int(step[5])
                    if c == 0:
                        pe.wait_ge(s["z_ok"], n + 1)
                    for p in range(2):
                        last = mm(ps[:, 6, c * C:(c + 1) * C], ysq[:, p, c * 128:(c + 1) * 128], w_sb["o"][:, p, :],
                                  start=p == 0, stop=p == 1)
                    last.then_inc(s["o_ps"], 1)

            pipeline(pe, emit)
            pe.wait_ge(s["slab_ok"], SLABS + 1)
            for t in range(0, TILES, FT):
                pe.wait_ge(s["xn2_ok"], t + FT)
                if t >= 2 * FT:
                    pe.wait_ge(s["xT2_ok"], t // FT - 1)
                for p in range(2):
                    for c in range(FT):
                        last = nc.tensor.transpose(ps[:, 2 * (t // FT % 2) + p, c * 128:(c + 1) * 128], xn2[:, t + c, p * 128:(p + 1) * 128], ident)
                last.then_inc(s["xT2_ps"], 1)
            pe.wait_ge(s["ffn_in"], 48)
            for t in range(TILES // FT):
                pe.wait_ge(s["xT2_ok"], t + 1)
                if t >= 2:
                    pe.wait_ge(s["red_ok"], t - 1)
                for p in range(2):
                    last = mm(ps[0:G, 6 + t % 2, :], wred_sb[:, p, :], xT2[:, p, t * FN:(t + 1) * FN], start=p == 0, stop=p == 1)
                last.then_inc(s["red_ps"], 1)
            pe.wait_ge(s["wgn_ok"], 1)
            nc.tensor.transpose(ps[0:G, 4, 0:E], wgn[0:E, :], ident[0:E, 0:E]).then_inc(s["wgT_ps"], 1)
            pe.wait_ge(s["wgT_ok"], 1)
            pe.wait_ge(s["red_ok"], TILES // FT)
            for t in range(TILES):
                last = mm(ps[:, 5, t * E:(t + 1) * E], red[0:G, t * 128:(t + 1) * 128], wgT[0:G, :], start=True, stop=True)
            last.then_inc(s["lg2_ps"], 1)
            pe.wait_ge(s["onehot_ok"], 1)
            pe.wait_ge(s["wgT_ok"], 1)
            mm(ps[:, 4, 0:128], cst["before"], onehot.rearrange("p t e -> p (t e)"), start=True, stop=True)
            mm(ps[:, 4, 128:256], ones_sb, onehot.rearrange("p t e -> p (t e)"), start=True, stop=True).then_inc(s["tot_ps"], 1)
            pe.wait_ge(s["route"], after("place"))
            pe.wait_ge(s["picked_ok"], 1)
            for t in range(0, TILES, FT):
                if t:
                    pe.wait_ge(s["pT_ok"], t // FT)
                for c in range(FT):
                    last = nc.tensor.transpose(ps[0:E, 6, c * 128:(c + 1) * 128], picked[:, t + c, :], ident)
                last.then_inc(s["pT_ps"], 1)
            for t in range(TILES):
                pe.wait_ge(s["pT_ok"], t // FT + 1)
                if t >= 2:
                    pe.wait_ge(s["b2_ok"], t - 1)
                mm(ps[:, 4 + t % 2, 0:C], pickedT[0:E, t * 128:(t + 1) * 128], b2_sb[0:E, :], start=True, stop=True).then_inc(s["b2_ps"], 1)
            pe.wait_ge(s["b2_ok"], TILES)
            pe.wait_ge(s["wexp_in"], 16 * (2 * E + 1))

            def up_x(q, b):
                pe.wait_ge(s[f"xs_in{b}"], 16 * (q // 2 + 1) if isinstance(q, int) else (q - b) * 8 + 16)
                if not isinstance(q, int) or q >= 2:
                    pe.wait_ge(s["xsT_ok"], q - 1)
                for p in range(2):
                    last = nc.tensor.transpose(ps[:, b, p * 128:(p + 1) * 128], x_s[b][:, p * 128:(p + 1) * 128], ident)
                last.then_inc(s["xsT_ps"], 1)

            def owner_of(q):
                return pe.value_load(owner[0:1, bass.ds(q, 1)], min_val=0, max_val=E - 1)

            def up_h(q, b, e):
                pe.wait_ge(s["xsT_ok"], q + 1)
                if not isinstance(q, int) or q >= 2:
                    pe.wait_ge(s["pre_ok"], q - 1)
                for p in range(2):
                    last = mm(ps[:, 2 + b, :], x_sT[b][:, p, :], W1_sb[:, bass.ds(e * (2 * HID) + p * HID, HID)], start=p == 0, stop=p == 1)
                last.then_inc(s["h_ps"], 1)

            def turn_h(q, b):
                pe.wait_ge(s["act_ok"], q + 1)
                if not isinstance(q, int) or q >= 2:
                    pe.wait_ge(s["hT_ok"], q - 1)
                for m in range(HC):
                    last = nc.tensor.transpose(ps[:, 4 + b, m * 128:(m + 1) * 128], h_act[b][:, m * 128:(m + 1) * 128], ident)
                last.then_inc(s["hT_ps"], 1)

            def down_h(q, b):
                e = owner_of(q)
                pe.wait_ge(s["hT_ok"], q + 1)
                if not isinstance(q, int) or q >= 2:
                    pe.wait_ge(s["o2_ok"], q - 1)
                for m in range(HC):
                    last = mm(ps[:, 6 + b, 0:C], hT[b][:, m, :], W2_sb[:, bass.ds(e * (HC * C) + m * C, C)], start=m == 0, stop=m == HC - 1)
                last.then_inc(s["o2_ps"], 1)

            pe.wait_ge(s["owner_u"], 1)

            def pe_tile(q, b, more=2):
                if more:
                    e = owner_of(q + 1)
                turn_h(q, b)
                if more:
                    up_h(q + 1, 1 - b, e)
                if more == 2:
                    up_x(q + 2, b)
                down_h(q, b)

            up_x(0, 0)
            up_x(1, 1)
            up_h(0, 0, owner_of(0))
            pe_tile(0, 0)
            pe_tile(1, 1)
            with pe.Fori(1, PAIRS) as j:
                for b in range(2):
                    pe_tile(2 * j + b, b)
            for q in range(2 * PAIRS, SORTED):
                pe_tile(q, q % 2, min(2, SORTED - 1 - q))


def kernel(**inputs):
    import numpy as np
    import concourse.bacc as bacc
    from concourse.bass_utils import run_bass_kernel_spmd

    a = {name: np.asarray(value) for name, value in inputs.items()}
    P = "L0_attn_"

    def two(w):
        return np.ascontiguousarray(w.reshape(2, 128, -1).transpose(1, 0, 2))

    row = np.arange(128)
    t = row % L
    col = np.arange(L)
    f = np.float32
    bd64 = (row[:, None] // 64 == row[None, :] // 64).astype(f)
    strict = (t[:, None] < col[None, :]).astype(f)
    low = [((t[:, None] // w == col[None, :] // w) & (t[:, None] % w >= w // 2) & (col[None, :] % w < w // 2)).astype(f)
           for w in (4, 8, 16, 32)]
    made = {
        "ident": np.eye(128, dtype=f), "ones_bd": bd64, "mean_bd": bd64 / f(HS),
        "strict_bd": ((row[:, None] // L == row[None, :] // L) & (t[:, None] < row[None, :] % L)).astype(f),
        "upto": np.concatenate([((t[:, None] <= col[None, :]) & (row[:, None] // 64 == e)).astype(f) for e in range(2)], axis=1),
        "pairs": strict * (t[:, None] // 2 == col[None, :] // 2).astype(f),
        "eye": (t[:, None] == col[None, :]).astype(f),
        "low": np.concatenate(low, axis=1),
        "half": (row[:, None] // L % 2 == np.arange(2)[None, :]).astype(f),
        "blocks": (row[:, None] // L == row[None, :] // L).astype(f),
        "before": (row[:, None] < row[None, :]).astype(f),
        "tile_rows": np.broadcast_to(128 * np.arange(TILES, dtype=f), (128, TILES)),
        "tile_no": np.broadcast_to(np.arange(SORTED, dtype=f), (128, SORTED)),
        "iota": np.broadcast_to(np.arange(E, dtype=f), (128, E)),
    }
    arrays = {
        "table": np.ascontiguousarray(a["L0_tok_weight"].T),
        "tokens": np.ascontiguousarray(a["x"].reshape(B, TILES, L).transpose(0, 2, 1).reshape(128, TILES)).view(np.uint32),
        "tok_bias": np.ascontiguousarray(np.broadcast_to(a["L0_tok_bias"], (128, C))),
        "cvec": np.ascontiguousarray(np.concatenate([a[P + v].reshape(2, 128).T for v in VECS], axis=1)),
        "consts": np.ascontiguousarray(np.concatenate([made[name] for name, _ in CONSTS], axis=1)),
        "W": np.stack([two(a[P + "W" + c]) for c in "rkvo"]),
        "w1": two(a[P + "w1"]), "w2": a[P + "w2"], "a1": two(a[P + "a1"]), "a2": a[P + "a2"],
        "v1": two(a[P + "v1"]), "v2": a[P + "v2"], "g1": two(a[P + "g1"]), "g2": a[P + "g2"],
        "w_red": two(a["L0_ffn_w_red"]), "wg": a["L0_ffn_wg"],
        "W1": np.ascontiguousarray(a["L0_ffn_W1"].reshape(E, 2, 128, HID).transpose(0, 2, 1, 3)),
        "b1": np.ascontiguousarray(np.broadcast_to(a["L0_ffn_b1"].reshape(1, E * HID), (128, E * HID))),
        "W2": np.ascontiguousarray(a["L0_ffn_W2"].reshape(E, HC, 128, C).transpose(0, 2, 1, 3)),
        "b2": a["L0_ffn_b2"],
    }
    arrays = {name: np.ascontiguousarray(value) for name, value in arrays.items()}
    nc = bacc.Bacc("TRN2", target_bir_lowering=False, num_devices=1)
    args = [nc.dram_tensor(name, value.shape, mybir.dt.from_np(value.dtype), kind="ExternalInput").ap()
            for name, value in arrays.items()]
    args += [nc.dram_tensor(name, (SORTED * 128, C), F32, kind="Internal").ap() for name in ("sorted_x", "sorted_o")]
    args.append(nc.dram_tensor("out", (TILES, 128, C), F32, kind="ExternalOutput").ap())
    build(nc, *args)
    got = run_bass_kernel_spmd(nc, [arrays], core_ids=[0]).results[0]["out"]
    return np.ascontiguousarray(np.asarray(got).reshape(TILES, B, L, C).transpose(1, 0, 2, 3).reshape(B, T, C))
```
